# Optimizing a Trainium2 kernel written in Bass

```python
import numpy as np
import jax
import jax.numpy as jnp

def _softmax(x, axis=-1):
    return jax.nn.softmax(x, axis=axis)

def _gelu(x):
    return jax.nn.gelu(x, approximate=True)

def _silu(x):
    return jax.nn.silu(x)

def _sigmoid(x):
    return jax.nn.sigmoid(x)

def _layernorm(x, axis=-1, eps=1e-05):
    m = jnp.mean(x, axis=axis, keepdims=True)
    v = jnp.var(x, axis=axis, keepdims=True)
    return (x - m) / jnp.sqrt(v + eps)

def _scatter_add(tgt, idx, src, axis=0):
    return tgt.at[idx].add(src)

def _segment_sum(src, seg, n):
    return jax.ops.segment_sum(src, seg, n)
kernel_name = 'mk_gnn_resnorm_d4_gnn_r32_e9afaa'

def setup_inputs(seed: int=0):
    np.random.seed(seed)
    _w = jnp.asarray

    def _rec_inputs():
        import jax
        import jax.numpy as jnp
        _gk = jax.random.key(seed)
        x = -8.776e-05 + 1 * jax.random.normal(jax.random.fold_in(_gk, 1), (10000, 512), jnp.float32)
        src = jax.random.randint(jax.random.fold_in(_gk, 2), (10000,), 0, 10000, jnp.int32)
        dst = jax.random.randint(jax.random.fold_in(_gk, 3), (10000,), 0, 10000, jnp.int32)
        _o = jnp.argsort(dst, stable=True)
        src = src[_o]
        dst = dst[_o]
        edge_attr_512 = 2.93046e-05 + 1.00006 * jax.random.normal(jax.random.fold_in(_gk, 11), (10000, 512), jnp.float32)
        return (x, src, dst, edge_attr_512)
    x, src, dst, edge_attr_512 = _rec_inputs()

    def _L0_gnn_setup():
        import jax, jax.numpy as jnp
        import numpy as np
        N, E, D = (10000, 5000, 512)
        BN_EPS = 1e-05
        key = jax.random.key(seed)
        k = jax.random.split(key, 6)
        x = jax.random.normal(k[0], (N, D), dtype=jnp.float32)
        edge_index = jax.random.randint(k[1], (2, E), 0, N, dtype=jnp.int32)
        edge_attr = jax.random.normal(k[2], (E, D), dtype=jnp.float32)
        W1 = jax.random.normal(k[3], (D, D), dtype=jnp.float32) * 0.02
        b1 = jnp.zeros((D,), dtype=jnp.float32)
        W2 = jax.random.normal(k[4], (D, D), dtype=jnp.float32) * 0.02
        b2 = jnp.zeros((D,), dtype=jnp.float32)
        gamma = jnp.ones((D,), dtype=jnp.float32)
        beta = jnp.zeros((D,), dtype=jnp.float32)
        return {'x': x, 'edge_index': edge_index, 'edge_attr': edge_attr, 'W1': W1, 'b1': b1, 'W2': W2, 'b2': b2, 'gamma': gamma, 'beta': beta}
    _L0_gnn_all = _L0_gnn_setup()
    _L0_gnn_in = {k: v for k, v in _L0_gnn_all.items() if k in ('W1', 'b1', 'W2', 'b2', 'gamma', 'beta')}
    del _L0_gnn_all

    def _L1_gnn_setup():
        import jax, jax.numpy as jnp
        import numpy as np
        N_NODES = 50000
        N_EDGES = 12500
        IN_DIM = 512
        OUT_DIM = 512
        key = jax.random.key(seed)
        k1, k2, k3, k4 = jax.random.split(key, 4)
        x = jax.random.normal(k1, (N_NODES, IN_DIM), dtype=jnp.float32)
        edge_index = jax.random.randint(k2, (2, N_EDGES), 0, N_NODES, dtype=jnp.int64)
        W = jax.random.normal(k3, (OUT_DIM, IN_DIM), dtype=jnp.float32) / np.sqrt(IN_DIM)
        b = jax.random.normal(k4, (OUT_DIM,), dtype=jnp.float32) * 0.01
        return {'x': x, 'edge_index': edge_index, 'W': W, 'b': b}
    _L1_gnn_all = _L1_gnn_setup()
    _L1_gnn_in = {k: v for k, v in _L1_gnn_all.items() if k in ('W', 'b')}
    del _L1_gnn_all

    def _L2_gnn_setup():
        import jax, jax.numpy as jnp
        import numpy as np
        N_FRAMES = 4096
        D_FEAT = 512
        N_SHOTS = 64
        SHOT_LEN = N_FRAMES // N_SHOTS
        key = jax.random.key(seed)
        x = jax.random.normal(key, (N_FRAMES, D_FEAT), dtype=jnp.float32)
        starts = jnp.arange(N_SHOTS, dtype=jnp.int64) * SHOT_LEN
        ends = starts + (SHOT_LEN - 1)
        graph = jnp.stack([starts, ends], axis=1)
        return {'input': x, 'graph': graph}
    _L2_gnn_all = _L2_gnn_setup()
    _L2_gnn_in = {k: v for k, v in _L2_gnn_all.items() if k in ()}
    del _L2_gnn_all

    def _L3_gnn_setup():
        import jax, jax.numpy as jnp
        import numpy as np
        N_NODES = 3125
        N_EDGES = 50000
        IN_CH = 512
        HID_CH = 128

        def _gcn_conv(x, edge_index, W_conv, b_conv):
            N = x.shape[0]
            loop = jnp.arange(N, dtype=edge_index.dtype)
            row = jnp.concatenate([edge_index[0], loop])
            col = jnp.concatenate([edge_index[1], loop])
            ones = jnp.ones(row.shape[0], dtype=x.dtype)
            deg = jax.ops.segment_sum(ones, col, num_segments=N)
            deg_inv_sqrt = jnp.where(deg > 0, jax.lax.rsqrt(deg), 0.0)
            norm = deg_inv_sqrt[row] * deg_inv_sqrt[col]
            h = x @ W_conv
            msg = h[row] * norm[:, None]
            out = jax.ops.segment_sum(msg, col, num_segments=N)
            return out + b_conv
        key = jax.random.key(seed)
        k1, k2, k3, k4, k5, k6 = jax.random.split(key, 6)
        x = jax.random.normal(k1, (N_NODES, IN_CH), dtype=jnp.float32)
        edge_index = jax.random.randint(k2, (2, N_EDGES), 0, N_NODES, dtype=jnp.int64)
        W_conv = jax.random.normal(k3, (IN_CH, HID_CH), dtype=jnp.float32) / np.sqrt(IN_CH)
        b_conv = jnp.zeros((HID_CH,), dtype=jnp.float32)
        W_lin = jax.random.normal(k4, (HID_CH, IN_CH), dtype=jnp.float32) / np.sqrt(HID_CH)
        b_lin = jnp.zeros((IN_CH,), dtype=jnp.float32)
        return {'x': x, 'edge_index': edge_index, 'W_conv': W_conv, 'b_conv': b_conv, 'W_lin': W_lin, 'b_lin': b_lin}
    _L3_gnn_all = _L3_gnn_setup()
    _L3_gnn_in = {k: v for k, v in _L3_gnn_all.items() if k in ('W_conv', 'b_conv', 'W_lin', 'b_lin')}
    del _L3_gnn_all
    return {'x': x, 'src': src, 'dst': dst, 'edge_attr_512': edge_attr_512, 'L0_gnn_W1': _L0_gnn_in['W1'], 'L0_gnn_b1': _L0_gnn_in['b1'], 'L0_gnn_W2': _L0_gnn_in['W2'], 'L0_gnn_b2': _L0_gnn_in['b2'], 'L0_gnn_gamma': _L0_gnn_in['gamma'], 'L0_gnn_beta': _L0_gnn_in['beta'], 'L1_gnn_W': _L1_gnn_in['W'], 'L1_gnn_b': _L1_gnn_in['b'], 'L3_gnn_W_conv': _L3_gnn_in['W_conv'], 'L3_gnn_b_conv': _L3_gnn_in['b_conv'], 'L3_gnn_W_lin': _L3_gnn_in['W_lin'], 'L3_gnn_b_lin': _L3_gnn_in['b_lin']}

def reference(x, src, dst, edge_attr_512, L0_gnn_W1, L0_gnn_b1, L0_gnn_W2, L0_gnn_b2, L0_gnn_gamma, L0_gnn_beta, L1_gnn_W, L1_gnn_b, L3_gnn_W_conv, L3_gnn_b_conv, L3_gnn_W_lin, L3_gnn_b_lin):
    import jax
    import jax.numpy as jnp

    def _L0_gnn_ref(x, edge_index, edge_attr, W1, b1, W2, b2, gamma, beta):
        import jax, jax.numpy as jnp
        import numpy as np
        N, E, D = (10000, 5000, 512)
        BN_EPS = 1e-05
        src, dst = (edge_index[0], edge_index[1])
        msg = jax.nn.relu(x[src] + edge_attr)
        agg = jax.ops.segment_sum(msg, dst, num_segments=x.shape[0])
        h = x + agg
        h = jax.nn.relu(h @ W1 + b1) @ W2 + b2
        h = x + h
        mean = h.mean(axis=0)
        var = h.var(axis=0)
        h = (h - mean) * jax.lax.rsqrt(var + BN_EPS) * gamma + beta
        return h

    def _L1_gnn_ref(x, edge_index, W, b):
        import jax, jax.numpy as jnp
        import numpy as np
        N_NODES = 50000
        N_EDGES = 12500
        IN_DIM = 512
        OUT_DIM = 512
        n = x.shape[0]
        loops = jnp.arange(n, dtype=edge_index.dtype)
        row = jnp.concatenate([edge_index[0], loops])
        col = jnp.concatenate([edge_index[1], loops])
        deg = jax.ops.segment_sum(jnp.ones(row.shape[0], dtype=x.dtype), row, num_segments=n)
        dis = jax.lax.rsqrt(deg)
        norm = dis[row] * dis[col]
        h = x @ W.T + b
        out = jax.ops.segment_sum(norm[:, None] * h[row], col, num_segments=n)
        return jax.nn.relu(out)

    def _L2_gnn_ref(input, graph):
        import jax, jax.numpy as jnp
        import numpy as np
        N_FRAMES = 4096
        D_FEAT = 512
        N_SHOTS = 64
        SHOT_LEN = N_FRAMES // N_SHOTS
        n = input.shape[0]
        s = graph.shape[0]
        starts = graph[:, 0]
        counts = (graph[:, 1] - graph[:, 0] + 1).astype(input.dtype)
        seg_ids = jnp.searchsorted(starts, jnp.arange(n), side='right') - 1
        sums = jax.ops.segment_sum(input, seg_ids, num_segments=s)
        means = sums / counts[:, None]
        return means[seg_ids]

    def _L3_gnn_ref(x, edge_index, W_conv, b_conv, W_lin, b_lin):
        import jax, jax.numpy as jnp
        import numpy as np
        N_NODES = 3125
        N_EDGES = 50000
        IN_CH = 512
        HID_CH = 128

        def _gcn_conv(x, edge_index, W_conv, b_conv):
            N = x.shape[0]
            loop = jnp.arange(N, dtype=edge_index.dtype)
            row = jnp.concatenate([edge_index[0], loop])
            col = jnp.concatenate([edge_index[1], loop])
            ones = jnp.ones(row.shape[0], dtype=x.dtype)
            deg = jax.ops.segment_sum(ones, col, num_segments=N)
            deg_inv_sqrt = jnp.where(deg > 0, jax.lax.rsqrt(deg), 0.0)
            norm = deg_inv_sqrt[row] * deg_inv_sqrt[col]
            h = x @ W_conv
            msg = h[row] * norm[:, None]
            out = jax.ops.segment_sum(msg, col, num_segments=N)
            return out + b_conv
        h = _gcn_conv(x, edge_index, W_conv, b_conv)
        return h @ W_lin + b_lin
    edge_index = jnp.stack([src, dst])
    edge_index_t = jnp.stack([src, dst], axis=1)
    x = _layernorm(x + _L0_gnn_ref(x, edge_index, edge_attr_512, L0_gnn_W1, L0_gnn_b1, L0_gnn_W2, L0_gnn_b2, L0_gnn_gamma, L0_gnn_beta), axis=-1)
    x = _layernorm(x + _L1_gnn_ref(x, edge_index, L1_gnn_W, L1_gnn_b), axis=-1)
    x = _layernorm(x + _L2_gnn_ref(x, edge_index_t), axis=-1)
    x = _layernorm(x + _L3_gnn_ref(x, edge_index, L3_gnn_W_conv, L3_gnn_b_conv, L3_gnn_W_lin, L3_gnn_b_lin), axis=-1)
    return x

_drawn_inputs = setup_inputs


def setup_inputs(seed=0):
    import zlib

    import numpy as np

    out = dict(_drawn_inputs(seed))
    spreads = {'L0_gnn_b1': (0.0, 0.694),
     'L0_gnn_b2': (0.0, 0.8),
     'L0_gnn_gamma': (1.0, 0.2),
     'L0_gnn_beta': (0.0, 0.1),
     'L3_gnn_b_conv': (0.0, 0.1),
     'L3_gnn_b_lin': (0.0, 0.1)}
    factors = {'L1_gnn_b': 7.311}
    for name, (base, spread) in spreads.items():
        noise = np.random.default_rng([zlib.crc32(name.encode()), seed]).standard_normal(out[name].shape)
        drawn = base * np.exp(spread * noise) if base else spread * noise
        out[name] = jnp.asarray(drawn.astype(out[name].dtype))
    for name, factor in factors.items():
        out[name] = (out[name] * factor).astype(out[name].dtype)
    return out
```

```python
from contextlib import ExitStack
import math

import numpy as np
import concourse.bass as bass
from concourse import mybir

F32 = mybir.dt.float32
BF16 = mybir.dt.bfloat16
I32 = mybir.dt.int32
ALU = mybir.AluOpType
ACT = mybir.ActivationFunctionType
AX = mybir.AxisListType

P = 128
N = 10000
E = 10000
D = 512
HID = 128
DC = D // P
NT = 80
NP = NT * P
PAIRS = NT // 2
WINDOW = P + 64
HALF = WINDOW - P
RUN = 3 * P
LEVELS = math.ceil(math.log2(E + 1))
SKIP = 30000
FAR = 32768
EPS = 1e-5
FIELDS = 6
SRC_A, EID_A, SRC_B, EID_B = 0, 2, 4, 5


def build(nc, x, ea, src_cols, dst_cols, runs, dst_steps, path, path_right, path_left,
          leaf_dst, leaf_src, dst_rows, w1, b1, w2, b2, gamma, beta, wt, b, wc, bc, wl, bl, out):
    ctx = ExitStack()
    with ctx:
        live = []

        def sem(name):
            live.append(nc.alloc_semaphore(name))
            return live[-1]

        def end_phase():
            nc.clear_and_free_semaphores(live)
            nc.all_engine_barrier()
            live.clear()

        def sb(scope, name, shape, dt=F32):
            return scope.enter_context(nc.sbuf_tensor(name, shape, dt))

        def ps(scope, name, shape=(P, D), dt=F32):
            return scope.enter_context(nc.psum_tensor(name, list(shape), dt))

        def rows(t):
            return bass.ds(t * P, P)

        table0 = nc.dram_tensor("table0", [NP, D], F32).ap()
        table1 = nc.dram_tensor("table1", [NP, D], F32).ap()
        table3 = nc.dram_tensor("table3", [NP, HID], F32).ap()
        sums1 = nc.dram_tensor("sums1", [NP, D], F32).ap()
        sums3 = nc.dram_tensor("sums3", [NP, HID], F32).ap()
        d_dram = nc.dram_tensor("d_dram", [NP, D], F32).ap()
        rid_dram = nc.dram_tensor("rid_dram", [NT, P], F32).ap()

        iota = sb(ctx, "iota", [P, P])
        iota_h = sb(ctx, "iota_h", [P, P], BF16)
        pcol = sb(ctx, "pcol", [P, 1])
        ident = sb(ctx, "ident", [P, P])
        ones = sb(ctx, "ones", [P, P])
        zeros_h = sb(ctx, "zeros_h", [P, D], BF16)
        eps = sb(ctx, "eps", [P, 1])
        IDX = sb(ctx, "IDX", [P, PAIRS, FIELDS], I32)
        dlA = sb(ctx, "dlA", [P, NT])
        dlB = sb(ctx, "dlB", [P, PAIRS])
        dis1 = sb(ctx, "dis1", [P, NT])
        dis3 = sb(ctx, "dis3", [P, NT])
        real = sb(ctx, "real", [P, NT])
        skey = sb(ctx, "skey", [P, NT])
        skey_in = sb(ctx, "skey_in", [P, NT])
        rcnt = sb(ctx, "rcnt", [P, NT])
        keys = sb(ctx, "keys", [P, NT])
        keycol = sb(ctx, "keycol", [NT, 1])
        mode_i = sb(ctx, "mode_i", [P, 1], I32)

        ld = [sem(f"prep_load{i}") for i in range(10)]
        p_iota = sem("p_iota")
        p_dve = sem("p_dve")
        p_hot = sem("p_hot")
        p_hot_used = sem("p_hot_used")
        p_run = sem("p_run")
        ev = {name: sem(name) for name in (
            "degrees_summed", "node_counts", "tile_counts", "tile_counts_in", "starts", "blocks_in", "flags_in",
            "flags_summed", "fields_in", "fields_turned", "lasts_in", "lasts_turned", "carries_in",
            "carries_turned", "rids_in", "last_rids_in", "last_rids_turned", "key_rows_in", "keys_turned",
            "columns_in", "columns_turned")}
        p_sqrt = sem("p_sqrt")
        with ExitStack() as s:
            sc = sb(s, "sc", [P, NT], I32)
            dc = sb(s, "dc", [P, NT], I32)
            steps = sb(s, "steps", [P, NT + 1], I32)
            pth = sb(s, "pth", [P, NT, LEVELS], I32)
            pr = sb(s, "pr", [P, NT, LEVELS])
            pl = sb(s, "pl", [P, NT, LEVELS])
            pm = sb(s, "pm", [P, NT, LEVELS])
            ldst = sb(s, "ldst", [P, NT], I32)
            lsrc = sb(s, "lsrc", [P, NT], I32)
            iota_i = sb(s, "iota_i", [P, P], I32)
            pcol_i = sb(s, "pcol_i", [P, 1], I32)
            node_i = sb(s, "node_i", [NT, P], I32)
            nodec_i = sb(s, "nodec_i", [P, NT], I32)
            node = sb(s, "node", [NT, P])
            nodec = sb(s, "nodec", [P, NT])
            tri = sb(s, "tri", [NT, NT])
            part_i = sb(s, "part_i", [P, 8, NT], I32)
            part = sb(s, "part", [P, 8, NT])
            low = sb(s, "low", [P, NT])
            upp = sb(s, "upp", [P, NT])
            tmp = sb(s, "tmp", [P, NT])
            low_i = sb(s, "low_i", [P, NT], I32)
            colv = sb(s, "colv", [P, NT])
            hot = sb(s, "hot", [P, 2, 5, P], BF16)
            hot_leaf = sb(s, "hot_leaf", [P, 2, 4, P], BF16)
            deg = sb(s, "deg", [P, 2, NT])
            cntc = sb(s, "cntc", [NT, 1])
            startc = sb(s, "startc", [NT, 1])
            start_i = sb(s, "start_i", [NT, 3], I32)
            blk = sb(s, "blk", [NT, 1], I32)
            bits_i = sb(s, "bits_i", [NT, 7], I32)
            bits = sb(s, "bits", [NT, 7])
            run_i = sb(s, "run_i", [NT, 2 * RUN], I32)
            run = sb(s, "run", [NT, 2, 2, RUN])
            diff = sb(s, "diff", [NT, 2, RUN])
            flags = sb(s, "flags", [P, 2])
            mode = sb(s, "mode", [P, 1])
            a0 = sb(s, "a0", [NT, WINDOW + 1])
            vld = sb(s, "vld", [NT, WINDOW])
            nvl = sb(s, "nvl", [NT, WINDOW])
            alt = sb(s, "alt", [NT, 2, P])
            fld = sb(s, "fld", [NT, 6, P])
            dcmp = sb(s, "dcmp", [P, NT])
            sg = sb(s, "sg", [NT, 4, P])
            hold = sb(s, "hold", [NT, 6, P])
            last = sb(s, "last", [NT, 4])
            lrow = sb(s, "lrow", [1, 8, NT])
            carry = sb(s, "carry", [NT, 4])
            psD = ps(s, "psD")
            psS = ps(s, "psS")
            psL = ps(s, "psL")
            psX = ps(s, "psX")
            psY = ps(s, "psY")
            psZ = ps(s, "psZ")

            with nc.Block() as block:
                @block.sync
                def _(sp):
                    for i, (to, of) in enumerate(((sc, src_cols), (dc, dst_cols), (steps, dst_steps), (pth, path),
                                                  (pr, path_right), (pl, path_left), (ldst, leaf_dst),
                                                  (lsrc, leaf_src))):
                        sp.dma_start(to[:], of).then_inc(ld[i], 16)

                    sp.wait_ge(ev["rids_in"], 1)
                    sp.dma_start(rid_dram, sg[:, 2, :]).then_inc(ld[8], 16)
                    sp.wait_ge(ld[8], 16)

                @block.gpsimd
                def _(pool):
                    nc.gpsimd.iota(iota_i[:], [[1, P]], base=0, channel_multiplier=0).then_inc(p_iota, 1)
                    nc.gpsimd.iota(pcol_i[:], [[1, 1]], base=0, channel_multiplier=1).then_inc(p_iota, 1)
                    nc.gpsimd.iota(node_i[:], [[1, P]], base=0, channel_multiplier=P).then_inc(p_iota, 1)
                    nc.gpsimd.iota(nodec_i[:], [[P, NT]], base=0, channel_multiplier=1).then_inc(p_iota, 1)
                    pool.wait_ge(ev["blocks_in"], 1)
                    pool.indirect_dma_start(out=run_i[:], out_offset=None, in_=runs,
                                            in_offset=bass.IndirectOffsetOnAxis(ap=blk[:], axis=0)).then_inc(p_run, 16)

                @block.scalar
                def _(act):
                    act.wait_ge(p_sqrt, 1)
                    nc.scalar.activation(deg[:], deg[:], ACT.Sqrt).then_inc(p_sqrt, 1)

                @block.vector
                def _(dve):
                    n = [0]

                    def step(ins):
                        n[0] += 1
                        ins.then_inc(p_dve, 1)
                        dve.wait_ge(p_dve, n[0])

                    V = nc.vector
                    V.memset(ones[:], 1.0)
                    V.memset(zeros_h[:], 0.0)
                    V.memset(eps[:], EPS)
                    V.memset(flags[:], 0.0)
                    V.memset(lrow[:], 0.0)
                    V.memset(hot[:], 0.0)
                    dve.wait_ge(p_iota, 4)
                    V.tensor_copy(iota[:], iota_i[:])
                    V.tensor_copy(iota_h[:], iota_i[:])
                    V.tensor_copy(pcol[:], pcol_i[:])
                    V.tensor_copy(node[:], node_i[:])
                    step(V.tensor_copy(nodec[:], nodec_i[:]))
                    V.tensor_scalar(ident[:], iota[:], pcol[:], None, ALU.is_equal)
                    V.tensor_scalar(real[:], nodec[:], float(N), None, ALU.is_lt)
                    V.tensor_scalar(tri[:], iota[0:NT, 0:NT], pcol[0:NT], None, ALU.is_gt)
                    V.tensor_scalar(colv[:], iota[:, 0:NT], 1.0, None, ALU.add)
                    for i, c in enumerate((sc, dc)):
                        dve.wait_ge(ld[i], 16)
                        V.tensor_scalar(part_i[:, 2 * i, :], c[:], 7, None, ALU.arith_shift_right)
                        V.tensor_scalar(part_i[:, 2 * i + 1, :], c[:], P - 1, None, ALU.bitwise_and)
                    for i in (3, 4, 5):
                        dve.wait_ge(ld[i], 16)
                    step(V.tensor_tensor(pm[:], pth[:], pr[:], ALU.mult))
                    step(V.tensor_reduce(low[:], pm[:], AX.X, ALU.max))
                    step(V.tensor_tensor(pm[:], pth[:], pl[:], ALU.add))
                    step(V.tensor_reduce(upp[:], pm[:], AX.X, ALU.min))
                    step(V.tensor_tensor(tmp[:], low[:], upp[:], ALU.is_ge))
                    step(V.scalar_tensor_tensor(out=low[:], in0=tmp[:], scalar=float(FAR), in1=low[:],
                                                op0=ALU.mult, op1=ALU.add))
                    step(V.tensor_copy(low_i[:], low[:]))
                    V.tensor_scalar(part_i[:, 4, :], low_i[:], 7, None, ALU.arith_shift_right)
                    V.tensor_scalar(part_i[:, 5, :], low_i[:], P - 1, None, ALU.bitwise_and)
                    for i in (6, 7):
                        dve.wait_ge(ld[i], 16)
                    step(V.tensor_tensor(tmp[:], ldst[:], lsrc[:], ALU.subtract))
                    step(V.tensor_scalar(tmp[:], tmp[:], 1.0, None, ALU.add))
                    step(V.tensor_copy(low_i[:], tmp[:]))
                    V.tensor_scalar(part_i[:, 6, :], low_i[:], 7, None, ALU.arith_shift_right)
                    step(V.tensor_scalar(part_i[:, 7, :], low_i[:], P - 1, None, ALU.bitwise_and))
                    step(V.tensor_copy(part[:], part_i[:]))
                    with dve.Fori(0, PAIRS) as k:
                        for u in (0, 1):
                            c = k * 2 + u
                            dve.wait_ge(p_hot_used, c + 1)

                            def col(f):
                                return part[:, f, bass.ds(c, 1)]
                            V.tensor_scalar(hot[:, u, 0, :], iota_h[:], col(1), None, ALU.is_equal)
                            V.tensor_scalar(hot[:, u, 1, 0:NT], iota_h[:, 0:NT], col(0), None, ALU.is_equal)
                            V.tensor_scalar(hot[:, u, 2, :], iota_h[:], col(3), None, ALU.is_equal)
                            V.tensor_scalar(hot[:, u, 3, 0:NT], iota_h[:, 0:NT], col(2), None, ALU.is_equal)
                            V.tensor_scalar(hot[:, u, 4, 0:NT], iota_h[:, 0:NT], col(4), None, ALU.is_equal)
                            for f, by in enumerate((colv[:, bass.ds(c, 1)], pcol[:], col(6), col(7))):
                                last_one = V.tensor_scalar(hot_leaf[:, u, f, :], iota_h[:], col(5), by,
                                                           ALU.is_equal, ALU.mult)
                            last_one.then_inc(p_hot, 1)
                    dve.wait_ge(ev["degrees_summed"], 1)
                    step(V.tensor_scalar(deg[:, 0, :], psS[:, 0:NT], 1.0, None, ALU.add))
                    V.tensor_scalar(deg[:, 1, :], psD[:, 0:NT], 1.0, None, ALU.add).then_inc(p_sqrt, 1)
                    V.tensor_copy(tmp[:], psD[:, 0:NT]).then_inc(ev["node_counts"], 1)
                    dve.wait_ge(ev["tile_counts"], 1)
                    V.tensor_copy(cntc[:], psX[0:NT, 0:1]).then_inc(ev["tile_counts_in"], 1)
                    dve.wait_ge(ev["starts"], 1)
                    step(V.tensor_copy(startc[:], psY[0:NT, 0:1]))
                    step(V.tensor_copy(start_i[:, 0:1], startc[:]))
                    V.tensor_scalar(blk[:], start_i[:, 0:1], 7, None, ALU.arith_shift_right).then_inc(ev["blocks_in"], 1)
                    for i in range(7):
                        step(V.tensor_scalar(bits_i[:, i:i + 1], start_i[:, 0:1], i, 1, ALU.logical_shift_right,
                                        ALU.bitwise_and))
                    step(V.tensor_copy(bits[:], bits_i[:]))
                    dve.wait_ge(p_sqrt, 2)
                    step(V.reciprocal(dis1[:], deg[:, 0, :]))
                    step(V.reciprocal(dis3[:], deg[:, 1, :]))
                    dve.wait_ge(ld[2], 16)
                    step(V.tensor_tensor(dcmp[:], steps[:, 0:NT], steps[:, 1:NT + 1], ALU.is_gt))
                    step(V.tensor_reduce(flags[:, 0:1], dcmp[:], AX.X, ALU.max))
                    dve.wait_ge(p_run, 16)
                    step(V.tensor_copy(run[:, 0, :, :], run_i[:].rearrange("t (a j) -> t a j", a=2)))
                    width, at = RUN, 0
                    for i in (6, 5, 4, 3, 2, 1, 0):
                        by = 1 << i
                        width -= by
                        now, then = run[:, at, :, 0:width], run[:, at, :, by:by + width]
                        step(V.tensor_tensor(diff[:, :, 0:width], then, now, ALU.subtract))
                        step(V.scalar_tensor_tensor(out=run[:, 1 - at, :, 0:width], in0=diff[:, :, 0:width],
                                                    scalar=bits[:, i:i + 1], in1=now, op0=ALU.mult, op1=ALU.add))
                        at = 1 - at
                    src_run, dst_run = run[:, at, 0, :], run[:, at, 1, :]
                    step(V.tensor_scalar(a0[:], dst_run[:, 0:WINDOW + 1], node[:, 0:1], None, ALU.subtract))
                    step(V.tensor_scalar(flags[0:NT, 1:2], a0[:, WINDOW:WINDOW + 1], float(P), None, ALU.is_lt))
                    step(V.tensor_scalar(vld[:], a0[:, 0:WINDOW], float(P), None, ALU.is_lt))
                    dve.nop().then_inc(ev["flags_in"], 1)
                    dve.wait_ge(ev["flags_summed"], 1)
                    step(V.tensor_reduce(mode[:], psX[:, 8:10], AX.X, ALU.max))
                    step(V.tensor_scalar(mode[:], mode[:], 1.0, None, ALU.min))
                    step(V.tensor_copy(mode_i[:], mode[:]))
                    m = mode[0:NT]
                    step(V.tensor_scalar(tmp[0:NT, 0:1], m, -1.0, 1.0, ALU.mult, ALU.add))
                    step(V.tensor_scalar(vld[:], vld[:], tmp[0:NT, 0:1], None, ALU.mult))
                    step(V.tensor_scalar(nvl[:], vld[:], -1.0, 1.0, ALU.mult, ALU.add))
                    step(V.tensor_scalar(alt[:, 0, :], node[:], -float(SKIP), None, ALU.add))
                    step(V.tensor_scalar(alt[:, 1, :], iota[0:NT, :], 1.0, None, ALU.add))
                    step(V.tensor_scalar(alt[:, 0, :], alt[:, 0, :], m, float(SKIP), ALU.mult, ALU.add))
                    step(V.tensor_scalar(alt[:, 1, :], alt[:, 1, :], m, -1.0, ALU.mult, ALU.add))
                    nva, va = nvl[:, 0:P], vld[:, 0:P]
                    for i in range(2):
                        step(V.tensor_tensor(alt[:, i, :], alt[:, i, :], nva, ALU.mult))
                    step(V.tensor_tensor(fld[:, 0, :], src_run[:, 0:P], va, ALU.mult))
                    step(V.tensor_scalar(fld[:, 1, :], iota[0:NT, :], startc[:], None, ALU.add))
                    step(V.tensor_tensor(fld[:, 2, :], a0[:, 0:P], va, ALU.mult))
                    step(V.tensor_tensor(fld[:, 1, :], fld[:, 1, :], va, ALU.mult))
                    step(V.scalar_tensor_tensor(out=fld[:, 0, :], in0=nva, scalar=float(SKIP), in1=fld[:, 0, :],
                                                op0=ALU.mult, op1=ALU.add))
                    step(V.tensor_tensor(fld[:, 1, :], fld[:, 1, :], alt[:, 0, :], ALU.add))
                    step(V.tensor_tensor(fld[:, 2, :], fld[:, 2, :], alt[:, 1, :], ALU.add))
                    step(V.tensor_scalar(tmp[0:NT, 0:HALF], iota[0:NT, 0:HALF], startc[:], float(P), ALU.add, ALU.add))
                    vb, nvb = vld[:, P:WINDOW], nvl[:, P:WINDOW]
                    for h in (0, HALF):
                        to = slice(h, h + HALF)
                        step(V.tensor_tensor(fld[:, 3, to], src_run[:, P:WINDOW], vb, ALU.mult))
                        step(V.tensor_tensor(fld[:, 4, to], tmp[0:NT, 0:HALF], vb, ALU.mult))
                        step(V.tensor_tensor(fld[:, 5, to], a0[:, P:WINDOW], vb, ALU.mult))
                        step(V.tensor_tensor(fld[:, 5, to], fld[:, 5, to], nvb, ALU.subtract))
                        for f in (3, 4):
                            step(V.scalar_tensor_tensor(out=fld[:, f, to], in0=nvb, scalar=float(SKIP),
                                                        in1=fld[:, f, to], op0=ALU.mult, op1=ALU.add))
                    dve.nop().then_inc(ev["fields_in"], 1)
                    dve.wait_ge(ev["fields_turned"], 1)
                    two = "p (k u) -> p k u"
                    A = psY[:, 0:3 * NT].rearrange("p (f k u) -> p f k u", f=3, u=2)
                    for f, to in ((0, SRC_A), (1, EID_A)):
                        step(V.tensor_copy(IDX[:, :, to:to + 2], A[:, f, :, :]))
                    step(V.tensor_copy(dlA[:].rearrange(two, u=2), A[:, 2, :, :]))
                    B = psZ[:, 0:3 * NT].rearrange("p (f k u) -> p f k u", f=3, u=2)
                    for h in (0, 1):
                        to = slice(h * HALF, (h + 1) * HALF)
                        step(V.tensor_copy(IDX[to, :, SRC_B], B[to, 0, :, h]))
                        step(V.tensor_copy(IDX[to, :, EID_B], B[to, 1, :, h]))
                        step(V.tensor_copy(dlB[to, :], B[to, 2, :, h]))
                    L = psL[0:NT, :].rearrange("t (f j) -> t f j", f=4)
                    step(V.tensor_copy(sg[:], L))
                    step(V.tensor_scalar(hold[:, 0, :], sg[:, 0, :], 0.0, None, ALU.is_equal))
                    step(V.tensor_scalar(hold[:, 1, :], sg[:, 0, :], float(P), None, ALU.mult))
                    step(V.tensor_tensor(hold[:, 1, :], hold[:, 1, :], sg[:, 1, :], ALU.add))
                    step(V.tensor_scalar(hold[:, 3, :], hold[:, 0, :], -float(P), float(P), ALU.mult, ALU.add))
                    step(V.tensor_scalar(hold[:, 2, :], sg[:, 2, :], float(P), None, ALU.mult))
                    step(V.tensor_tensor(hold[:, 1, :], hold[:, 1, :], hold[:, 3, :], ALU.subtract))
                    step(V.tensor_tensor(hold[:, 2, :], hold[:, 2, :], sg[:, 3, :], ALU.add))
                    step(V.tensor_tensor_scan(hold[:, 3, :], hold[:, 0, :], hold[:, 1, :], 0.0, ALU.mult, ALU.add))
                    step(V.tensor_tensor_scan(hold[:, 4, :], hold[:, 0, :], hold[:, 2, :], 0.0, ALU.mult, ALU.add))
                    step(V.tensor_reduce(last[:, 0:1], hold[:, 0, :], AX.X, ALU.min))
                    step(V.tensor_copy(last[:, 1:2], hold[:, 3, P - 1:P]))
                    V.tensor_copy(last[:, 2:3], hold[:, 4, P - 1:P]).then_inc(ev["lasts_in"], 1)
                    dve.wait_ge(ev["lasts_turned"], 1)
                    step(V.tensor_copy(lrow[:, 0:3, :], psX[0:1, 0:3 * NT].rearrange("o (f t) -> o f t", f=3)))
                    step(V.tensor_tensor_scan(lrow[:, 3, :], lrow[:, 0, :], lrow[:, 1, :], 0.0, ALU.mult, ALU.add))
                    step(V.tensor_tensor_scan(lrow[:, 4, :], lrow[:, 0, :], lrow[:, 2, :], 0.0, ALU.mult, ALU.add))
                    step(V.tensor_copy(lrow[:, 5, 1:NT], lrow[:, 3, 0:NT - 1]))
                    V.tensor_copy(lrow[:, 6, 1:NT], lrow[:, 4, 0:NT - 1]).then_inc(ev["carries_in"], 1)
                    dve.wait_ge(ev["carries_turned"], 1)
                    step(V.tensor_copy(carry[:, 0:2], psY[0:NT, 0:2]))
                    step(V.tensor_tensor_scan(sg[:, 0, :], hold[:, 0, :], hold[:, 1, :], carry[:, 0:1], ALU.mult,
                                              ALU.add))
                    step(V.tensor_tensor_scan(sg[:, 1, :], hold[:, 0, :], hold[:, 2, :], carry[:, 1:2], ALU.mult,
                                              ALU.add))
                    step(V.tensor_scalar(sg[:, 2, :], sg[:, 0, :], 0.0, float(N), ALU.is_equal, ALU.mult))
                    step(V.tensor_tensor(sg[:, 2, :], sg[:, 2, :], sg[:, 0, :], ALU.add))
                    dve.nop().then_inc(ev["rids_in"], 1)
                    V.tensor_copy(last[:, 3:4], sg[:, 2, P - 1:P]).then_inc(ev["last_rids_in"], 1)
                    dve.wait_ge(ev["last_rids_turned"], 1)
                    step(V.memset(lrow[:, 0, 0:1], float(N)))
                    step(V.tensor_copy(lrow[:, 0, 1:NT], psX[0:1, 0:NT - 1]))
                    step(V.memset(lrow[:, 1, 0:1], 0.0))
                    step(V.tensor_tensor(lrow[:, 1, 1:NT], lrow[:, 0, 1:NT], lrow[:, 0, 0:NT - 1], ALU.is_equal))
                    step(V.tensor_scalar(lrow[:, 2, 1:NT], lrow[:, 0, 1:NT], float(N), None, ALU.is_equal))
                    step(V.memset(lrow[:, 2, 0:1], 0.0))
                    step(V.tensor_tensor(lrow[:, 1, :], lrow[:, 1, :], lrow[:, 2, :], ALU.add))
                    step(V.scalar_tensor_tensor(out=lrow[:, 1, :], in0=lrow[:, 1, :], scalar=-float(FAR),
                                                in1=lrow[:, 0, :], op0=ALU.mult, op1=ALU.add))
                    dve.nop().then_inc(ev["key_rows_in"], 1)
                    dve.wait_ge(ev["keys_turned"], 1)
                    step(V.tensor_copy(carry[:, 2:3], psY[0:NT, 4:5]))
                    step(V.tensor_copy(keycol[:], psY[0:NT, 5:6]))
                    step(V.tensor_copy(keys[:], psZ[:, 0:NT]))
                    step(V.tensor_scalar(hold[:, 3, :], sg[:, 2, :], carry[:, 2:3], 0.0, ALU.is_equal, ALU.is_equal))
                    step(V.tensor_scalar(hold[:, 4, :], sg[:, 2, :], last[:, 3:4], 0.0, ALU.is_equal, ALU.is_equal))
                    step(V.tensor_scalar(hold[:, 5, :], node[:], float(N), None, ALU.is_lt))
                    step(V.tensor_tensor(sg[:, 0, :], sg[:, 0, :], hold[:, 5, :], ALU.mult))
                    step(V.tensor_tensor(sg[:, 3, :], sg[:, 0, :], hold[:, 3, :], ALU.mult))
                    step(V.tensor_tensor(sg[:, 3, :], sg[:, 3, :], hold[:, 4, :], ALU.mult))
                    dve.nop().then_inc(ev["columns_in"], 1)
                    dve.wait_ge(ev["columns_turned"], 1)
                    step(V.tensor_copy(skey[:], psX[:, 0:NT]))
                    step(V.tensor_copy(skey_in[:], psX[:, NT:2 * NT]))
                    step(V.reciprocal(rcnt[:], psX[:, 2 * NT:3 * NT]))

                @block.tensor
                def _(pe):
                    mm = nc.tensor.matmul
                    pe.wait_ge(p_dve, 1)
                    for o, m_, w in ((psD, P, NT), (psS, P, NT), (psL, NT, 4 * P)):
                        last_one = mm(o[0:m_, 0:w], zeros_h[:, 0:m_], zeros_h[:, 0:w], start=True, stop=False)
                    last_one.then_inc(p_hot_used, 2)
                    with pe.Fori(0, PAIRS) as k:
                        for u in (0, 1):
                            pe.wait_ge(p_hot, k * 2 + u + 1)
                            mm(psS[:, 0:NT], hot[:, u, 0, :], hot[:, u, 1, 0:NT], start=False, stop=False)
                            mm(psD[:, 0:NT], hot[:, u, 2, :], hot[:, u, 3, 0:NT], start=False, stop=False)
                            mm(psL[0:NT, :], hot[:, u, 4, 0:NT], hot_leaf[:, u, :, :].rearrange("p f j -> p (f j)"),
                               start=False, stop=False).then_inc(p_hot_used, 1)
                    for o, m_, w in ((psD, P, NT), (psS, P, NT), (psL, NT, 4 * P)):
                        last_one = mm(o[0:m_, 0:w], zeros_h[:, 0:m_], zeros_h[:, 0:w], start=False, stop=True)
                    last_one.then_inc(ev["degrees_summed"], 1)
                    pe.wait_ge(ev["node_counts"], 1)
                    mm(psX[0:NT, 0:1], tmp[:], ones[:, 0:1], start=True, stop=True).then_inc(ev["tile_counts"], 1)
                    pe.wait_ge(ev["tile_counts_in"], 1)
                    mm(psY[0:NT, 0:1], tri[:], cntc[:], start=True, stop=True).then_inc(ev["starts"], 1)
                    pe.wait_ge(ev["flags_in"], 1)
                    mm(psX[:, 8:10], ones[:], flags[:], start=True, stop=True).then_inc(ev["flags_summed"], 1)
                    pe.wait_ge(ev["fields_in"], 1)
                    for f in range(3):
                        nc.tensor.transpose(psY[:, f * NT:(f + 1) * NT], fld[:, f, :], ident[0:NT, 0:NT])
                    for f in range(3):
                        last_one = nc.tensor.transpose(psZ[:, f * NT:(f + 1) * NT], fld[:, 3 + f, :],
                                                       ident[0:NT, 0:NT])
                    last_one.then_inc(ev["fields_turned"], 1)
                    pe.wait_ge(ev["lasts_in"], 1)
                    for f in range(3):
                        last_one = mm(psX[0:1, f * NT:(f + 1) * NT], last[:, f:f + 1], ident[0:NT, 0:NT],
                                      start=True, stop=True)
                    last_one.then_inc(ev["lasts_turned"], 1)
                    pe.wait_ge(ev["carries_in"], 1)
                    for f in range(2):
                        last_one = mm(psY[0:NT, f:f + 1], lrow[:, 5 + f, :], ones[0:1, 0:1], start=True, stop=True)
                    last_one.then_inc(ev["carries_turned"], 1)
                    pe.wait_ge(ev["last_rids_in"], 1)
                    mm(psX[0:1, 0:NT], last[:, 3:4], ident[0:NT, 0:NT],
                       start=True, stop=True).then_inc(ev["last_rids_turned"], 1)
                    pe.wait_ge(ev["key_rows_in"], 1)
                    mm(psY[0:NT, 4:5], lrow[:, 0, :], ones[0:1, 0:1], start=True, stop=True)
                    mm(psY[0:NT, 5:6], lrow[:, 1, :], ones[0:1, 0:1], start=True, stop=True)
                    mm(psZ[:, 0:NT], ones[0:1, :], lrow[:, 1, :], start=True, stop=True).then_inc(ev["keys_turned"], 1)
                    pe.wait_ge(ev["columns_in"], 1)
                    for f, of in enumerate((0, 3, 1)):
                        last_one = nc.tensor.transpose(psX[:, f * NT:(f + 1) * NT], sg[:, of, :], ident[0:NT, 0:NT])
                    last_one.then_inc(ev["columns_turned"], 1)
            end_phase()

        def wait(eng, semaphore, value):
            if not (isinstance(value, int) and value <= 0):
                eng.wait_ge(semaphore, value)

        def pipe(eng, stages, count, unroll):
            first = 2 * unroll
            for t in range(first):
                for f, lag in stages:
                    if t - lag >= 0:
                        f(t - lag, (t - lag) % unroll, (t - lag) // unroll)
            with eng.Fori(2, count // unroll) as r:
                for u in range(unroll):
                    for f, lag in stages:
                        f(r * unroll + (u - lag), (u - lag) % unroll, r + (u - lag) // unroll)
            for t in range(count, count + max(lag for _, lag in stages)):
                for f, lag in stages:
                    if t - lag < count:
                        f(t - lag, (t - lag) % unroll, (t - lag) // unroll)

        class TablePass:

            def __init__(self, scope, name, table, sums, width, buffers, squares, psum, edge_rows=None):
                self.msg, self.cur, self.edge, self.zero = (buffers[:, i, :] for i in range(4))
                self.eq, self.eq_below, self.below = (squares[:, i, :] for i in range(3))
                self.psum = psum
                self.table, self.sums, self.edge_rows = table, sums, edge_rows
                self.src_i = sb(scope, f"{name}_src_i", [P, NT], I32)
                self.dst_i = sb(scope, f"{name}_dst_i", [P, NT], I32)
                self.dst = sb(scope, f"{name}_dst", [P, NT])
                self.row_i = sb(scope, f"{name}_row_i", [P, P], I32)
                self.dup = sb(scope, f"{name}_dup", [P, 1])
                self.to = sb(scope, f"{name}_to", [P, 1], I32)
                self.of = sb(scope, f"{name}_of", [P, 1], I32)
                self.width = width
                self.cols_ld = [sem(f"{name}_cols{i}") for i in range(2)]
                self.zero_in = sem(f"{name}_zero_in")
                self.zeroed = sem(f"{name}_zeroed")
                self.step_in = sem(f"{name}_step")
                self.tile = sem(f"{name}_tile")
                self.row_ld = sem(f"{name}_row_ld")
                self.edge_ld = sem(f"{name}_edge_ld")
                self.of_in = sem(f"{name}_of_in")
                self.msg_ld = sem(f"{name}_msg_ld")
                self.msg_in = sem(f"{name}_msg_in")
                self.to_in = sem(f"{name}_to_in")
                self.sum_done = sem(f"{name}_sum_done")
                self.cur_ld = sem(f"{name}_cur_ld")
                self.cur_in = sem(f"{name}_cur_in")
                self.cur_st = sem(f"{name}_cur_st")
                self.seen = sem(f"{name}_seen")
                self.seen_sp = sem(f"{name}_seen_sp")

            def on_sync(self, sp):
                mode = sp.value_load(mode_i[0:1, 0:1], min_val=0, max_val=1)
                with sp.If(mode > 0):
                    sp.dma_start(self.src_i[:], src_cols).then_inc(self.cols_ld[0], 16)
                    sp.dma_start(self.dst_i[:], dst_cols).then_inc(self.cols_ld[1], 16)
                    sp.wait_ge(self.zero_in, 1)
                    with sp.Fori(0, NT) as t:
                        sp.dma_start(self.sums[rows(t), :], self.zero).then_inc(self.zeroed, 16)
                        sp.wait_ge(self.zeroed, 16 * (t + 1))
                        sp.nop().then_inc(self.seen_sp, 1)
                    with sp.Fori(0, NT) as t:
                        sp.wait_ge(self.tile, t + 1)
                        sp.nop().then_inc(self.seen_sp, 1)
                        sp.dma_start(self.row_i[:], dst_rows[bass.ds(t, 1), :].to_broadcast([P, P])
                                     ).then_inc(self.row_ld, 16)
                        if self.edge_rows is not None:
                            sp.dma_start(self.edge, self.edge_rows[rows(t), :]).then_inc(self.edge_ld, 16)

            def on_gpsimd(self, pool):
                mode = pool.value_load(mode_i[0:1, 0:1], min_val=0, max_val=1)
                with pool.If(mode > 0):
                    pool.wait_ge(self.cols_ld[0], 16)
                    pool.wait_ge(self.zero_in, 1)
                    pool.wait_ge(self.zeroed, 16 * NT)
                    pool.nop().then_inc(self.tile, 1)
                    with pool.Fori(0, NT) as t:
                        nc.gpsimd.tensor_copy(self.of[:], self.src_i[:, bass.ds(t, 1)]).then_inc(self.of_in, 1)
                        pool.wait_ge(self.of_in, t + 1)
                        pool.nop().then_inc(self.seen, 1)
                        pool.indirect_dma_start(out=self.msg, out_offset=None, in_=self.table,
                                                in_offset=bass.IndirectOffsetOnAxis(ap=self.of[:], axis=0),
                                                bounds_check=N - 1, oob_is_err=False).then_inc(self.msg_ld, 16)
                        pool.wait_ge(self.to_in, t + 1)
                        pool.nop().then_inc(self.seen, 1)
                        pool.indirect_dma_start(out=self.cur, out_offset=None, in_=self.sums,
                                                in_offset=bass.IndirectOffsetOnAxis(ap=self.to[:], axis=0),
                                                bounds_check=N - 1, oob_is_err=False).then_inc(self.cur_ld, 16)
                        pool.wait_ge(self.cur_in, t + 1)
                        pool.nop().then_inc(self.seen, 1)
                        pool.indirect_dma_start(out=self.sums, in_=self.cur, in_offset=None,
                                                out_offset=bass.IndirectOffsetOnAxis(ap=self.to[:], axis=0),
                                                bounds_check=N - 1, oob_is_err=False).then_inc(self.cur_st, 16)
                        pool.wait_ge(self.cur_st, 16 * (t + 1))
                        pool.wait_ge(self.msg_ld, 16 * (t + 1))
                        pool.nop().then_inc(self.tile, 1)

            def on_vector(self, dve):
                V = nc.vector
                mode = dve.value_load(mode_i[0:1, 0:1], min_val=0, max_val=1)
                with dve.If(mode > 0):
                    V.memset(self.msg, 0.0)
                    V.memset(self.cur, 0.0)
                    V.tensor_scalar(self.below, iota[:], pcol[:], None, ALU.is_lt)
                    V.memset(self.zero, 0.0).then_inc(self.zero_in, 1)
                    dve.wait_ge(self.cols_ld[1], 16)
                    V.tensor_copy(self.dst[:], self.dst_i[:]).then_inc(self.step_in, 1)
                    dve.wait_ge(self.step_in, 1)
                    steps_ = 3 if self.edge_rows is None else 4
                    with dve.Fori(0, NT) as t:
                        n = [0]

                        def step(ins):
                            n[0] += 1
                            ins.then_inc(self.step_in, 1)
                            dve.wait_ge(self.step_in, t * steps_ + (n[0] + 1))
                        dve.wait_ge(self.row_ld, 16 * (t + 1))
                        step(V.tensor_scalar(self.eq, self.row_i[:], self.dst[:, bass.ds(t, 1)], None, ALU.is_equal))
                        step(V.tensor_tensor(self.eq_below, self.eq, self.below, ALU.mult))
                        step(V.tensor_reduce(self.dup[:], self.eq_below, AX.X, ALU.max))
                        V.tensor_scalar(self.to[:], self.dup[:], float(SKIP), self.dst[:, bass.ds(t, 1)],
                                        ALU.mult, ALU.add).then_inc(self.to_in, 1)
                        dve.wait_ge(self.msg_ld, 16 * (t + 1))
                        if self.edge_rows is not None:
                            dve.wait_ge(self.edge_ld, 16 * (t + 1))
                            step(V.tensor_tensor(self.msg, self.msg, self.edge, ALU.add))
                            V.tensor_scalar(self.msg, self.msg, 0.0, None, ALU.max).then_inc(self.msg_in, 1)
                        else:
                            dve.nop().then_inc(self.msg_in, 1)
                        dve.wait_ge(self.cur_ld, 16 * (t + 1))
                        dve.wait_ge(self.sum_done, t + 1)
                        V.tensor_tensor(self.cur, self.cur, self.psum[:, 0:self.width],
                                        ALU.add).then_inc(self.cur_in, 1)

            def on_tensor(self, pe):
                mode = pe.value_load(mode_i[0:1, 0:1], min_val=0, max_val=1)
                with pe.If(mode > 0):
                    with pe.Fori(0, NT) as t:
                        pe.wait_ge(self.msg_in, t + 1)
                        nc.tensor.matmul(self.psum[:, 0:self.width], self.eq, self.msg,
                                         start=True, stop=True).then_inc(self.sum_done, 1)

        aB = sb(ctx, "aB", [P, D])
        cB = sb(ctx, "cB", [P, D])

        NQ, Q = NT // 4, 4
        with ExitStack() as s:
            w1s = sb(s, "w1s", [P, DC, D])
            w2s = sb(s, "w2s", [P, DC, D])
            b1s = sb(s, "b1s", [P, DC])
            slotidx = sb(s, "slotidx", [P, 2, FIELDS], I32)
            gA = sb(s, "gA", [P, Q, D])
            mA = sb(s, "mA", [P, Q, D])
            gB = sb(s, "gB", [P, 2, D])
            mB = sb(s, "mB", [P, 2, D])
            xs = sb(s, "xs", [P, 2 * Q, D])
            ohA = sb(s, "ohA", [P, Q, P])
            ohB = sb(s, "ohB", [P, 2, P])
            hT = sb(s, "hT", [P, DC, Q * P])
            gT = sb(s, "gT", [P, DC, Q * P])
            ds = sb(s, "ds", [P, Q, D])
            sq = sb(s, "sq", [P, 2, D])
            S1 = sb(s, "S1", [P, D])
            S2 = sb(s, "S2", [P, D])
            row = sb(s, "row", [P, 3, D])
            mean = sb(s, "mean", [P, D])
            var = sb(s, "var", [P, D])
            half = sb(s, "half", [P, 1])
            psH = [ps(s, f"psH{i}") for i in range(2)]
            psG = [ps(s, f"psG{i}") for i in range(2)]
            psU = [ps(s, f"psU{i}") for i in range(2)]

            tp = TablePass(s, "t0", x, table0, D, gA, ohA, psH[0], ea)
            w_ld = [sem(f"l0_weights{i}") for i in range(3)]
            clear = sem("l0_clear")
            idx_seen = sem("l0_idx_seen")
            idx_in = sem("l0_idx_in")
            gA_ld = [sem(f"l0_gA{i}") for i in range(Q)]
            mA_ld = [sem(f"l0_mA{i}") for i in range(Q)]
            gB_ld = [sem(f"l0_gB{i}") for i in range(2)]
            mB_ld = [sem(f"l0_mB{i}") for i in range(2)]
            xs_ld = [sem(f"l0_x{i}") for i in range(2 * Q)]
            d_st = [sem(f"l0_d{i}") for i in range(Q)]
            sumA = sem("l0_sumA")
            sumB = sem("l0_sumB")
            msgA = sem("l0_msgA")
            msgB = sem("l0_msgB")
            agg_done = sem("l0_agg_done")
            hT_in = sem("l0_hT_in")
            g1_done = sem("l0_g1_done")
            gT_in = sem("l0_gT_in")
            g2_done = sem("l0_g2_done")
            d_in = sem("l0_d_in")
            s1_in = sem("l0_s1_in")
            sq_in = sem("l0_sq_in")
            s2_in = sem("l0_s2_in")
            bn_sum = sem("bn_sum")
            bn_var = sem("bn_var")
            bn_pow = sem("bn_pow")
            bn_step = sem("bn_step")
            bn_row = [sem(f"bn_row{i}") for i in range(3)]

            with nc.Block() as block:
                @block.sync
                def _(sp):
                    tp.on_sync(sp)
                    sp.dma_start(w1s[:], w1.rearrange("(c p) n -> p c n", p=P)).then_inc(w_ld[0], 16)
                    sp.dma_start(b1s[:], b1).then_inc(w_ld[1], 16)
                    sp.dma_start(w2s[:], w2.rearrange("(c p) n -> p c n", p=P)).then_inc(w_ld[2], 16)
                    for i, r_ in enumerate((gamma, beta, b2)):
                        sp.dma_start(row[:, i, :], r_.to_broadcast([P, D])).then_inc(bn_row[i], 16)

                    def load(q, v, r):
                        for u in range(Q):
                            wait(sp, d_in, Q * q + u - 2 * Q + 1)
                            wait(sp, agg_done, Q * q + u - 2 * Q + 1)
                            sp.dma_start(xs[:, Q * v + u, :], x[rows(q * Q + u), :]).then_inc(xs_ld[Q * v + u], 16)

                    def store(q, v, r):
                        for u in range(Q):
                            wait(sp, d_in, Q * q + u + 1)
                            sp.dma_start(d_dram[rows(q * Q + u), :], ds[:, u, :]).then_inc(d_st[u], 16)
                    pipe(sp, [(load, 0), (store, 2)], NQ, 2)
                    for u in range(Q):
                        sp.wait_ge(d_st[u], 16 * NQ)

                @block.gpsimd
                def _(pool):
                    tp.on_gpsimd(pool)
                    pool.memset(gA[:], 0.0).then_inc(clear, 1)
                    pool.memset(mA[:], 0.0).then_inc(clear, 1)
                    pool.memset(gB[:], 0.0).then_inc(clear, 1)
                    pool.memset(mB[:], 0.0).then_inc(clear, 1)
                    pool.memset(half[:], -0.5).then_inc(clear, 1)
                    pool.memset(S2[:], 0.0).then_inc(clear, 1)
                    pool.wait_ge(clear, 6)
                    table_mode = pool.value_load(mode_i[0:1, 0:1], min_val=0, max_val=1)

                    def fetch(into, table, field, v, signal, bound):
                        pool.indirect_dma_start(
                            out=into, out_offset=None, in_=table,
                            in_offset=bass.IndirectOffsetOnAxis(ap=slotidx[:, v, field:field + 1], axis=0),
                            bounds_check=bound, oob_is_err=False).then_inc(signal, 16)

                    def gather(q, v, r):
                        for h in (0, 1):
                            k = q * 2 + h
                            for w in (gA_ld, mA_ld):
                                for u in (0, 1):
                                    wait(pool, w[2 * h + u], 16 * q)
                            wait(pool, gB_ld[h], 16 * q)
                            wait(pool, mB_ld[h], 16 * q)
                            nc.gpsimd.tensor_copy(slotidx[:, h, :], IDX[:, bass.ds(k, 1), :].rearrange("p a f -> p (a f)")
                                                  ).then_inc(idx_in, 1)
                            wait(pool, agg_done, Q * q + 2 * h + 2 - Q)
                            wait(pool, idx_in, k + 1)
                            pool.nop().then_inc(idx_seen, 1)
                            for u in (0, 1):
                                t = 2 * h + u
                                fetch(gA[:, t, :], x, SRC_A + u, h, gA_ld[t], N - 1)
                            fetch(gB[:, h, :], x, SRC_B, h, gB_ld[h], N - 1)
                            with pool.If(table_mode > 0):
                                for u in (0, 1):
                                    t = 2 * h + u
                                    fetch(mA[:, t, :], table0, EID_A + u, h, mA_ld[t], NP - 1)
                            with pool.Else():
                                for u in (0, 1):
                                    t = 2 * h + u
                                    fetch(mA[:, t, :], ea, EID_A + u, h, mA_ld[t], N - 1)
                            fetch(mB[:, h, :], ea, EID_B, h, mB_ld[h], N - 1)

                    def squares(q, v, r):
                        for u in range(Q):
                            wait(pool, sq_in, Q * q + u + 1)
                            wait(pool, s2_in, Q * q + u)
                            nc.gpsimd.tensor_tensor(S2[:], S2[:], sq[:, u % 2, :], ALU.add).then_inc(s2_in, 1)
                    pipe(pool, [(gather, 0), (squares, 1)], NQ, 2)
                    pool.wait_ge(bn_var, 1)
                    for c in range(DC):
                        o = slice(c * P, (c + 1) * P)
                        last_one = nc.gpsimd.tensor_tensor(aB[:, o], var[:, o], half[:].to_broadcast([P, P]), ALU.pow)
                    last_one.then_inc(bn_pow, 1)

                @block.vector
                def _(dve):
                    tp.on_vector(dve)
                    V = nc.vector
                    V.memset(S1[:], 0.0).then_inc(s1_in, 1)
                    dve.wait_ge(clear, 4)

                    def messages(q, v, r):
                        for u in range(Q):
                            t = Q * q + u
                            dve.wait_ge(gA_ld[u], 16 * (q + 1))
                            dve.wait_ge(mA_ld[u], 16 * (q + 1))
                            wait(dve, agg_done, t + 1 - Q)
                            V.tensor_scalar(ohA[:, u, :], iota[:], dlA[:, bass.ds(t, 1)], None, ALU.is_equal)
                            V.tensor_tensor(mA[:, u, :], mA[:, u, :], gA[:, u, :], ALU.add).then_inc(sumA, 1)
                            if u % 2 == 0:
                                h = u // 2
                                wait(dve, agg_done, t + 2 - Q)
                                V.tensor_scalar(ohB[:, h, :], iota[:], dlB[:, bass.ds(q * 2 + h, 1)], None,
                                                ALU.is_equal)
                                dve.wait_ge(gB_ld[h], 16 * (q + 1))
                                dve.wait_ge(mB_ld[h], 16 * (q + 1))
                                V.tensor_tensor(mB[:, h, :], mB[:, h, :], gB[:, h, :], ALU.add).then_inc(sumB, 1)

                    def residual(q, v, r):
                        for u in range(Q):
                            t = Q * q + u
                            dve.wait_ge(g2_done, t + 1)
                            wait(dve, d_st[u], 16 * q)
                            wait(dve, sq_in, t + 1 - Q)
                            V.tensor_tensor(ds[:, u, :], psU[u % 2][:, :], xs[:, Q * v + u, :], ALU.add).then_inc(d_in, 1)
                            dve.wait_ge(d_in, t + 1)
                            dve.wait_ge(s1_in, t + 1)
                            V.scalar_tensor_tensor(out=S1[:], in0=ds[:, u, :], scalar=real[:, bass.ds(t, 1)], in1=S1[:],
                                                   op0=ALU.mult, op1=ALU.add).then_inc(s1_in, 1)
                    pipe(dve, [(messages, 0), (residual, 1)], NQ, 2)
                    n = [0]

                    def step(ins):
                        n[0] += 1
                        ins.then_inc(bn_step, 1)
                        dve.wait_ge(bn_step, n[0])
                    dve.wait_ge(bn_sum, 1)
                    for i in range(3):
                        dve.wait_ge(bn_row[i], 16)
                    step(V.tensor_scalar(mean[:], psH[0][:, :], 1.0 / N, None, ALU.mult))
                    step(V.tensor_scalar(var[:], psH[1][:, :], 1.0 / N, EPS, ALU.mult, ALU.add))
                    step(V.tensor_tensor(cB[:], mean[:], mean[:], ALU.mult))
                    V.tensor_tensor(var[:], var[:], cB[:], ALU.subtract).then_inc(bn_var, 1)
                    step(V.tensor_tensor(mean[:], mean[:], row[:, 2, :], ALU.add))
                    step(V.tensor_tensor(cB[:], row[:, 2, :], mean[:], ALU.subtract))
                    dve.wait_ge(bn_pow, 1)
                    step(V.tensor_tensor(aB[:], aB[:], row[:, 0, :], ALU.mult))
                    step(V.tensor_tensor(cB[:], cB[:], aB[:], ALU.mult))
                    step(V.tensor_tensor(cB[:], cB[:], row[:, 1, :], ALU.add))

                @block.scalar
                def _(act):
                    def messages(q, v, r):
                        for u in range(Q):
                            t = Q * q + u
                            act.wait_ge(sumA, t + 1)
                            nc.scalar.activation(mA[:, u, :], mA[:, u, :], ACT.Relu).then_inc(msgA, 1)
                            if u % 2 == 0:
                                h = u // 2
                                act.wait_ge(sumB, 2 * q + h + 1)
                                nc.scalar.activation(mB[:, h, :], mB[:, h, :], ACT.Relu).then_inc(msgB, 1)

                    def relus(q, v, r):
                        for c in range(DC):
                            act.wait_ge(g1_done, DC * q + c + 1)
                            wait(act, g2_done, Q * q)
                            nc.scalar.activation(gT[:, c, :], psG[c % 2][:, :], ACT.Relu,
                                                 bias=b1s[:, c:c + 1]).then_inc(gT_in, 1)

                    def turned(q, v, r):
                        for u in range(Q):
                            act.wait_ge(agg_done, Q * q + u + 1)
                            wait(act, g1_done, DC * q)
                            nc.scalar.activation(hT[:, :, u * P:(u + 1) * P],
                                                 psH[u % 2][:, :].rearrange("p (c n) -> p c n", c=DC),
                                                 ACT.Copy).then_inc(hT_in, 1)

                    def squares(q, v, r):
                        for u in range(Q):
                            t = Q * q + u
                            act.wait_ge(d_in, t + 1)
                            wait(act, s2_in, t - 1)
                            nc.scalar.activation(sq[:, u % 2, :], ds[:, u, :], ACT.Square,
                                                 scale=real[:, bass.ds(t, 1)]).then_inc(sq_in, 1)
                    act.wait_ge(w_ld[1], 16)
                    pipe(act, [(messages, 0), (relus, 1), (turned, 0), (squares, 1)], NQ, 2)

                @block.tensor
                def _(pe):
                    tp.on_tensor(pe)
                    mm = nc.tensor.matmul

                    def sums(q, v, r):
                        for u in range(Q):
                            t = Q * q + u
                            half_ = slice((u % 2) * HALF, (u % 2 + 1) * HALF)
                            pe.wait_ge(xs_ld[Q * v + u], 16 * (r + 1))
                            pe.wait_ge(msgA, t + 1)
                            pe.wait_ge(msgB, 2 * q + u // 2 + 1)
                            wait(pe, hT_in, t - 1)
                            for c in range(DC):
                                o, f = psH[u % 2][:, c * P:(c + 1) * P], slice(c * P, (c + 1) * P)
                                mm(o, xs[:, Q * v + u, f], ident[:], start=True, stop=False)
                                mm(o, mA[:, u, f], ohA[:, u, :], start=False, stop=False)
                                last_one = mm(o, mB[half_, u // 2, f], ohB[half_, u // 2, :], start=False, stop=True)
                            last_one.then_inc(agg_done, 1)

                    def first(q, v, r):
                        pe.wait_ge(hT_in, Q * q + Q)
                        for m in range(DC):
                            wait(pe, gT_in, DC * q + m - 1)
                            for c in range(DC):
                                last_one = mm(psG[m % 2][:, :], w1s[:, c, m * P:(m + 1) * P], hT[:, c, :],
                                              start=c == 0, stop=c == DC - 1)
                            last_one.then_inc(g1_done, 1)

                    def second(q, v, r):
                        pe.wait_ge(gT_in, DC * q + DC)
                        for u in range(Q):
                            wait(pe, d_in, Q * q + u - 1)
                            for c in range(DC):
                                last_one = mm(psU[u % 2][:, :], gT[:, c, u * P:(u + 1) * P], w2s[:, c, :],
                                              start=c == 0, stop=c == DC - 1)
                            last_one.then_inc(g2_done, 1)
                    pe.wait_ge(w_ld[0], 16)
                    pe.wait_ge(w_ld[2], 16)
                    pipe(pe, [(first, 1), (sums, 0), (second, 1)], NQ, 2)
                    pe.wait_ge(s1_in, NT + 1)
                    pe.wait_ge(hT_in, NT)
                    mm(psH[0][:, :], ones[:], S1[:], start=True, stop=True)
                    pe.wait_ge(s2_in, NT)
                    mm(psH[1][:, :], ones[:], S2[:], start=True, stop=True).then_inc(bn_sum, 1)
            end_phase()

        X = sb(ctx, "X", [P, NT, D])

        class Norm:

            def __init__(self, scope, name, slots, y=None):
                self.slots = slots
                self.y = sb(scope, f"{name}_y", [P, slots, D]) if y is None else y
                self.st = sb(scope, f"{name}_st", [P, slots, 6])
                self.mv = sb(scope, f"{name}_mv", [P, slots, 2])
                self.ve = sb(scope, f"{name}_ve", [P, slots])
                self.rs = sb(scope, f"{name}_rs", [P, slots])
                self.half = sb(scope, f"{name}_half", [P, 1])
                self.y_in = sem(f"{name}_y_in")
                self.st_in = sem(f"{name}_st_in")
                self.st_seen = sem(f"{name}_st_seen")
                self.mv_in = sem(f"{name}_mv_in")
                self.ve_in = sem(f"{name}_ve_in")
                self.rs_in = sem(f"{name}_rs_in")
                self.x_in = sem(f"{name}_x_in")
                self.half_in = sem(f"{name}_half_in")

            def statistics(self, dve, t, u, at=None):
                at = u if at is None else at
                V = nc.vector
                dve.wait_ge(self.y_in, t + 1)
                V.bn_stats(self.st[:, u, :], self.y[:, at, :]).then_inc(self.st_in, 1)
                dve.wait_ge(self.st_in, t + 1)
                dve.nop().then_inc(self.st_seen, 1)
                V.bn_aggr(self.mv[:, u, :], self.st[:, u, :]).then_inc(self.mv_in, 1)
                dve.wait_ge(self.mv_in, t + 1)
                wait(dve, self.rs_in, t + 1 - self.slots)
                V.tensor_scalar(self.ve[:, u:u + 1], self.mv[:, u, 1:2], EPS, None, ALU.add).then_inc(self.ve_in, 1)

            def begin(self, pool):
                pool.memset(self.half[:], -0.5).then_inc(self.half_in, 1)
                pool.wait_ge(self.half_in, 1)

            def power(self, pool, t, u):
                pool.wait_ge(self.ve_in, t + 1)
                wait(pool, self.x_in, t + 1 - self.slots)
                nc.gpsimd.tensor_tensor(self.rs[:, u:u + 1], self.ve[:, u:u + 1], self.half[:],
                                        ALU.pow).then_inc(self.rs_in, 1)

            def apply(self, dve, t, u, to, at=None):
                at = u if at is None else at
                dve.wait_ge(self.rs_in, t + 1)
                nc.vector.tensor_scalar(to, self.y[:, at, :], self.mv[:, u, 0:1], self.rs[:, u:u + 1],
                                        ALU.subtract, ALU.mult).then_inc(self.x_in, 1)

        def state(t):
            return X[:, bass.ds(t, 1), :].rearrange("p a d -> p (a d)")

        with ExitStack() as s:
            ws = sb(s, "wts", [P, DC, D])
            bB = sb(s, "bB", [P, D])
            dl = sb(s, "n1_d", [P, Q, D])
            xl = sb(s, "n1_x", [P, Q, D])
            xT = sb(s, "n1_xT", [P, 2, D])
            hs = sb(s, "n1_h", [P, 2, D])
            ln = Norm(s, "n1", 2, xl)
            psT = [ps(s, f"n1_psT{i}") for i in range(2)]
            psU = [ps(s, f"n1_psU{i}") for i in range(2)]
            w_ld = [sem(f"n1_w{i}") for i in range(2)]
            d_ld = [sem(f"n1_d_ld{i}") for i in range(Q)]
            x_ld = [sem(f"n1_x_ld{i}") for i in range(Q)]
            h_st = [sem(f"n1_h_st{i}") for i in range(2)]
            da_in = sem("n1_da_in")
            xc_in = sem("n1_xc_in")
            X_in = sem("n1_X_in")
            T_done = sem("n1_T_done")
            xT_in = sem("n1_xT_in")
            G_done = sem("n1_G_done")
            hb_in = sem("n1_hb_in")
            h_in = sem("n1_h_in")

            with nc.Block() as block:
                @block.sync
                def _(sp):
                    sp.dma_start(ws[:], wt.rearrange("(c p) n -> p c n", p=P)).then_inc(w_ld[0], 16)
                    sp.dma_start(bB[:], b.to_broadcast([P, D])).then_inc(w_ld[1], 16)

                    def load(t, u, r):
                        wait(sp, X_in, t + 1 - Q)
                        wait(sp, T_done, t + 1 - Q)
                        sp.dma_start(dl[:, u, :], d_dram[rows(t), :]).then_inc(d_ld[u], 16)
                        sp.dma_start(xl[:, u, :], x[rows(t), :]).then_inc(x_ld[u], 16)

                    def store(t, u, r):
                        wait(sp, h_in, t + 1)
                        sp.dma_start(table1[rows(t), :], hs[:, u % 2, :]).then_inc(h_st[u % 2], 16)
                    pipe(sp, [(load, 0), (store, 6)], NT, Q)
                    for i in range(2):
                        sp.wait_ge(h_st[i], 16 * NT // 2)

                @block.gpsimd
                def _(pool):
                    ln.begin(pool)

                    def addend(t, u, r):
                        pool.wait_ge(x_ld[u], 16 * (r + 1))
                        nc.gpsimd.tensor_tensor(xl[:, u, :], xl[:, u, :], cB[:], ALU.add).then_inc(xc_in, 1)

                    def power(t, u, r):
                        ln.power(pool, t, u % 2)
                    pipe(pool, [(addend, 0), (power, 1)], NT, Q)

                @block.vector
                def _(dve):
                    V = nc.vector

                    def sum_(t, u, r):
                        dve.wait_ge(d_ld[u], 16 * (r + 1))
                        V.tensor_tensor(dl[:, u, :], dl[:, u, :], aB[:], ALU.mult).then_inc(da_in, 1)
                        dve.wait_ge(da_in, t + 1)
                        dve.wait_ge(xc_in, t + 1)
                        V.tensor_tensor(xl[:, u, :], dl[:, u, :], xl[:, u, :], ALU.add).then_inc(ln.y_in, 1)
                        ln.statistics(dve, t, u % 2, u)

                    def norm(t, u, r):
                        ln.apply(dve, t, u % 2, xl[:, u, :], u)

                    def bias(t, u, r):
                        dve.wait_ge(G_done, t + 1)
                        wait(dve, h_st[u % 2], 16 * (r * 2 + u // 2))
                        V.tensor_tensor(hs[:, u % 2, :], psU[u % 2][:, :], bB[:], ALU.add).then_inc(hb_in, 1)
                    dve.wait_ge(w_ld[1], 16)
                    pipe(dve, [(sum_, 0), (norm, 1), (bias, 3)], NT, Q)

                @block.scalar
                def _(act):
                    def keep(t, u, r):
                        act.wait_ge(ln.x_in, t + 1)
                        nc.scalar.activation(state(t), xl[:, u, :], ACT.Copy).then_inc(X_in, 1)

                    def turned(t, u, r):
                        act.wait_ge(T_done, t + 1)
                        wait(act, G_done, t - 1)
                        nc.scalar.activation(xT[:, u % 2, :], psT[u % 2][:, :], ACT.Copy).then_inc(xT_in, 1)

                    def scale(t, u, r):
                        act.wait_ge(hb_in, t + 1)
                        nc.scalar.activation(hs[:, u % 2, :], hs[:, u % 2, :], ACT.Copy,
                                             scale=dis1[:, bass.ds(t, 1)]).then_inc(h_in, 1)
                    pipe(act, [(keep, 1), (turned, 1), (scale, 3)], NT, Q)

                @block.tensor
                def _(pe):
                    def turn(t, u, r):
                        pe.wait_ge(ln.x_in, t + 1)
                        wait(pe, xT_in, t - 1)
                        for c in range(DC):
                            f = slice(c * P, (c + 1) * P)
                            last_one = nc.tensor.transpose(psT[u % 2][:, f], xl[:, u, f], ident[:])
                        last_one.then_inc(T_done, 1)

                    def product(t, u, r):
                        pe.wait_ge(xT_in, t + 1)
                        wait(pe, hb_in, t - 1)
                        for c in range(DC):
                            last_one = nc.tensor.matmul(psU[u % 2][:, :], xT[:, u % 2, c * P:(c + 1) * P], ws[:, c, :],
                                                        start=c == 0, stop=c == DC - 1)
                        last_one.then_inc(G_done, 1)
                    pe.wait_ge(w_ld[0], 16)
                    pipe(pe, [(turn, 0), (product, 1)], NT, Q)
            end_phase()

        full = sb(ctx, "full", [NT, D])

        with ExitStack() as s:
            slotidx = sb(s, "n2_idx", [P, 2, FIELDS], I32)
            gA = sb(s, "n2_gA", [P, Q, D])
            gB = sb(s, "n2_gB", [P, 2, D])
            hs = sb(s, "n2_hs", [P, Q, D])
            o = sb(s, "n2_o", [P, 2, D])
            ohA = sb(s, "n2_ohA", [P, Q, P])
            ohB = sb(s, "n2_ohB", [P, 2, P])
            kh = sb(s, "n2_kh", [P, 2, NT])
            ln = Norm(s, "n2", 2)
            psA = [ps(s, f"n2_psA{i}") for i in range(2)]
            psF = ps(s, "n2_psF")
            tp = TablePass(s, "t1", table1, sums1, D, gA, ohA, psA[0])
            clear = sem("n2_clear")
            idx_seen = sem("n2_idx_seen")
            idx_in = sem("n2_idx_in")
            gA_ld = [sem(f"n2_gA{i}") for i in range(Q)]
            gB_ld = [sem(f"n2_gB{i}") for i in range(2)]
            hs_ld = [sem(f"n2_hs{i}") for i in range(Q)]
            oh_in = sem("n2_oh_in")
            agg_done = sem("n2_agg_done")
            o_in = sem("n2_o_in")
            r_in = sem("n2_r_in")
            kh_in = sem("n2_kh_in")
            F_done = sem("n2_F_done")
            full_in = sem("n2_full_in")

            with nc.Block() as block:
                @block.sync
                def _(sp):
                    tp.on_sync(sp)
                    def load(t, u, r):
                        wait(sp, o_in, t + 1 - Q)
                        sp.dma_start(hs[:, u, :], table1[rows(t), :]).then_inc(hs_ld[u], 16)
                    pipe(sp, [(load, 0)], NT, Q)

                @block.gpsimd
                def _(pool):
                    tp.on_gpsimd(pool)
                    ln.begin(pool)
                    pool.memset(gA[:], 0.0).then_inc(clear, 1)
                    pool.memset(gB[:], 0.0).then_inc(clear, 1)
                    pool.wait_ge(clear, 2)

                    table_mode = pool.value_load(mode_i[0:1, 0:1], min_val=0, max_val=1)

                    def fetch(into, table, field, v, signal):
                        pool.indirect_dma_start(
                            out=into, out_offset=None, in_=table,
                            in_offset=bass.IndirectOffsetOnAxis(ap=slotidx[:, v, field:field + 1], axis=0),
                            bounds_check=NP - 1, oob_is_err=False).then_inc(signal, 16)

                    def gather(t, u, r):
                        if u % 2:
                            return
                        h = u // 2
                        k = r * 2 + h
                        wait(pool, gA_ld[u], 16 * r)
                        wait(pool, gA_ld[u + 1], 16 * r)
                        wait(pool, gB_ld[h], 16 * r)
                        nc.gpsimd.tensor_copy(slotidx[:, h, :], IDX[:, bass.ds(k, 1), :].rearrange("p a f -> p (a f)")
                                              ).then_inc(idx_in, 1)
                        wait(pool, agg_done, t + 2 - Q)
                        wait(pool, idx_in, k + 1)
                        pool.nop().then_inc(idx_seen, 1)
                        with pool.If(table_mode > 0):
                            fetch(gA[:, u, :], sums1, EID_A, h, gA_ld[u])
                            fetch(gA[:, u + 1, :], sums1, EID_A + 1, h, gA_ld[u + 1])
                        with pool.Else():
                            fetch(gA[:, u, :], table1, SRC_A, h, gA_ld[u])
                            fetch(gA[:, u + 1, :], table1, SRC_A + 1, h, gA_ld[u + 1])
                        fetch(gB[:, h, :], table1, SRC_B, h, gB_ld[h])

                    def power(t, u, r):
                        ln.power(pool, t, u % 2)
                    pipe(pool, [(gather, 0), (power, 4)], NT, Q)

                @block.vector
                def _(dve):
                    tp.on_vector(dve)
                    V = nc.vector
                    dve.wait_ge(clear, 2)

                    def hots(t, u, r):
                        wait(dve, agg_done, t + 1 - Q)
                        if u % 2 == 0:
                            wait(dve, agg_done, t + 2 - Q)
                            V.tensor_scalar(ohB[:, u // 2, :], iota[:], dlB[:, bass.ds(r * 2 + u // 2, 1)], None,
                                            ALU.is_equal)
                        V.tensor_scalar(ohA[:, u, :], iota[:], dlA[:, bass.ds(t, 1)], None,
                                        ALU.is_equal).then_inc(oh_in, 1)

                    def own(t, u, r):
                        dve.wait_ge(agg_done, t + 1)
                        dve.wait_ge(hs_ld[u], 16 * (r + 1))
                        wait(dve, r_in, t - 1)
                        V.tensor_tensor(o[:, u % 2, :], psA[u % 2][:, :], hs[:, u, :], ALU.add).then_inc(o_in, 1)

                    def sum_(t, u, r):
                        dve.wait_ge(r_in, t + 1)
                        wait(dve, ln.x_in, t - 1)
                        V.tensor_tensor(ln.y[:, u % 2, :], o[:, u % 2, :], state(t), ALU.add).then_inc(ln.y_in, 1)
                        ln.statistics(dve, t, u % 2)

                    def norm(t, u, r):
                        wait(dve, F_done, t - 1)
                        V.tensor_scalar(kh[:, u % 2, :], keys[:], skey[:, bass.ds(t, 1)], None,
                                        ALU.is_equal).then_inc(kh_in, 1)
                        ln.apply(dve, t, u % 2, state(t))
                    pipe(dve, [(hots, 0), (own, 1), (sum_, 2), (norm, 3)], NT, Q)
                    dve.wait_ge(full_in, 1)
                    V.tensor_copy(full[:], psF[0:NT, :])

                @block.scalar
                def _(act):
                    def relu(t, u, r):
                        act.wait_ge(o_in, t + 1)
                        nc.scalar.activation(o[:, u % 2, :], o[:, u % 2, :], ACT.Relu,
                                             scale=dis1[:, bass.ds(t, 1)]).then_inc(r_in, 1)
                    pipe(act, [(relu, 0)], NT, Q)

                @block.tensor
                def _(pe):
                    tp.on_tensor(pe)
                    mm = nc.tensor.matmul
                    mm(psF[0:NT, :], zeros_h[:, 0:NT], zeros_h[:], start=True, stop=False)

                    def sums(t, u, r):
                        h, half_ = u // 2, slice((u % 2) * HALF, (u % 2 + 1) * HALF)
                        pe.wait_ge(oh_in, t + 1)
                        pe.wait_ge(gA_ld[u], 16 * (r + 1))
                        pe.wait_ge(gB_ld[h], 16 * (r + 1))
                        wait(pe, o_in, t - 1)
                        mm(psA[u % 2][:, :], ohA[:, u, :], gA[:, u, :], start=True, stop=False)
                        mm(psA[u % 2][:, :], ohB[half_, h, :], gB[half_, h, :], start=False,
                           stop=True).then_inc(agg_done, 1)

                    def segments(t, u, r):
                        pe.wait_ge(ln.x_in, t + 1)
                        mm(psF[0:NT, :], kh[:, u % 2, :], state(t), start=False, stop=False).then_inc(F_done, 1)
                    pipe(pe, [(sums, 0), (segments, 3)], NT, Q)
                    mm(psF[0:NT, :], zeros_h[:, 0:NT], zeros_h[:], start=False, stop=True).then_inc(full_in, 1)
            end_phase()

        with ExitStack() as s:
            ws = sb(s, "wcs", [P, DC, HID])
            rid = sb(s, "n3_rid", [P, Q, P])
            inm = sb(s, "n3_in", [P, 2, P])
            ek = sb(s, "n3_ek", [NT, 2, P])
            xn = sb(s, "n3_xn", [P, 2, D])
            xT = sb(s, "n3_xT", [P, 2, D])
            hs = sb(s, "n3_h", [P, 2, HID])
            ln = Norm(s, "n3", 2)
            psM = [ps(s, f"n3_psM{i}") for i in range(2)]
            psT = [ps(s, f"n3_psT{i}") for i in range(2)]
            psU = [ps(s, f"n3_psU{i}") for i in range(2)]
            w_ld = sem("n3_w")
            rid_ld = [sem(f"n3_rid{i}") for i in range(Q)]
            h_st = [sem(f"n3_h_st{i}") for i in range(2)]
            sel_in = sem("n3_sel_in")
            M_done = sem("n3_M_done")
            X_in = sem("n3_X_in")
            T_done = sem("n3_T_done")
            xT_in = sem("n3_xT_in")
            G_done = sem("n3_G_done")
            h_in = sem("n3_h_in")

            with nc.Block() as block:
                @block.sync
                def _(sp):
                    sp.dma_start(ws[:], wc.rearrange("(c p) n -> p c n", p=P)).then_inc(w_ld, 16)

                    def load(t, u, r):
                        wait(sp, sel_in, t + 1 - Q)
                        sp.dma_start(rid[:, u, :], rid_dram[bass.ds(t, 1), :].to_broadcast([P, P])).then_inc(rid_ld[u], 16)

                    def store(t, u, r):
                        wait(sp, h_in, t + 1)
                        sp.dma_start(table3[rows(t), :], hs[:, u % 2, :]).then_inc(h_st[u % 2], 16)
                    pipe(sp, [(load, 0), (store, 6)], NT, Q)
                    for i in range(2):
                        sp.wait_ge(h_st[i], 16 * NT // 2)

                @block.gpsimd
                def _(pool):
                    ln.begin(pool)
                    pipe(pool, [(lambda t, u, r: ln.power(pool, t, u % 2), 0)], NT, Q)

                @block.vector
                def _(dve):
                    V = nc.vector

                    def select(t, u, r):
                        dve.wait_ge(rid_ld[u], 16 * (r + 1))
                        wait(dve, M_done, t - 1)
                        V.tensor_scalar(inm[:, u % 2, :], rid[:, u, :], skey_in[:, bass.ds(t, 1)], None, ALU.is_equal)
                        V.tensor_scalar(ek[:, u % 2, :], rid[0:NT, u, :], keycol[:], None,
                                        ALU.is_equal).then_inc(sel_in, 1)

                    def sum_(t, u, r):
                        dve.wait_ge(M_done, t + 1)
                        wait(dve, ln.x_in, t - 1)
                        V.scalar_tensor_tensor(out=ln.y[:, u % 2, :], in0=psM[u % 2][:, :], scalar=rcnt[:, bass.ds(t, 1)],
                                               in1=state(t), op0=ALU.mult, op1=ALU.add).then_inc(ln.y_in, 1)
                        ln.statistics(dve, t, u % 2)

                    def norm(t, u, r):
                        wait(dve, X_in, t - 1)
                        wait(dve, T_done, t - 1)
                        ln.apply(dve, t, u % 2, xn[:, u % 2, :])
                    pipe(dve, [(select, 0), (sum_, 1), (norm, 2)], NT, Q)

                @block.scalar
                def _(act):
                    def keep(t, u, r):
                        act.wait_ge(ln.x_in, t + 1)
                        nc.scalar.activation(state(t), xn[:, u % 2, :], ACT.Copy).then_inc(X_in, 1)

                    def turned(t, u, r):
                        act.wait_ge(T_done, t + 1)
                        wait(act, G_done, t - 1)
                        nc.scalar.activation(xT[:, u % 2, :], psT[u % 2][:, :], ACT.Copy).then_inc(xT_in, 1)

                    def scale(t, u, r):
                        act.wait_ge(G_done, t + 1)
                        wait(act, h_st[u % 2], 16 * (r * 2 + u // 2))
                        nc.scalar.activation(hs[:, u % 2, :], psU[u % 2][:, 0:HID], ACT.Copy,
                                             scale=dis3[:, bass.ds(t, 1)]).then_inc(h_in, 1)
                    pipe(act, [(keep, 0), (turned, 0), (scale, 1)], NT, Q)

                @block.tensor
                def _(pe):
                    mm = nc.tensor.matmul

                    def means(t, u, r):
                        pe.wait_ge(sel_in, t + 1)
                        wait(pe, ln.y_in, t - 1)
                        mm(psM[u % 2][:, :], ek[:, u % 2, :], full[:], start=True, stop=False)
                        mm(psM[u % 2][:, :], inm[:, u % 2, :], state(t), start=False, stop=True).then_inc(M_done, 1)

                    def turn(t, u, r):
                        pe.wait_ge(ln.x_in, t + 1)
                        wait(pe, xT_in, t - 1)
                        for c in range(DC):
                            f = slice(c * P, (c + 1) * P)
                            last_one = nc.tensor.transpose(psT[u % 2][:, f], xn[:, u % 2, f], ident[:])
                        last_one.then_inc(T_done, 1)

                    def product(t, u, r):
                        pe.wait_ge(xT_in, t + 1)
                        wait(pe, h_in, t - 1)
                        for c in range(DC):
                            last_one = mm(psU[u % 2][:, 0:HID], xT[:, u % 2, c * P:(c + 1) * P], ws[:, c, :],
                                          start=c == 0, stop=c == DC - 1)
                        last_one.then_inc(G_done, 1)
                    pe.wait_ge(w_ld, 16)
                    pipe(pe, [(means, 0), (turn, 2), (product, 3)], NT, Q)
            end_phase()

        with ExitStack() as s:
            ws = sb(s, "wls", [HID, D])
            bcs = sb(s, "bcs", [HID, 1])
            bcB = sb(s, "bcB", [HID, P])
            blB = sb(s, "blB", [P, D])
            cl = sb(s, "cl", [P, D])
            slotidx = sb(s, "n4_idx", [P, 2, FIELDS], I32)
            gA = sb(s, "n4_gA", [P, Q, HID])
            gB = sb(s, "n4_gB", [P, 2, HID])
            hs = sb(s, "n4_hs", [P, Q, HID])
            ohA = sb(s, "n4_ohA", [P, Q, P])
            ohB = sb(s, "n4_ohB", [P, 2, P])
            aT = sb(s, "n4_aT", [HID, 2, P])
            xc = sb(s, "n4_xc", [P, 2, D])
            xo = sb(s, "n4_xo", [P, 2, D])
            ln = Norm(s, "n4", 2)
            psA = [ps(s, f"n4_psA{i}") for i in range(2)]
            psO = [ps(s, f"n4_psO{i}") for i in range(2)]
            psC = ps(s, "n4_psC")
            w_ld = [sem(f"n4_w{i}") for i in range(3)]
            tp = TablePass(s, "t3", table3, sums3, HID, gA, ohA, psA[0])
            clear = sem("n4_clear")
            bc_in = sem("n4_bc_in")
            cl_done = sem("n4_cl_done")
            cl_in = sem("n4_cl_in")
            idx_seen = sem("n4_idx_seen")
            idx_in = sem("n4_idx_in")
            gA_ld = [sem(f"n4_gA{i}") for i in range(Q)]
            gB_ld = [sem(f"n4_gB{i}") for i in range(2)]
            hs_ld = [sem(f"n4_hs{i}") for i in range(Q)]
            o_st = [sem(f"n4_o_st{i}") for i in range(2)]
            oh_in = sem("n4_oh_in")
            agg_done = sem("n4_agg_done")
            aT_in = sem("n4_aT_in")
            O_done = sem("n4_O_done")
            xc_in = sem("n4_xc_in")

            with nc.Block() as block:
                @block.sync
                def _(sp):
                    tp.on_sync(sp)
                    sp.dma_start(ws[:], wl).then_inc(w_ld[0], 16)
                    sp.dma_start(bcs[:], bc).then_inc(w_ld[1], 16)
                    sp.dma_start(blB[:], bl.to_broadcast([P, D])).then_inc(w_ld[2], 16)

                    def load(t, u, r):
                        wait(sp, agg_done, t + 1 - Q)
                        sp.dma_start(hs[:, u, :], table3[rows(t), :]).then_inc(hs_ld[u], 16)

                    def store(t, u, r):
                        wait(sp, ln.x_in, t + 1)
                        sp.dma_start(out[rows(t), :], xo[:, u % 2, :]).then_inc(o_st[u % 2], 16)
                    pipe(sp, [(load, 0), (store, 6)], NT, Q)
                    for i in range(2):
                        sp.wait_ge(o_st[i], 16 * NT // 2)

                @block.gpsimd
                def _(pool):
                    tp.on_gpsimd(pool)
                    ln.begin(pool)
                    pool.memset(gA[:], 0.0).then_inc(clear, 1)
                    pool.memset(gB[:], 0.0).then_inc(clear, 1)
                    pool.wait_ge(clear, 2)
                    pool.wait_ge(cl_in, 1)

                    table_mode = pool.value_load(mode_i[0:1, 0:1], min_val=0, max_val=1)

                    def fetch(into, table, field, v, signal):
                        pool.indirect_dma_start(
                            out=into, out_offset=None, in_=table,
                            in_offset=bass.IndirectOffsetOnAxis(ap=slotidx[:, v, field:field + 1], axis=0),
                            bounds_check=NP - 1, oob_is_err=False).then_inc(signal, 16)

                    def gather(t, u, r):
                        if u % 2:
                            return
                        h = u // 2
                        k = r * 2 + h
                        wait(pool, gA_ld[u], 16 * r)
                        wait(pool, gA_ld[u + 1], 16 * r)
                        wait(pool, gB_ld[h], 16 * r)
                        nc.gpsimd.tensor_copy(slotidx[:, h, :], IDX[:, bass.ds(k, 1), :].rearrange("p a f -> p (a f)")
                                              ).then_inc(idx_in, 1)
                        wait(pool, agg_done, t + 2 - Q)
                        wait(pool, idx_in, k + 1)
                        pool.nop().then_inc(idx_seen, 1)
                        with pool.If(table_mode > 0):
                            fetch(gA[:, u, :], sums3, EID_A, h, gA_ld[u])
                            fetch(gA[:, u + 1, :], sums3, EID_A + 1, h, gA_ld[u + 1])
                        with pool.Else():
                            fetch(gA[:, u, :], table3, SRC_A, h, gA_ld[u])
                            fetch(gA[:, u + 1, :], table3, SRC_A + 1, h, gA_ld[u + 1])
                        fetch(gB[:, h, :], table3, SRC_B, h, gB_ld[h])

                    def addend(t, u, r):
                        wait(pool, ln.y_in, t - 1)
                        nc.gpsimd.tensor_tensor(xc[:, u % 2, :], state(t), cl[:], ALU.add).then_inc(xc_in, 1)

                    def power(t, u, r):
                        ln.power(pool, t, u % 2)
                    pipe(pool, [(gather, 0), (addend, 1), (power, 4)], NT, Q)

                @block.vector
                def _(dve):
                    tp.on_vector(dve)
                    V = nc.vector
                    dve.wait_ge(w_ld[1], 16)
                    V.tensor_scalar(bcB[:], ones[:], bcs[:], None, ALU.mult).then_inc(bc_in, 1)
                    dve.wait_ge(w_ld[2], 16)
                    dve.wait_ge(cl_done, 1)
                    V.tensor_tensor(cl[:], psC[:, :], blB[:], ALU.add).then_inc(cl_in, 1)
                    dve.wait_ge(clear, 2)

                    def hots(t, u, r):
                        wait(dve, agg_done, t + 1 - Q)
                        if u % 2 == 0:
                            wait(dve, agg_done, t + 2 - Q)
                            V.tensor_scalar(ohB[:, u // 2, :], iota[:], dlB[:, bass.ds(r * 2 + u // 2, 1)], None,
                                            ALU.is_equal)
                        V.tensor_scalar(ohA[:, u, :], iota[:], dlA[:, bass.ds(t, 1)], None,
                                        ALU.is_equal).then_inc(oh_in, 1)

                    def sum_(t, u, r):
                        dve.wait_ge(O_done, t + 1)
                        dve.wait_ge(xc_in, t + 1)
                        wait(dve, ln.x_in, t - 1)
                        V.scalar_tensor_tensor(out=ln.y[:, u % 2, :], in0=psO[u % 2][:, :], scalar=dis3[:, bass.ds(t, 1)],
                                               in1=xc[:, u % 2, :], op0=ALU.mult, op1=ALU.add).then_inc(ln.y_in, 1)
                        ln.statistics(dve, t, u % 2)

                    def norm(t, u, r):
                        wait(dve, o_st[u % 2], 16 * (r * 2 + u // 2))
                        ln.apply(dve, t, u % 2, xo[:, u % 2, :])
                    pipe(dve, [(hots, 0), (sum_, 2), (norm, 3)], NT, Q)

                @block.scalar
                def _(act):
                    def turned(t, u, r):
                        act.wait_ge(agg_done, t + 1)
                        wait(act, O_done, t - 1)
                        nc.scalar.activation(aT[:, u % 2, :], psA[u % 2][:, 0:P], ACT.Copy).then_inc(aT_in, 1)
                    pipe(act, [(turned, 0)], NT, Q)

                @block.tensor
                def _(pe):
                    tp.on_tensor(pe)
                    mm = nc.tensor.matmul
                    pe.wait_ge(w_ld[0], 16)
                    pe.wait_ge(bc_in, 1)
                    mm(psC[:, :], bcB[:], ws[:], start=True, stop=True).then_inc(cl_done, 1)

                    def sums(t, u, r):
                        h, half_ = u // 2, slice((u % 2) * HALF, (u % 2 + 1) * HALF)
                        pe.wait_ge(oh_in, t + 1)
                        pe.wait_ge(gA_ld[u], 16 * (r + 1))
                        pe.wait_ge(gB_ld[h], 16 * (r + 1))
                        pe.wait_ge(hs_ld[u], 16 * (r + 1))
                        wait(pe, aT_in, t - 1)
                        to = psA[u % 2][:, 0:P]
                        mm(to, hs[:, u, :], ident[:], start=True, stop=False)
                        mm(to, gA[:, u, :], ohA[:, u, :], start=False, stop=False)
                        mm(to, gB[half_, h, :], ohB[half_, h, :], start=False, stop=True).then_inc(agg_done, 1)

                    def product(t, u, r):
                        pe.wait_ge(aT_in, t + 1)
                        wait(pe, ln.y_in, t - 1)
                        mm(psO[u % 2][:, :], aT[:, u % 2, :], ws[:], start=True, stop=True).then_inc(O_done, 1)
                    pipe(pe, [(sums, 0), (product, 1)], NT, Q)


def _search_path():
    low, high = np.zeros(E + 1, np.int64), np.full(E + 1, E)
    mids, rights = [], []
    for _ in range(LEVELS):
        mid = low + (high - low) // 2
        right = np.arange(E + 1) > mid
        mids.append(mid)
        rights.append(right)
        low, high = np.where(right, mid, low), np.where(right, high, mid)
    return np.minimum(np.stack(mids, 1), E - 1), np.stack(rights, 1)


def _columns(a, fill=0):
    a = np.concatenate([a, np.full((NP - len(a), *a.shape[1:]), fill, a.dtype)])
    return np.ascontiguousarray(np.swapaxes(a.reshape(NT, P, *a.shape[1:]), 0, 1))


def _layout(i):
    i = {k: np.asarray(v) for k, v in i.items()}
    src, dst = i["src"], i["dst"]
    pad = np.full(NP + RUN + P - E, 2 * E, np.int32)
    srcp, dstp = np.concatenate([src, pad]), np.concatenate([dst, pad])
    mids, rights = _search_path()
    before = (np.arange(E + 1) - 1) % E
    left = np.where(rights, FAR, 0).astype(np.float32)
    return {
        "x": np.concatenate([i["x"], np.zeros((NP - N, D), np.float32)]),
        "ea": np.concatenate([i["edge_attr_512"], np.zeros((NP - E, D), np.float32)]),
        "src_cols": _columns(src, 2 * E), "dst_cols": _columns(dst, 2 * E),
        "runs": np.stack([np.concatenate([srcp[r * P:r * P + RUN], dstp[r * P:r * P + RUN]]) for r in range(NT)]),
        "dst_steps": np.stack([dstp[r * NT:r * NT + NT + 1] for r in range(P)]),
        "path": _columns(src[mids]),
        "path_right": _columns(rights.astype(np.float32)),
        "path_left": _columns(left, -FAR),
        "leaf_dst": _columns(dst[before]), "leaf_src": _columns(src[before]),
        "dst_rows": dstp[:NP].reshape(NT, P),
        "w1": i["L0_gnn_W1"], "b1": np.ascontiguousarray(i["L0_gnn_b1"].reshape(DC, P).T),
        "w2": i["L0_gnn_W2"], "b2": i["L0_gnn_b2"].reshape(1, D),
        "gamma": i["L0_gnn_gamma"].reshape(1, D), "beta": i["L0_gnn_beta"].reshape(1, D),
        "wt": np.ascontiguousarray(i["L1_gnn_W"].T), "b": i["L1_gnn_b"].reshape(1, D),
        "wc": i["L3_gnn_W_conv"], "bc": i["L3_gnn_b_conv"].reshape(HID, 1),
        "wl": i["L3_gnn_W_lin"], "bl": i["L3_gnn_b_lin"].reshape(1, D),
    }


def kernel(**inputs):
    import concourse.bacc as bacc
    from concourse.bass_utils import run_bass_kernel_spmd

    nc = bacc.Bacc("TRN2", target_bir_lowering=False, num_devices=1)
    arrays = {f"in_{k}": np.ascontiguousarray(a) for k, a in _layout(inputs).items()}
    args = [nc.dram_tensor(k, a.shape, mybir.dt.from_np(a.dtype), kind="ExternalInput").ap()
            for k, a in arrays.items()]
    args.append(nc.dram_tensor("out_x", [NP, D], F32, kind="ExternalOutput").ap())
    build(nc, *args)
    r = run_bass_kernel_spmd(nc, [arrays], core_ids=[0])
    return r.results[0]["out_x"][:N]
```

```python
from contextlib import ExitStack
import math

import numpy as np
import concourse.bass as bass
from concourse import mybir

F32 = mybir.dt.float32
F32R = mybir.dt.float32r
BF16 = mybir.dt.bfloat16
I32 = mybir.dt.int32
ALU = mybir.AluOpType
ACT = mybir.ActivationFunctionType
AX = mybir.AxisListType

P = 128
N = 10000
E = 10000
D = 512
HID = 128
DC = D // P
NT = 80
NP = NT * P
PAIRS = NT // 2
WINDOW = P + 64
HALF = WINDOW - P
RUN = 3 * P
LEVELS = math.ceil(math.log2(E + 1))
SKIP = 30000
FAR = 32768
EPS = 1e-5
FIELDS = 6
SRC_A, EID_A, SRC_B, EID_B = 0, 2, 4, 5


def build(nc, x, ea, src_cols, dst_cols, runs, dst_steps, path, path_right, path_left,
          leaf_dst, leaf_src, dst_rows, w1, b1, w2, bn_cols, wt, b, wc, bc, wl, bl, out):
    ctx = ExitStack()
    with ctx:
        live = []

        def sem(name):
            live.append(nc.alloc_semaphore(name))
            return live[-1]

        def end_phase():
            nc.clear_and_free_semaphores(live)
            nc.all_engine_barrier()
            live.clear()

        def sb(scope, name, shape, dt=F32):
            return scope.enter_context(nc.sbuf_tensor(name, shape, dt))

        def ps(scope, name, shape=(P, D), dt=F32):
            return scope.enter_context(nc.psum_tensor(name, list(shape), dt))

        def rows(t):
            return bass.ds(t * P, P)

        table0 = nc.dram_tensor("table0", [NP, D], F32).ap()
        table1 = nc.dram_tensor("table1", [NP, D], F32).ap()
        table3 = nc.dram_tensor("table3", [NP, HID], F32).ap()
        sums1 = nc.dram_tensor("sums1", [NP, D], F32).ap()
        sums3 = nc.dram_tensor("sums3", [NP, HID], F32).ap()
        d_dram = nc.dram_tensor("d_dram", [NP, D], F32).ap()
        rid_dram = nc.dram_tensor("rid_dram", [NT, P], F32).ap()

        iota = sb(ctx, "iota", [P, P])
        iota_h = sb(ctx, "iota_h", [P, P], BF16)
        pcol = sb(ctx, "pcol", [P, 1])
        ident = sb(ctx, "ident", [P, P])
        ones = sb(ctx, "ones", [P, P])
        zeros_h = sb(ctx, "zeros_h", [P, D], BF16)
        eps = sb(ctx, "eps", [P, 1])
        IDX = sb(ctx, "IDX", [P, PAIRS, FIELDS], I32)
        dlA = sb(ctx, "dlA", [P, NT])
        dlB = sb(ctx, "dlB", [P, PAIRS])
        dis1 = sb(ctx, "dis1", [P, NT])
        dis3 = sb(ctx, "dis3", [P, NT])
        real = sb(ctx, "real", [P, NT])
        skey = sb(ctx, "skey", [P, NT])
        skey_in = sb(ctx, "skey_in", [P, NT])
        rcnt = sb(ctx, "rcnt", [P, NT])
        keys = sb(ctx, "keys", [P, NT])
        keycol = sb(ctx, "keycol", [NT, 1])
        mode_i = sb(ctx, "mode_i", [P, 1], I32)

        ld = [sem(f"prep_load{i}") for i in range(10)]
        p_iota = sem("p_iota")
        p_dve = sem("p_dve")
        p_hot = sem("p_hot")
        p_hot_used = sem("p_hot_used")
        p_run = sem("p_run")
        ev = {name: sem(name) for name in (
            "degrees_summed", "node_counts", "tile_counts", "tile_counts_in", "starts", "blocks_in", "flags_in",
            "flags_summed", "fields_in", "fields_turned", "lasts_in", "lasts_turned", "carries_in",
            "carries_turned", "rids_in", "last_rids_in", "last_rids_turned", "key_rows_in", "keys_turned",
            "columns_in", "columns_turned")}
        p_sqrt = sem("p_sqrt")
        with ExitStack() as s:
            sc = sb(s, "sc", [P, NT], I32)
            dc = sb(s, "dc", [P, NT], I32)
            steps = sb(s, "steps", [P, NT + 1], I32)
            pth = sb(s, "pth", [P, NT, LEVELS], I32)
            pr = sb(s, "pr", [P, NT, LEVELS])
            pl = sb(s, "pl", [P, NT, LEVELS])
            pm = sb(s, "pm", [P, NT, LEVELS])
            ldst = sb(s, "ldst", [P, NT], I32)
            lsrc = sb(s, "lsrc", [P, NT], I32)
            iota_i = sb(s, "iota_i", [P, P], I32)
            pcol_i = sb(s, "pcol_i", [P, 1], I32)
            node_i = sb(s, "node_i", [NT, P], I32)
            nodec_i = sb(s, "nodec_i", [P, NT], I32)
            node = sb(s, "node", [NT, P])
            nodec = sb(s, "nodec", [P, NT])
            tri = sb(s, "tri", [NT, NT])
            part_i = sb(s, "part_i", [P, 8, NT], I32)
            part = sb(s, "part", [P, 8, NT])
            low = sb(s, "low", [P, NT])
            upp = sb(s, "upp", [P, NT])
            tmp = sb(s, "tmp", [P, NT])
            low_i = sb(s, "low_i", [P, NT], I32)
            colv = sb(s, "colv", [P, NT])
            hot = sb(s, "hot", [P, 2, 5, P], BF16)
            hot_leaf = sb(s, "hot_leaf", [P, 2, 4, P], BF16)
            deg = sb(s, "deg", [P, 2, NT])
            cntc = sb(s, "cntc", [NT, 1])
            startc = sb(s, "startc", [NT, 1])
            start_i = sb(s, "start_i", [NT, 3], I32)
            blk = sb(s, "blk", [NT, 1], I32)
            bits_i = sb(s, "bits_i", [NT, 7], I32)
            bits = sb(s, "bits", [NT, 7])
            run_i = sb(s, "run_i", [NT, 2 * RUN], I32)
            run = sb(s, "run", [NT, 2, 2, RUN])
            diff = sb(s, "diff", [NT, 2, RUN])
            flags = sb(s, "flags", [P, 2])
            mode = sb(s, "mode", [P, 1])
            a0 = sb(s, "a0", [NT, WINDOW + 1])
            vld = sb(s, "vld", [NT, WINDOW])
            nvl = sb(s, "nvl", [NT, WINDOW])
            alt = sb(s, "alt", [NT, 2, P])
            fld = sb(s, "fld", [NT, 6, P])
            dcmp = sb(s, "dcmp", [P, NT])
            sg = sb(s, "sg", [NT, 4, P])
            hold = sb(s, "hold", [NT, 6, P])
            last = sb(s, "last", [NT, 4])
            lrow = sb(s, "lrow", [1, 8, NT])
            carry = sb(s, "carry", [NT, 4])
            psD = ps(s, "psD")
            psS = ps(s, "psS")
            psL = ps(s, "psL")
            psX = ps(s, "psX")
            psY = ps(s, "psY")
            psZ = ps(s, "psZ")

            with nc.Block() as block:
                @block.sync
                def _(sp):
                    for i, (to, of) in enumerate(((sc, src_cols), (dc, dst_cols), (steps, dst_steps), (pth, path),
                                                  (pr, path_right), (pl, path_left), (ldst, leaf_dst),
                                                  (lsrc, leaf_src))):
                        sp.dma_start(to[:], of).then_inc(ld[i], 16)

                    sp.wait_ge(ev["rids_in"], 1)
                    sp.dma_start(rid_dram, sg[:, 2, :]).then_inc(ld[8], 16)
                    sp.wait_ge(ld[8], 16)

                @block.gpsimd
                def _(pool):
                    nc.gpsimd.iota(iota_i[:], [[1, P]], base=0, channel_multiplier=0).then_inc(p_iota, 1)
                    nc.gpsimd.iota(pcol_i[:], [[1, 1]], base=0, channel_multiplier=1).then_inc(p_iota, 1)
                    nc.gpsimd.iota(node_i[:], [[1, P]], base=0, channel_multiplier=P).then_inc(p_iota, 1)
                    nc.gpsimd.iota(nodec_i[:], [[P, NT]], base=0, channel_multiplier=1).then_inc(p_iota, 1)
                    pool.wait_ge(ev["blocks_in"], 1)
                    pool.indirect_dma_start(out=run_i[:], out_offset=None, in_=runs,
                                            in_offset=bass.IndirectOffsetOnAxis(ap=blk[:], axis=0)).then_inc(p_run, 16)

                @block.scalar
                def _(act):
                    act.wait_ge(p_sqrt, 1)
                    nc.scalar.activation(deg[:], deg[:], ACT.Sqrt).then_inc(p_sqrt, 1)

                @block.vector
                def _(dve):
                    n = [0]

                    def step(ins):
                        n[0] += 1
                        ins.then_inc(p_dve, 1)
                        dve.wait_ge(p_dve, n[0])

                    V = nc.vector
                    V.memset(ones[:], 1.0)
                    V.memset(zeros_h[:], 0.0)
                    V.memset(eps[:], EPS)
                    V.memset(flags[:], 0.0)
                    V.memset(lrow[:], 0.0)
                    V.memset(hot[:], 0.0)
                    dve.wait_ge(p_iota, 4)
                    V.tensor_copy(iota[:], iota_i[:])
                    V.tensor_copy(iota_h[:], iota_i[:])
                    V.tensor_copy(pcol[:], pcol_i[:])
                    V.tensor_copy(node[:], node_i[:])
                    step(V.tensor_copy(nodec[:], nodec_i[:]))
                    V.tensor_scalar(ident[:], iota[:], pcol[:], None, ALU.is_equal)
                    V.tensor_scalar(real[:], nodec[:], float(N), None, ALU.is_lt)
                    V.tensor_scalar(tri[:], iota[0:NT, 0:NT], pcol[0:NT], None, ALU.is_gt)
                    V.tensor_scalar(colv[:], iota[:, 0:NT], 1.0, None, ALU.add)
                    for i, c in enumerate((sc, dc)):
                        dve.wait_ge(ld[i], 16)
                        V.tensor_scalar(part_i[:, 2 * i, :], c[:], 7, None, ALU.arith_shift_right)
                        V.tensor_scalar(part_i[:, 2 * i + 1, :], c[:], P - 1, None, ALU.bitwise_and)
                    for i in (3, 4, 5):
                        dve.wait_ge(ld[i], 16)
                    step(V.tensor_tensor(pm[:], pth[:], pr[:], ALU.mult))
                    step(V.tensor_reduce(low[:], pm[:], AX.X, ALU.max))
                    step(V.tensor_tensor(pm[:], pth[:], pl[:], ALU.add))
                    step(V.tensor_reduce(upp[:], pm[:], AX.X, ALU.min))
                    step(V.tensor_tensor(tmp[:], low[:], upp[:], ALU.is_ge))
                    step(V.scalar_tensor_tensor(out=low[:], in0=tmp[:], scalar=float(FAR), in1=low[:],
                                                op0=ALU.mult, op1=ALU.add))
                    step(V.tensor_copy(low_i[:], low[:]))
                    V.tensor_scalar(part_i[:, 4, :], low_i[:], 7, None, ALU.arith_shift_right)
                    V.tensor_scalar(part_i[:, 5, :], low_i[:], P - 1, None, ALU.bitwise_and)
                    for i in (6, 7):
                        dve.wait_ge(ld[i], 16)
                    step(V.tensor_tensor(tmp[:], ldst[:], lsrc[:], ALU.subtract))
                    step(V.tensor_scalar(tmp[:], tmp[:], 1.0, None, ALU.add))
                    step(V.tensor_copy(low_i[:], tmp[:]))
                    V.tensor_scalar(part_i[:, 6, :], low_i[:], 7, None, ALU.arith_shift_right)
                    step(V.tensor_scalar(part_i[:, 7, :], low_i[:], P - 1, None, ALU.bitwise_and))
                    step(V.tensor_copy(part[:], part_i[:]))
                    with dve.Fori(0, PAIRS) as k:
                        for u in (0, 1):
                            c = k * 2 + u
                            dve.wait_ge(p_hot_used, c + 1)

                            def col(f):
                                return part[:, f, bass.ds(c, 1)]
                            V.tensor_scalar(hot[:, u, 0, :], iota_h[:], col(1), None, ALU.is_equal)
                            V.tensor_scalar(hot[:, u, 1, 0:NT], iota_h[:, 0:NT], col(0), None, ALU.is_equal)
                            V.tensor_scalar(hot[:, u, 2, :], iota_h[:], col(3), None, ALU.is_equal)
                            V.tensor_scalar(hot[:, u, 3, 0:NT], iota_h[:, 0:NT], col(2), None, ALU.is_equal)
                            V.tensor_scalar(hot[:, u, 4, 0:NT], iota_h[:, 0:NT], col(4), None, ALU.is_equal)
                            for f, by in enumerate((colv[:, bass.ds(c, 1)], pcol[:], col(6), col(7))):
                                last_one = V.tensor_scalar(hot_leaf[:, u, f, :], iota_h[:], col(5), by,
                                                           ALU.is_equal, ALU.mult)
                            last_one.then_inc(p_hot, 1)
                    dve.wait_ge(ev["degrees_summed"], 1)
                    step(V.tensor_scalar(deg[:, 0, :], psS[:, 0:NT], 1.0, None, ALU.add))
                    V.tensor_scalar(deg[:, 1, :], psD[:, 0:NT], 1.0, None, ALU.add).then_inc(p_sqrt, 1)
                    V.tensor_copy(tmp[:], psD[:, 0:NT]).then_inc(ev["node_counts"], 1)
                    dve.wait_ge(ev["tile_counts"], 1)
                    V.tensor_copy(cntc[:], psX[0:NT, 0:1]).then_inc(ev["tile_counts_in"], 1)
                    dve.wait_ge(ev["starts"], 1)
                    step(V.tensor_copy(startc[:], psY[0:NT, 0:1]))
                    step(V.tensor_copy(start_i[:, 0:1], startc[:]))
                    V.tensor_scalar(blk[:], start_i[:, 0:1], 7, None, ALU.arith_shift_right).then_inc(ev["blocks_in"], 1)
                    for i in range(7):
                        step(V.tensor_scalar(bits_i[:, i:i + 1], start_i[:, 0:1], i, 1, ALU.logical_shift_right,
                                        ALU.bitwise_and))
                    step(V.tensor_copy(bits[:], bits_i[:]))
                    dve.wait_ge(p_sqrt, 2)
                    step(V.reciprocal(dis1[:], deg[:, 0, :]))
                    step(V.reciprocal(dis3[:], deg[:, 1, :]))
                    dve.wait_ge(ld[2], 16)
                    step(V.tensor_tensor(dcmp[:], steps[:, 0:NT], steps[:, 1:NT + 1], ALU.is_gt))
                    step(V.tensor_reduce(flags[:, 0:1], dcmp[:], AX.X, ALU.max))
                    dve.wait_ge(p_run, 16)
                    step(V.tensor_copy(run[:, 0, :, :], run_i[:].rearrange("t (a j) -> t a j", a=2)))
                    width, at = RUN, 0
                    for i in (6, 5, 4, 3, 2, 1, 0):
                        by = 1 << i
                        width -= by
                        now, then = run[:, at, :, 0:width], run[:, at, :, by:by + width]
                        step(V.tensor_tensor(diff[:, :, 0:width], then, now, ALU.subtract))
                        step(V.scalar_tensor_tensor(out=run[:, 1 - at, :, 0:width], in0=diff[:, :, 0:width],
                                                    scalar=bits[:, i:i + 1], in1=now, op0=ALU.mult, op1=ALU.add))
                        at = 1 - at
                    src_run, dst_run = run[:, at, 0, :], run[:, at, 1, :]
                    step(V.tensor_scalar(a0[:], dst_run[:, 0:WINDOW + 1], node[:, 0:1], None, ALU.subtract))
                    step(V.tensor_scalar(flags[0:NT, 1:2], a0[:, WINDOW:WINDOW + 1], float(P), None, ALU.is_lt))
                    step(V.tensor_scalar(vld[:], a0[:, 0:WINDOW], float(P), None, ALU.is_lt))
                    dve.nop().then_inc(ev["flags_in"], 1)
                    dve.wait_ge(ev["flags_summed"], 1)
                    step(V.tensor_reduce(mode[:], psX[:, 8:10], AX.X, ALU.max))
                    step(V.tensor_scalar(mode[:], mode[:], 1.0, None, ALU.min))
                    step(V.tensor_copy(mode_i[:], mode[:]))
                    m = mode[0:NT]
                    step(V.tensor_scalar(tmp[0:NT, 0:1], m, -1.0, 1.0, ALU.mult, ALU.add))
                    step(V.tensor_scalar(vld[:], vld[:], tmp[0:NT, 0:1], None, ALU.mult))
                    step(V.tensor_scalar(nvl[:], vld[:], -1.0, 1.0, ALU.mult, ALU.add))
                    step(V.tensor_scalar(alt[:, 0, :], node[:], -float(SKIP), None, ALU.add))
                    step(V.tensor_scalar(alt[:, 1, :], iota[0:NT, :], 1.0, None, ALU.add))
                    step(V.tensor_scalar(alt[:, 0, :], alt[:, 0, :], m, float(SKIP), ALU.mult, ALU.add))
                    step(V.tensor_scalar(alt[:, 1, :], alt[:, 1, :], m, -1.0, ALU.mult, ALU.add))
                    nva, va = nvl[:, 0:P], vld[:, 0:P]
                    for i in range(2):
                        step(V.tensor_tensor(alt[:, i, :], alt[:, i, :], nva, ALU.mult))
                    step(V.tensor_tensor(fld[:, 0, :], src_run[:, 0:P], va, ALU.mult))
                    step(V.tensor_scalar(fld[:, 1, :], iota[0:NT, :], startc[:], None, ALU.add))
                    step(V.tensor_tensor(fld[:, 2, :], a0[:, 0:P], va, ALU.mult))
                    step(V.tensor_tensor(fld[:, 1, :], fld[:, 1, :], va, ALU.mult))
                    step(V.scalar_tensor_tensor(out=fld[:, 0, :], in0=nva, scalar=float(SKIP), in1=fld[:, 0, :],
                                                op0=ALU.mult, op1=ALU.add))
                    step(V.tensor_tensor(fld[:, 1, :], fld[:, 1, :], alt[:, 0, :], ALU.add))
                    step(V.tensor_tensor(fld[:, 2, :], fld[:, 2, :], alt[:, 1, :], ALU.add))
                    step(V.tensor_scalar(tmp[0:NT, 0:HALF], iota[0:NT, 0:HALF], startc[:], float(P), ALU.add, ALU.add))
                    vb, nvb = vld[:, P:WINDOW], nvl[:, P:WINDOW]
                    for h in (0, HALF):
                        to = slice(h, h + HALF)
                        step(V.tensor_tensor(fld[:, 3, to], src_run[:, P:WINDOW], vb, ALU.mult))
                        step(V.tensor_tensor(fld[:, 4, to], tmp[0:NT, 0:HALF], vb, ALU.mult))
                        step(V.tensor_tensor(fld[:, 5, to], a0[:, P:WINDOW], vb, ALU.mult))
                        step(V.tensor_tensor(fld[:, 5, to], fld[:, 5, to], nvb, ALU.subtract))
                        for f in (3, 4):
                            step(V.scalar_tensor_tensor(out=fld[:, f, to], in0=nvb, scalar=float(SKIP),
                                                        in1=fld[:, f, to], op0=ALU.mult, op1=ALU.add))
                    dve.nop().then_inc(ev["fields_in"], 1)
                    dve.wait_ge(ev["fields_turned"], 1)
                    two = "p (k u) -> p k u"
                    A = psY[:, 0:3 * NT].rearrange("p (f k u) -> p f k u", f=3, u=2)
                    for f, to in ((0, SRC_A), (1, EID_A)):
                        step(V.tensor_copy(IDX[:, :, to:to + 2], A[:, f, :, :]))
                    step(V.tensor_copy(dlA[:].rearrange(two, u=2), A[:, 2, :, :]))
                    B = psZ[:, 0:3 * NT].rearrange("p (f k u) -> p f k u", f=3, u=2)
                    for h in (0, 1):
                        to = slice(h * HALF, (h + 1) * HALF)
                        step(V.tensor_copy(IDX[to, :, SRC_B], B[to, 0, :, h]))
                        step(V.tensor_copy(IDX[to, :, EID_B], B[to, 1, :, h]))
                        step(V.tensor_copy(dlB[to, :], B[to, 2, :, h]))
                    L = psL[0:NT, :].rearrange("t (f j) -> t f j", f=4)
                    step(V.tensor_copy(sg[:], L))
                    step(V.tensor_scalar(hold[:, 0, :], sg[:, 0, :], 0.0, None, ALU.is_equal))
                    step(V.tensor_scalar(hold[:, 1, :], sg[:, 0, :], float(P), None, ALU.mult))
                    step(V.tensor_tensor(hold[:, 1, :], hold[:, 1, :], sg[:, 1, :], ALU.add))
                    step(V.tensor_scalar(hold[:, 3, :], hold[:, 0, :], -float(P), float(P), ALU.mult, ALU.add))
                    step(V.tensor_scalar(hold[:, 2, :], sg[:, 2, :], float(P), None, ALU.mult))
                    step(V.tensor_tensor(hold[:, 1, :], hold[:, 1, :], hold[:, 3, :], ALU.subtract))
                    step(V.tensor_tensor(hold[:, 2, :], hold[:, 2, :], sg[:, 3, :], ALU.add))
                    step(V.tensor_tensor_scan(hold[:, 3, :], hold[:, 0, :], hold[:, 1, :], 0.0, ALU.mult, ALU.add))
                    step(V.tensor_tensor_scan(hold[:, 4, :], hold[:, 0, :], hold[:, 2, :], 0.0, ALU.mult, ALU.add))
                    step(V.tensor_reduce(last[:, 0:1], hold[:, 0, :], AX.X, ALU.min))
                    step(V.tensor_copy(last[:, 1:2], hold[:, 3, P - 1:P]))
                    V.tensor_copy(last[:, 2:3], hold[:, 4, P - 1:P]).then_inc(ev["lasts_in"], 1)
                    dve.wait_ge(ev["lasts_turned"], 1)
                    step(V.tensor_copy(lrow[:, 0:3, :], psX[0:1, 0:3 * NT].rearrange("o (f t) -> o f t", f=3)))
                    step(V.tensor_tensor_scan(lrow[:, 3, :], lrow[:, 0, :], lrow[:, 1, :], 0.0, ALU.mult, ALU.add))
                    step(V.tensor_tensor_scan(lrow[:, 4, :], lrow[:, 0, :], lrow[:, 2, :], 0.0, ALU.mult, ALU.add))
                    step(V.tensor_copy(lrow[:, 5, 1:NT], lrow[:, 3, 0:NT - 1]))
                    V.tensor_copy(lrow[:, 6, 1:NT], lrow[:, 4, 0:NT - 1]).then_inc(ev["carries_in"], 1)
                    dve.wait_ge(ev["carries_turned"], 1)
                    step(V.tensor_copy(carry[:, 0:2], psY[0:NT, 0:2]))
                    step(V.tensor_tensor_scan(sg[:, 0, :], hold[:, 0, :], hold[:, 1, :], carry[:, 0:1], ALU.mult,
                                              ALU.add))
                    step(V.tensor_tensor_scan(sg[:, 1, :], hold[:, 0, :], hold[:, 2, :], carry[:, 1:2], ALU.mult,
                                              ALU.add))
                    step(V.tensor_scalar(sg[:, 2, :], sg[:, 0, :], 0.0, float(N), ALU.is_equal, ALU.mult))
                    step(V.tensor_tensor(sg[:, 2, :], sg[:, 2, :], sg[:, 0, :], ALU.add))
                    dve.nop().then_inc(ev["rids_in"], 1)
                    V.tensor_copy(last[:, 3:4], sg[:, 2, P - 1:P]).then_inc(ev["last_rids_in"], 1)
                    dve.wait_ge(ev["last_rids_turned"], 1)
                    step(V.memset(lrow[:, 0, 0:1], float(N)))
                    step(V.tensor_copy(lrow[:, 0, 1:NT], psX[0:1, 0:NT - 1]))
                    step(V.memset(lrow[:, 1, 0:1], 0.0))
                    step(V.tensor_tensor(lrow[:, 1, 1:NT], lrow[:, 0, 1:NT], lrow[:, 0, 0:NT - 1], ALU.is_equal))
                    step(V.tensor_scalar(lrow[:, 2, 1:NT], lrow[:, 0, 1:NT], float(N), None, ALU.is_equal))
                    step(V.memset(lrow[:, 2, 0:1], 0.0))
                    step(V.tensor_tensor(lrow[:, 1, :], lrow[:, 1, :], lrow[:, 2, :], ALU.add))
                    step(V.scalar_tensor_tensor(out=lrow[:, 1, :], in0=lrow[:, 1, :], scalar=-float(FAR),
                                                in1=lrow[:, 0, :], op0=ALU.mult, op1=ALU.add))
                    dve.nop().then_inc(ev["key_rows_in"], 1)
                    dve.wait_ge(ev["keys_turned"], 1)
                    step(V.tensor_copy(carry[:, 2:3], psY[0:NT, 4:5]))
                    step(V.tensor_copy(keycol[:], psY[0:NT, 5:6]))
                    step(V.tensor_copy(keys[:], psZ[:, 0:NT]))
                    step(V.tensor_scalar(hold[:, 3, :], sg[:, 2, :], carry[:, 2:3], 0.0, ALU.is_equal, ALU.is_equal))
                    step(V.tensor_scalar(hold[:, 4, :], sg[:, 2, :], last[:, 3:4], 0.0, ALU.is_equal, ALU.is_equal))
                    step(V.tensor_scalar(hold[:, 5, :], node[:], float(N), None, ALU.is_lt))
                    step(V.tensor_tensor(sg[:, 0, :], sg[:, 0, :], hold[:, 5, :], ALU.mult))
                    step(V.tensor_tensor(sg[:, 3, :], sg[:, 0, :], hold[:, 3, :], ALU.mult))
                    step(V.tensor_tensor(sg[:, 3, :], sg[:, 3, :], hold[:, 4, :], ALU.mult))
                    dve.nop().then_inc(ev["columns_in"], 1)
                    dve.wait_ge(ev["columns_turned"], 1)
                    step(V.tensor_copy(skey[:], psX[:, 0:NT]))
                    step(V.tensor_copy(skey_in[:], psX[:, NT:2 * NT]))
                    step(V.reciprocal(rcnt[:], psX[:, 2 * NT:3 * NT]))

                @block.tensor
                def _(pe):
                    mm = nc.tensor.matmul
                    pe.wait_ge(p_dve, 1)
                    for o, m_, w in ((psD, P, NT), (psS, P, NT), (psL, NT, 4 * P)):
                        last_one = mm(o[0:m_, 0:w], zeros_h[:, 0:m_], zeros_h[:, 0:w], start=True, stop=False)
                    last_one.then_inc(p_hot_used, 2)
                    with pe.Fori(0, PAIRS) as k:
                        for u in (0, 1):
                            pe.wait_ge(p_hot, k * 2 + u + 1)
                            mm(psS[:, 0:NT], hot[:, u, 0, :], hot[:, u, 1, 0:NT], start=False, stop=False)
                            mm(psD[:, 0:NT], hot[:, u, 2, :], hot[:, u, 3, 0:NT], start=False, stop=False)
                            mm(psL[0:NT, :], hot[:, u, 4, 0:NT], hot_leaf[:, u, :, :].rearrange("p f j -> p (f j)"),
                               start=False, stop=False).then_inc(p_hot_used, 1)
                    for o, m_, w in ((psD, P, NT), (psS, P, NT), (psL, NT, 4 * P)):
                        last_one = mm(o[0:m_, 0:w], zeros_h[:, 0:m_], zeros_h[:, 0:w], start=False, stop=True)
                    last_one.then_inc(ev["degrees_summed"], 1)
                    pe.wait_ge(ev["node_counts"], 1)
                    mm(psX[0:NT, 0:1], tmp[:], ones[:, 0:1], start=True, stop=True).then_inc(ev["tile_counts"], 1)
                    pe.wait_ge(ev["tile_counts_in"], 1)
                    mm(psY[0:NT, 0:1], tri[:], cntc[:], start=True, stop=True).then_inc(ev["starts"], 1)
                    pe.wait_ge(ev["flags_in"], 1)
                    mm(psX[:, 8:10], ones[:], flags[:], start=True, stop=True).then_inc(ev["flags_summed"], 1)
                    pe.wait_ge(ev["fields_in"], 1)
                    for f in range(3):
                        nc.tensor.transpose(psY[:, f * NT:(f + 1) * NT], fld[:, f, :], ident[0:NT, 0:NT])
                    for f in range(3):
                        last_one = nc.tensor.transpose(psZ[:, f * NT:(f + 1) * NT], fld[:, 3 + f, :],
                                                       ident[0:NT, 0:NT])
                    last_one.then_inc(ev["fields_turned"], 1)
                    pe.wait_ge(ev["lasts_in"], 1)
                    for f in range(3):
                        last_one = mm(psX[0:1, f * NT:(f + 1) * NT], last[:, f:f + 1], ident[0:NT, 0:NT],
                                      start=True, stop=True)
                    last_one.then_inc(ev["lasts_turned"], 1)
                    pe.wait_ge(ev["carries_in"], 1)
                    for f in range(2):
                        last_one = mm(psY[0:NT, f:f + 1], lrow[:, 5 + f, :], ones[0:1, 0:1], start=True, stop=True)
                    last_one.then_inc(ev["carries_turned"], 1)
                    pe.wait_ge(ev["last_rids_in"], 1)
                    mm(psX[0:1, 0:NT], last[:, 3:4], ident[0:NT, 0:NT],
                       start=True, stop=True).then_inc(ev["last_rids_turned"], 1)
                    pe.wait_ge(ev["key_rows_in"], 1)
                    mm(psY[0:NT, 4:5], lrow[:, 0, :], ones[0:1, 0:1], start=True, stop=True)
                    mm(psY[0:NT, 5:6], lrow[:, 1, :], ones[0:1, 0:1], start=True, stop=True)
                    mm(psZ[:, 0:NT], ones[0:1, :], lrow[:, 1, :], start=True, stop=True).then_inc(ev["keys_turned"], 1)
                    pe.wait_ge(ev["columns_in"], 1)
                    for f, of in enumerate((0, 3, 1)):
                        last_one = nc.tensor.transpose(psX[:, f * NT:(f + 1) * NT], sg[:, of, :], ident[0:NT, 0:NT])
                    last_one.then_inc(ev["columns_turned"], 1)
            end_phase()

        def wait(eng, semaphore, value):
            if not (isinstance(value, int) and value <= 0):
                eng.wait_ge(semaphore, value)

        def pipe(eng, stages, count, unroll):
            first = 2 * unroll
            for t in range(first):
                for f, lag, *more in stages:
                    if t - lag >= 0:
                        f(t - lag, (t - lag) % unroll, (t - lag) // unroll, *more)
            with eng.Fori(2, count // unroll) as r:
                for u in range(unroll):
                    for f, lag, *more in stages:
                        f(r * unroll + (u - lag), (u - lag) % unroll, r + (u - lag) // unroll, *more)
            for t in range(count, count + max(stage[1] for stage in stages)):
                for f, lag, *more in stages:
                    if t - lag < count:
                        f(t - lag, (t - lag) % unroll, (t - lag) // unroll, *more)

        class TablePass:

            def __init__(self, scope, name, table, sums, width, buffers, squares, psum, edge_rows=None):
                self.msg, self.cur, self.edge, self.zero = (buffers[:, i, :] for i in range(4))
                self.eq, self.eq_below, self.below = (squares[:, i, :] for i in range(3))
                self.psum = psum
                self.table, self.sums, self.edge_rows = table, sums, edge_rows
                self.src_i = sb(scope, f"{name}_src_i", [P, NT], I32)
                self.dst_i = sb(scope, f"{name}_dst_i", [P, NT], I32)
                self.dst = sb(scope, f"{name}_dst", [P, NT])
                self.row_i = sb(scope, f"{name}_row_i", [P, P], I32)
                self.dup = sb(scope, f"{name}_dup", [P, 1])
                self.to = sb(scope, f"{name}_to", [P, 1], I32)
                self.of = sb(scope, f"{name}_of", [P, 1], I32)
                self.width = width
                self.cols_ld = [sem(f"{name}_cols{i}") for i in range(2)]
                self.zero_in = sem(f"{name}_zero_in")
                self.zeroed = sem(f"{name}_zeroed")
                self.step_in = sem(f"{name}_step")
                self.tile = sem(f"{name}_tile")
                self.row_ld = sem(f"{name}_row_ld")
                self.edge_ld = sem(f"{name}_edge_ld")
                self.of_in = sem(f"{name}_of_in")
                self.msg_ld = sem(f"{name}_msg_ld")
                self.msg_in = sem(f"{name}_msg_in")
                self.to_in = sem(f"{name}_to_in")
                self.sum_done = sem(f"{name}_sum_done")
                self.cur_ld = sem(f"{name}_cur_ld")
                self.cur_in = sem(f"{name}_cur_in")
                self.cur_st = sem(f"{name}_cur_st")
                self.seen = sem(f"{name}_seen")
                self.seen_sp = sem(f"{name}_seen_sp")

            def on_sync(self, sp):
                mode = sp.value_load(mode_i[0:1, 0:1], min_val=0, max_val=1)
                with sp.If(mode > 0):
                    sp.dma_start(self.src_i[:], src_cols).then_inc(self.cols_ld[0], 16)
                    sp.dma_start(self.dst_i[:], dst_cols).then_inc(self.cols_ld[1], 16)
                    sp.wait_ge(self.zero_in, 1)
                    with sp.Fori(0, NT) as t:
                        sp.dma_start(self.sums[rows(t), :], self.zero).then_inc(self.zeroed, 16)
                        sp.wait_ge(self.zeroed, 16 * (t + 1))
                        sp.nop().then_inc(self.seen_sp, 1)
                    with sp.Fori(0, NT) as t:
                        sp.wait_ge(self.tile, t + 1)
                        sp.nop().then_inc(self.seen_sp, 1)
                        sp.dma_start(self.row_i[:], dst_rows[bass.ds(t, 1), :].to_broadcast([P, P])
                                     ).then_inc(self.row_ld, 16)
                        if self.edge_rows is not None:
                            sp.dma_start(self.edge, self.edge_rows[rows(t), :]).then_inc(self.edge_ld, 16)

            def on_gpsimd(self, pool):
                mode = pool.value_load(mode_i[0:1, 0:1], min_val=0, max_val=1)
                with pool.If(mode > 0):
                    pool.wait_ge(self.cols_ld[0], 16)
                    pool.wait_ge(self.zero_in, 1)
                    pool.wait_ge(self.zeroed, 16 * NT)
                    pool.nop().then_inc(self.tile, 1)
                    with pool.Fori(0, NT) as t:
                        nc.gpsimd.tensor_copy(self.of[:], self.src_i[:, bass.ds(t, 1)]).then_inc(self.of_in, 1)
                        pool.wait_ge(self.of_in, t + 1)
                        pool.nop().then_inc(self.seen, 1)
                        pool.indirect_dma_start(out=self.msg, out_offset=None, in_=self.table,
                                                in_offset=bass.IndirectOffsetOnAxis(ap=self.of[:], axis=0),
                                                bounds_check=N - 1, oob_is_err=False).then_inc(self.msg_ld, 16)
                        pool.wait_ge(self.to_in, t + 1)
                        pool.nop().then_inc(self.seen, 1)
                        pool.indirect_dma_start(out=self.cur, out_offset=None, in_=self.sums,
                                                in_offset=bass.IndirectOffsetOnAxis(ap=self.to[:], axis=0),
                                                bounds_check=N - 1, oob_is_err=False).then_inc(self.cur_ld, 16)
                        pool.wait_ge(self.cur_in, t + 1)
                        pool.nop().then_inc(self.seen, 1)
                        pool.indirect_dma_start(out=self.sums, in_=self.cur, in_offset=None,
                                                out_offset=bass.IndirectOffsetOnAxis(ap=self.to[:], axis=0),
                                                bounds_check=N - 1, oob_is_err=False).then_inc(self.cur_st, 16)
                        pool.wait_ge(self.cur_st, 16 * (t + 1))
                        pool.wait_ge(self.msg_ld, 16 * (t + 1))
                        pool.nop().then_inc(self.tile, 1)

            def on_vector(self, dve):
                V = nc.vector
                mode = dve.value_load(mode_i[0:1, 0:1], min_val=0, max_val=1)
                with dve.If(mode > 0):
                    V.memset(self.msg, 0.0)
                    V.memset(self.cur, 0.0)
                    V.tensor_scalar(self.below, iota[:], pcol[:], None, ALU.is_lt)
                    V.memset(self.zero, 0.0).then_inc(self.zero_in, 1)
                    dve.wait_ge(self.cols_ld[1], 16)
                    V.tensor_copy(self.dst[:], self.dst_i[:]).then_inc(self.step_in, 1)
                    dve.wait_ge(self.step_in, 1)
                    steps_ = 3 if self.edge_rows is None else 4
                    with dve.Fori(0, NT) as t:
                        n = [0]

                        def step(ins):
                            n[0] += 1
                            ins.then_inc(self.step_in, 1)
                            dve.wait_ge(self.step_in, t * steps_ + (n[0] + 1))
                        dve.wait_ge(self.row_ld, 16 * (t + 1))
                        step(V.tensor_scalar(self.eq, self.row_i[:], self.dst[:, bass.ds(t, 1)], None, ALU.is_equal))
                        step(V.tensor_tensor(self.eq_below, self.eq, self.below, ALU.mult))
                        step(V.tensor_reduce(self.dup[:], self.eq_below, AX.X, ALU.max))
                        V.tensor_scalar(self.to[:], self.dup[:], float(SKIP), self.dst[:, bass.ds(t, 1)],
                                        ALU.mult, ALU.add).then_inc(self.to_in, 1)
                        dve.wait_ge(self.msg_ld, 16 * (t + 1))
                        if self.edge_rows is not None:
                            dve.wait_ge(self.edge_ld, 16 * (t + 1))
                            step(V.tensor_tensor(self.msg, self.msg, self.edge, ALU.add))
                            V.tensor_scalar(self.msg, self.msg, 0.0, None, ALU.max).then_inc(self.msg_in, 1)
                        else:
                            dve.nop().then_inc(self.msg_in, 1)
                        dve.wait_ge(self.cur_ld, 16 * (t + 1))
                        dve.wait_ge(self.sum_done, t + 1)
                        V.tensor_tensor(self.cur, self.cur, self.psum[:, 0:self.width],
                                        ALU.add).then_inc(self.cur_in, 1)

            def on_tensor(self, pe):
                mode = pe.value_load(mode_i[0:1, 0:1], min_val=0, max_val=1)
                with pe.If(mode > 0):
                    with pe.Fori(0, NT) as t:
                        pe.wait_ge(self.msg_in, t + 1)
                        nc.tensor.matmul(self.psum[:, 0:self.width], self.eq, self.msg,
                                         start=True, stop=True).then_inc(self.sum_done, 1)

        aB = sb(ctx, "aB", [P, D])
        cB = sb(ctx, "cB", [P, D])

        NQ, Q = NT // 4, 4
        with ExitStack() as s:
            w1p = sb(s, "w1p", [P, 2, DC, D], F32R)
            w2p = sb(s, "w2p", [P, 2, DC, D], F32R)
            b1s = sb(s, "b1s", [P, DC])
            bn_in = sb(s, "bn_in", [P, 3, DC])
            slotidx = sb(s, "slotidx", [P, 2, FIELDS], I32)
            gA = sb(s, "gA", [P, 2 * Q, D])
            mA = sb(s, "mA", [P, 2 * Q, D])
            gB = sb(s, "gB", [P, Q, D])
            mB = sb(s, "mB", [P, Q, D])
            pA = sb(s, "pA", [P, Q, 2, D], F32R)
            pB = sb(s, "pB", [P, 2, 2, D], F32R)
            xs = sb(s, "xs", [P, 2 * Q, D])
            ohA = sb(s, "ohA", [P, Q, P], F32R)
            ohB = sb(s, "ohB", [P, 2, P], F32R)
            hs = sb(s, "hs", [P, Q, D])
            hT = sb(s, "hT", [P, 2, DC, Q * P], F32R)
            gf = sb(s, "gf", [P, 2, Q * P])
            gT = sb(s, "gT", [P, 2, DC, Q * P], F32R)
            ds = sb(s, "ds", [P, Q, D])
            sq = sb(s, "sq", [P, Q, D])
            S1 = sb(s, "S1", [P, D])
            S2 = sb(s, "S2", [P, D])
            col = sb(s, "col", [P, 6, DC])
            half = sb(s, "half", [P, 1])
            psA = [ps(s, f"psA{i}") for i in range(2)]
            psT = [ps(s, f"psT{i}") for i in range(2)]
            psG = [ps(s, f"psG{i}") for i in range(2)]
            psU = [ps(s, f"psU{i}") for i in range(2)]

            tp = TablePass(s, "t0", x, table0, D, gA, sq[:, :, 0:P], psA[0], ea)
            w_ld = [sem(f"l0_weights{i}") for i in range(3)]
            w_hi = sem("l0_weights_high")
            w_lo = sem("l0_weights_low")
            clear = sem("l0_clear")
            idx_seen = sem("l0_idx_seen")
            idx_in = sem("l0_idx_in")
            gA_ld = [sem(f"l0_gA{i}") for i in range(2 * Q)]
            mA_ld = [sem(f"l0_mA{i}") for i in range(2 * Q)]
            gB_ld = [sem(f"l0_gB{i}") for i in range(Q)]
            mB_ld = [sem(f"l0_mB{i}") for i in range(Q)]
            xs_ld = [sem(f"l0_x{i}") for i in range(2 * Q)]
            d_st = [sem(f"l0_d{i}") for i in range(Q)]
            sumA = sem("l0_sumA")
            sumB = sem("l0_sumB")
            hiA = sem("l0_highA")
            hiB = sem("l0_highB")
            loA = sem("l0_lowA")
            loB = sem("l0_lowB")
            agg_done = sem("l0_agg_done")
            h_in = sem("l0_h_in")
            T_done = sem("l0_T_done")
            hT_hi = sem("l0_hT_high")
            hT_lo = sem("l0_hT_low")
            g1_done = sem("l0_g1_done")
            gf_in = sem("l0_gf_in")
            gT_hi = sem("l0_gT_high")
            gT_lo = sem("l0_gT_low")
            g2_done = sem("l0_g2_done")
            d_in = sem("l0_d_in")
            s1_in = sem("l0_s1_in")
            sq_in = sem("l0_sq_in")
            s2_in = sem("l0_s2_in")
            bn_sum = sem("bn_sum")
            bn_var = sem("bn_var")
            bn_pow = sem("bn_pow")
            bn_step = sem("bn_step")
            bn_diag = sem("bn_diag")
            bn_rows = sem("bn_rows")

            with nc.Block() as block:
                @block.sync
                def _(sp):
                    sp.dma_start(ds[:], w1.rearrange("(c p) n -> p c n", p=P)).then_inc(w_ld[0], 16)
                    sp.dma_start(b1s[:], b1).then_inc(w_ld[1], 16)
                    sp.dma_start(bn_in[:], bn_cols).then_inc(w_ld[2], 16)
                    tp.on_sync(sp)
                    sp.wait_ge(w_hi, 1)
                    sp.wait_ge(w_lo, 1)
                    sp.dma_start(ds[:], w2.rearrange("(c p) n -> p c n", p=P)).then_inc(w_ld[0], 16)

                    def load(q, v, r):
                        for u in range(Q):
                            wait(sp, d_in, Q * q + u - 2 * Q + 1)
                            sp.dma_start(xs[:, Q * v + u, :], x[rows(q * Q + u), :]).then_inc(xs_ld[Q * v + u], 16)

                    def store(q, v, r, u):
                        wait(sp, d_in, Q * q + u + 1)
                        sp.dma_start(d_dram[rows(q * Q + u), :], ds[:, u, :]).then_inc(d_st[u], 16)
                    pipe(sp, [(store, 2, 0), (store, 2, 1), (store, 2, 2), (store, 2, 3), (load, 0)], NQ, 2)
                    for u in range(Q):
                        sp.wait_ge(d_st[u], 16 * NQ)

                @block.gpsimd
                def _(pool):
                    tp.on_gpsimd(pool)
                    pool.memset(gA[:], 0.0).then_inc(clear, 1)
                    pool.memset(gB[:], 0.0).then_inc(clear, 1)
                    pool.memset(half[:], -0.5).then_inc(clear, 1)
                    pool.memset(S2[:], 0.0).then_inc(clear, 1)
                    pool.wait_ge(clear, 6)
                    table_mode = pool.value_load(mode_i[0:1, 0:1], min_val=0, max_val=1)

                    def fetch(into, table, field, v, signal, bound):
                        pool.indirect_dma_start(
                            out=into, out_offset=None, in_=table,
                            in_offset=bass.IndirectOffsetOnAxis(ap=slotidx[:, v, field:field + 1], axis=0),
                            bounds_check=bound, oob_is_err=False).then_inc(signal, 16)

                    def gather(q, v, r, h):
                        k = q * 2 + h
                        a, b_ = Q * v + 2 * h, 2 * v + h
                        before, round_ = (0, r) if v else (1, r - 1)
                        for w in (gA_ld, mA_ld):
                            for u in (0, 1):
                                wait(pool, w[Q * before + 2 * h + u], 16 * (round_ + 1))
                        wait(pool, gB_ld[2 * before + h], 16 * (round_ + 1))
                        wait(pool, mB_ld[2 * before + h], 16 * (round_ + 1))
                        nc.gpsimd.tensor_copy(slotidx[:, h, :], IDX[:, bass.ds(k, 1), :].rearrange("p a f -> p (a f)")
                                              ).then_inc(idx_in, 1)
                        wait(pool, loA, Q * q + 2 * h + 2 - 2 * Q)
                        wait(pool, loB, k + 1 - Q)
                        wait(pool, idx_in, k + 1)
                        pool.nop().then_inc(idx_seen, 1)
                        for u in (0, 1):
                            fetch(gA[:, a + u, :], x, SRC_A + u, h, gA_ld[a + u], N - 1)
                        with pool.If(table_mode > 0):
                            for u in (0, 1):
                                fetch(mA[:, a + u, :], table0, EID_A + u, h, mA_ld[a + u], NP - 1)
                        with pool.Else():
                            for u in (0, 1):
                                fetch(mA[:, a + u, :], ea, EID_A + u, h, mA_ld[a + u], N - 1)
                        fetch(gB[:, b_, :], x, SRC_B, h, gB_ld[b_], N - 1)
                        fetch(mB[:, b_, :], ea, EID_B, h, mB_ld[b_], N - 1)

                    def squares(q, v, r, u):
                        wait(pool, sq_in, Q * q + u + 1)
                        wait(pool, s2_in, Q * q + u)
                        nc.gpsimd.tensor_tensor(S2[:], S2[:], sq[:, u, :], ALU.add).then_inc(s2_in, 1)
                    pipe(pool, [(squares, 3, 0), (gather, 0, 0), (squares, 3, 1), (squares, 3, 2), (gather, 0, 1),
                                (squares, 3, 3)], NQ, 2)
                    pool.wait_ge(bn_var, 1)
                    nc.gpsimd.tensor_tensor(col[:, 3, :], col[:, 1, :], half[:].to_broadcast([P, DC]),
                                            ALU.pow).then_inc(bn_pow, 1)

                @block.vector
                def _(dve):
                    V = nc.vector
                    tp.on_vector(dve)
                    V.memset(mA[:], 0.0).then_inc(clear, 1)
                    V.memset(mB[:], 0.0).then_inc(clear, 1)
                    V.memset(S1[:], 0.0).then_inc(s1_in, 1)
                    for i, w in enumerate((w1p, w2p)):
                        dve.wait_ge(w_hi, i + 1)
                        V.tensor_tensor(w[:, 1, :, :], ds[:], w[:, 0, :, :], ALU.subtract).then_inc(w_lo, 1)
                    dve.wait_ge(clear, 6)

                    def addA(q, v, r, u):
                        t = Q * q + u
                        dve.wait_ge(gA_ld[Q * v + u], 16 * (r + 1))
                        dve.wait_ge(mA_ld[Q * v + u], 16 * (r + 1))
                        V.tensor_tensor(mA[:, Q * v + u, :], mA[:, Q * v + u, :], gA[:, Q * v + u, :],
                                        ALU.add).then_inc(sumA, 1)
                        wait(dve, agg_done, t + 1 - Q)
                        V.tensor_scalar(ohA[:, u, :], iota[:], dlA[:, bass.ds(t, 1)], None, ALU.is_equal)

                    def addB(q, v, r, h):
                        b_ = 2 * v + h
                        dve.wait_ge(gB_ld[b_], 16 * (r + 1))
                        dve.wait_ge(mB_ld[b_], 16 * (r + 1))
                        V.tensor_tensor(mB[:, b_, :], mB[:, b_, :], gB[:, b_, :], ALU.add).then_inc(sumB, 1)
                        wait(dve, agg_done, Q * q + 2 * h + 2 - Q)
                        V.tensor_scalar(ohB[:, h, :], iota[:], dlB[:, bass.ds(q * 2 + h, 1)], None, ALU.is_equal)

                    def lowA(q, v, r, u):
                        dve.wait_ge(hiA, Q * q + u + 1)
                        V.scalar_tensor_tensor(out=pA[:, u, 1, :], in0=mA[:, Q * v + u, :], scalar=0.0,
                                               in1=pA[:, u, 0, :], op0=ALU.max, op1=ALU.subtract).then_inc(loA, 1)

                    def lowB(q, v, r, h):
                        dve.wait_ge(hiB, 2 * q + h + 1)
                        V.scalar_tensor_tensor(out=pB[:, h, 1, :], in0=mB[:, 2 * v + h, :], scalar=0.0,
                                               in1=pB[:, h, 0, :], op0=ALU.max, op1=ALU.subtract).then_inc(loB, 1)

                    def with_x(q, v, r, u):
                        t = Q * q + u
                        dve.wait_ge(xs_ld[Q * v + u], 16 * (r + 1))
                        dve.wait_ge(agg_done, t + 1)
                        wait(dve, T_done, t + 1 - Q)
                        V.tensor_tensor(hs[:, u, :], psA[u % 2][:, :], xs[:, Q * v + u, :], ALU.add).then_inc(h_in, 1)

                    def low_h(q, v, r, u):
                        dve.wait_ge(hT_hi, Q * q + u + 1)
                        o = slice(u * P, (u + 1) * P)
                        V.tensor_tensor(hT[:, 1, :, o], psT[u % 2][:, :].rearrange("p (c n) -> p c n", c=DC),
                                        hT[:, 0, :, o], ALU.subtract).then_inc(hT_lo, 1)

                    def low_g(q, v, r, c):
                        dve.wait_ge(gT_hi, DC * q + c + 1)
                        V.tensor_tensor(gT[:, 1, c, :], gf[:, c % 2, :], gT[:, 0, c, :], ALU.subtract
                                        ).then_inc(gT_lo, 1)

                    def residual(q, v, r, u):
                        t = Q * q + u
                        dve.wait_ge(g2_done, t + 1)
                        wait(dve, d_st[u], 16 * q)
                        wait(dve, sq_in, t + 1 - Q)
                        V.tensor_tensor(ds[:, u, :], psU[u % 2][:, :], xs[:, Q * v + u, :], ALU.add).then_inc(d_in, 1)

                    def total(q, v, r, u):
                        t = Q * q + u
                        dve.wait_ge(d_in, t + 1)
                        dve.wait_ge(s1_in, t + 1)
                        V.scalar_tensor_tensor(out=S1[:], in0=ds[:, u, :], scalar=real[:, bass.ds(t, 1)], in1=S1[:],
                                               op0=ALU.mult, op1=ALU.add).then_inc(s1_in, 1)
                    pipe(dve, [(with_x, 1, 0), (low_g, 2, 0), (addA, 0, 0), (with_x, 1, 1), (lowA, 0, 0),
                               (low_g, 2, 1), (addB, 0, 0), (with_x, 1, 2), (addA, 0, 1), (lowB, 0, 0),
                               (low_g, 2, 2), (lowA, 0, 1), (with_x, 1, 3), (low_g, 2, 3),
                               (low_h, 1, 0), (addA, 0, 2), (low_h, 1, 1), (residual, 2, 0), (lowA, 0, 2),
                               (total, 2, 0), (addB, 0, 1), (low_h, 1, 2), (residual, 2, 1), (lowB, 0, 1),
                               (total, 2, 1), (addA, 0, 3), (low_h, 1, 3), (residual, 2, 2), (lowA, 0, 3),
                               (total, 2, 2), (residual, 2, 3), (total, 2, 3)], NQ, 2)
                    n = [0]

                    def step(ins):
                        n[0] += 1
                        ins.then_inc(bn_step, 1)
                        dve.wait_ge(bn_step, n[0])
                    mean, var, tmp_, pow_, a_, c_ = (col[:, i, :] for i in range(6))
                    gamma, beta, b2 = (bn_in[:, i, :] for i in range(3))
                    dve.wait_ge(bn_sum, 1)
                    dve.wait_ge(w_ld[2], 16)
                    step(V.tensor_scalar(mean, psA[0][:, 0:DC], 1.0 / N, None, ALU.mult))
                    step(V.tensor_scalar(var, psA[0][:, DC:2 * DC], 1.0 / N, EPS, ALU.mult, ALU.add))
                    step(V.tensor_tensor(tmp_, mean, mean, ALU.mult))
                    V.tensor_tensor(var, var, tmp_, ALU.subtract).then_inc(bn_var, 1)
                    step(V.tensor_tensor(mean, mean, b2, ALU.add))
                    step(V.tensor_tensor(c_, b2, mean, ALU.subtract))
                    dve.wait_ge(bn_pow, 1)
                    step(V.tensor_tensor(a_, pow_, gamma, ALU.mult))
                    step(V.tensor_tensor(c_, c_, a_, ALU.mult))
                    step(V.tensor_tensor(c_, c_, beta, ALU.add))
                    for i in range(2):
                        for c in range(DC):
                            last_one = V.tensor_scalar(sq[:, i, c * P:(c + 1) * P], ident[:], col[:, 4 + i, c:c + 1],
                                                       None, ALU.mult)
                    last_one.then_inc(bn_diag, 1)
                    dve.wait_ge(bn_rows, 1)
                    V.tensor_copy(aB[:], psT[0][:, :])
                    V.tensor_copy(cB[:], psT[1][:, :])

                @block.scalar
                def _(act):
                    for i, w in enumerate((w1p, w2p)):
                        act.wait_ge(w_ld[0], 16 * (i + 1))
                        nc.scalar.activation(w[:, 0, :, :], ds[:], ACT.Copy).then_inc(w_hi, 1)

                    def highA(q, v, r, u):
                        t = Q * q + u
                        wait(act, agg_done, t + 1 - Q)
                        act.wait_ge(sumA, t + 1)
                        nc.scalar.activation(pA[:, u, 0, :], mA[:, Q * v + u, :], ACT.Relu).then_inc(hiA, 1)

                    def highB(q, v, r, h):
                        wait(act, agg_done, Q * q + 2 * h + 2 - Q)
                        act.wait_ge(sumB, 2 * q + h + 1)
                        nc.scalar.activation(pB[:, h, 0, :], mB[:, 2 * v + h, :], ACT.Relu).then_inc(hiB, 1)

                    def relus(q, v, r, c):
                        j = DC * q + c
                        act.wait_ge(g1_done, j + 1)
                        wait(act, gT_lo, j - 1)
                        nc.scalar.activation(gf[:, c % 2, :], psG[c % 2][:, :], ACT.Relu,
                                             bias=b1s[:, c:c + 1]).then_inc(gf_in, 1)
                        wait(act, g2_done, Q * q)
                        act.wait_ge(gf_in, j + 1)
                        nc.scalar.activation(gT[:, 0, c, :], gf[:, c % 2, :], ACT.Copy).then_inc(gT_hi, 1)

                    def high_h(q, v, r, u):
                        act.wait_ge(T_done, Q * q + u + 1)
                        wait(act, g1_done, DC * q)
                        nc.scalar.activation(hT[:, 0, :, u * P:(u + 1) * P],
                                             psT[u % 2][:, :].rearrange("p (c n) -> p c n", c=DC),
                                             ACT.Copy).then_inc(hT_hi, 1)

                    def squares(q, v, r, u):
                        t = Q * q + u
                        act.wait_ge(d_in, t + 1)
                        wait(act, s2_in, t + 1 - Q)
                        nc.scalar.activation(sq[:, u, :], ds[:, u, :], ACT.Square,
                                             scale=real[:, bass.ds(t, 1)]).then_inc(sq_in, 1)
                    act.wait_ge(w_ld[1], 16)
                    pipe(act, [(relus, 2, 0), (highA, 0, 0), (relus, 2, 1), (highB, 0, 0), (relus, 2, 2),
                               (highA, 0, 1), (relus, 2, 3), (high_h, 1, 0), (high_h, 1, 1), (highA, 0, 2),
                               (squares, 2, 0), (highB, 0, 1), (high_h, 1, 2), (squares, 2, 1), (high_h, 1, 3),
                               (highA, 0, 3), (squares, 2, 2), (squares, 2, 3)], NQ, 2)

                @block.tensor
                def _(pe):
                    mm = nc.tensor.matmul
                    tp.on_tensor(pe)

                    def sums(q, v, r, u):
                        t = Q * q + u
                        half_ = slice((u % 2) * HALF, (u % 2 + 1) * HALF)
                        pe.wait_ge(loA, t + 1)
                        pe.wait_ge(loB, 2 * q + u // 2 + 1)
                        wait(pe, h_in, t - 1)
                        o = psA[u % 2][:, :]
                        mm(o, ohA[:, u, :], pA[:, u, 0, :], start=True, stop=False)
                        mm(o, ohA[:, u, :], pA[:, u, 1, :], start=False, stop=False)
                        mm(o, ohB[half_, u // 2, :], pB[half_, u // 2, 0, :], start=False, stop=False)
                        mm(o, ohB[half_, u // 2, :], pB[half_, u // 2, 1, :], start=False, stop=True
                           ).then_inc(agg_done, 1)

                    def turn(q, v, r, u):
                        t = Q * q + u
                        pe.wait_ge(h_in, t + 1)
                        wait(pe, hT_lo, t - 1)
                        for c in range(DC):
                            f = slice(c * P, (c + 1) * P)
                            last_one = nc.tensor.transpose(psT[u % 2][:, f], hs[:, u, f], ident[:])
                        last_one.then_inc(T_done, 1)

                    def first(q, v, r, m):
                        pe.wait_ge(hT_lo, Q * q + Q)
                        wait(pe, gf_in, DC * q + m - 1)
                        for c in range(DC):
                            f = slice(m * P, (m + 1) * P)
                            for i, j in ((0, 0), (0, 1), (1, 0)):
                                last_one = mm(psG[m % 2][:, :], w1p[:, i, c, f], hT[:, j, c, :],
                                              start=c + i + j == 0, stop=c + i == DC)
                        last_one.then_inc(g1_done, 1)

                    def second(q, v, r, u):
                        pe.wait_ge(gT_lo, DC * q + DC)
                        wait(pe, d_in, Q * q + u - 1)
                        for c in range(DC):
                            f = slice(u * P, (u + 1) * P)
                            for i, j in ((0, 0), (0, 1), (1, 0)):
                                last_one = mm(psU[u % 2][:, :], gT[:, i, c, f], w2p[:, j, c, :],
                                              start=c + i + j == 0, stop=c + i == DC)
                        last_one.then_inc(g2_done, 1)
                    pe.wait_ge(w_lo, 2)
                    pipe(pe, [(first, 2, 0), (sums, 1, 0), (first, 2, 1), (sums, 1, 1), (first, 2, 2), (sums, 1, 2),
                              (first, 2, 3), (sums, 1, 3), (turn, 1, 0), (turn, 1, 1), (second, 2, 0), (turn, 1, 2),
                              (second, 2, 1), (turn, 1, 3), (second, 2, 2), (second, 2, 3)], NQ, 2)
                    pe.wait_ge(s1_in, NT + 1)
                    pe.wait_ge(s2_in, NT)
                    for i, of in enumerate((S1, S2)):
                        for c in range(DC):
                            last_one = mm(psA[0][:, DC * i + c:DC * i + c + 1], of[:, c * P:(c + 1) * P], ones[:, 0:1],
                                          start=True, stop=True)
                    last_one.then_inc(bn_sum, 1)
                    pe.wait_ge(bn_diag, 1)
                    for i in range(2):
                        last_one = mm(psT[i][:, :], ones[:], sq[:, i, :], start=True, stop=True)
                    last_one.then_inc(bn_rows, 1)
            end_phase()

        X = sb(ctx, "X", [P, NT, D])

        class Norm:

            def __init__(self, scope, name, slots, y=None):
                self.slots = slots
                self.y = sb(scope, f"{name}_y", [P, slots, D]) if y is None else y
                self.st = sb(scope, f"{name}_st", [P, slots, 6])
                self.mv = sb(scope, f"{name}_mv", [P, slots, 2])
                self.ve = sb(scope, f"{name}_ve", [P, slots])
                self.rs = sb(scope, f"{name}_rs", [P, slots])
                self.half = sb(scope, f"{name}_half", [P, 1])
                self.y_in = sem(f"{name}_y_in")
                self.st_in = sem(f"{name}_st_in")
                self.st_seen = sem(f"{name}_st_seen")
                self.mv_in = sem(f"{name}_mv_in")
                self.ve_in = sem(f"{name}_ve_in")
                self.rs_in = sem(f"{name}_rs_in")
                self.x_in = sem(f"{name}_x_in")
                self.half_in = sem(f"{name}_half_in")

            def statistics(self, dve, t, u, at=None):
                at = u if at is None else at
                V = nc.vector
                dve.wait_ge(self.y_in, t + 1)
                V.bn_stats(self.st[:, u, :], self.y[:, at, :]).then_inc(self.st_in, 1)
                dve.wait_ge(self.st_in, t + 1)
                dve.nop().then_inc(self.st_seen, 1)
                V.bn_aggr(self.mv[:, u, :], self.st[:, u, :]).then_inc(self.mv_in, 1)
                dve.wait_ge(self.mv_in, t + 1)
                wait(dve, self.rs_in, t + 1 - self.slots)
                V.tensor_scalar(self.ve[:, u:u + 1], self.mv[:, u, 1:2], EPS, None, ALU.add).then_inc(self.ve_in, 1)

            def begin(self, pool):
                pool.memset(self.half[:], -0.5).then_inc(self.half_in, 1)
                pool.wait_ge(self.half_in, 1)

            def power(self, pool, t, u):
                pool.wait_ge(self.ve_in, t + 1)
                wait(pool, self.x_in, t + 1 - self.slots)
                nc.gpsimd.tensor_tensor(self.rs[:, u:u + 1], self.ve[:, u:u + 1], self.half[:],
                                        ALU.pow).then_inc(self.rs_in, 1)

            def apply(self, dve, t, u, to, at=None):
                at = u if at is None else at
                dve.wait_ge(self.rs_in, t + 1)
                nc.vector.tensor_scalar(to, self.y[:, at, :], self.mv[:, u, 0:1], self.rs[:, u:u + 1],
                                        ALU.subtract, ALU.mult).then_inc(self.x_in, 1)

        def state(t):
            return X[:, bass.ds(t, 1), :].rearrange("p a d -> p (a d)")

        with ExitStack() as s:
            ws = sb(s, "wts", [P, DC, D])
            bB = sb(s, "bB", [P, D])
            dl = sb(s, "n1_d", [P, Q, D])
            xl = sb(s, "n1_x", [P, Q, D])
            xT = sb(s, "n1_xT", [P, 2, D])
            hs = sb(s, "n1_h", [P, 2, D])
            ln = Norm(s, "n1", 2, xl)
            psT = [ps(s, f"n1_psT{i}") for i in range(2)]
            psU = [ps(s, f"n1_psU{i}") for i in range(2)]
            w_ld = [sem(f"n1_w{i}") for i in range(2)]
            d_ld = [sem(f"n1_d_ld{i}") for i in range(Q)]
            x_ld = [sem(f"n1_x_ld{i}") for i in range(Q)]
            h_st = [sem(f"n1_h_st{i}") for i in range(2)]
            da_in = sem("n1_da_in")
            xc_in = sem("n1_xc_in")
            X_in = sem("n1_X_in")
            T_done = sem("n1_T_done")
            xT_in = sem("n1_xT_in")
            G_done = sem("n1_G_done")
            hb_in = sem("n1_hb_in")
            h_in = sem("n1_h_in")

            with nc.Block() as block:
                @block.sync
                def _(sp):
                    sp.dma_start(ws[:], wt.rearrange("(c p) n -> p c n", p=P)).then_inc(w_ld[0], 16)
                    sp.dma_start(bB[:], b.to_broadcast([P, D])).then_inc(w_ld[1], 16)

                    def load(t, u, r):
                        wait(sp, X_in, t + 1 - Q)
                        wait(sp, T_done, t + 1 - Q)
                        sp.dma_start(dl[:, u, :], d_dram[rows(t), :]).then_inc(d_ld[u], 16)
                        sp.dma_start(xl[:, u, :], x[rows(t), :]).then_inc(x_ld[u], 16)

                    def store(t, u, r):
                        wait(sp, h_in, t + 1)
                        sp.dma_start(table1[rows(t), :], hs[:, u % 2, :]).then_inc(h_st[u % 2], 16)
                    pipe(sp, [(load, 0), (store, 6)], NT, Q)
                    for i in range(2):
                        sp.wait_ge(h_st[i], 16 * NT // 2)

                @block.gpsimd
                def _(pool):
                    ln.begin(pool)

                    def addend(t, u, r):
                        pool.wait_ge(x_ld[u], 16 * (r + 1))
                        nc.gpsimd.tensor_tensor(xl[:, u, :], xl[:, u, :], cB[:], ALU.add).then_inc(xc_in, 1)

                    def power(t, u, r):
                        ln.power(pool, t, u % 2)
                    pipe(pool, [(addend, 0), (power, 1)], NT, Q)

                @block.vector
                def _(dve):
                    V = nc.vector

                    def sum_(t, u, r):
                        dve.wait_ge(d_ld[u], 16 * (r + 1))
                        V.tensor_tensor(dl[:, u, :], dl[:, u, :], aB[:], ALU.mult).then_inc(da_in, 1)
                        dve.wait_ge(da_in, t + 1)
                        dve.wait_ge(xc_in, t + 1)
                        V.tensor_tensor(xl[:, u, :], dl[:, u, :], xl[:, u, :], ALU.add).then_inc(ln.y_in, 1)
                        ln.statistics(dve, t, u % 2, u)

                    def norm(t, u, r):
                        ln.apply(dve, t, u % 2, xl[:, u, :], u)

                    def bias(t, u, r):
                        dve.wait_ge(G_done, t + 1)
                        wait(dve, h_st[u % 2], 16 * (r * 2 + u // 2))
                        V.tensor_tensor(hs[:, u % 2, :], psU[u % 2][:, :], bB[:], ALU.add).then_inc(hb_in, 1)
                    dve.wait_ge(w_ld[1], 16)
                    pipe(dve, [(sum_, 0), (norm, 1), (bias, 3)], NT, Q)

                @block.scalar
                def _(act):
                    def keep(t, u, r):
                        act.wait_ge(ln.x_in, t + 1)
                        nc.scalar.activation(state(t), xl[:, u, :], ACT.Copy).then_inc(X_in, 1)

                    def turned(t, u, r):
                        act.wait_ge(T_done, t + 1)
                        wait(act, G_done, t - 1)
                        nc.scalar.activation(xT[:, u % 2, :], psT[u % 2][:, :], ACT.Copy).then_inc(xT_in, 1)

                    def scale(t, u, r):
                        act.wait_ge(hb_in, t + 1)
                        nc.scalar.activation(hs[:, u % 2, :], hs[:, u % 2, :], ACT.Copy,
                                             scale=dis1[:, bass.ds(t, 1)]).then_inc(h_in, 1)
                    pipe(act, [(keep, 1), (turned, 1), (scale, 3)], NT, Q)

                @block.tensor
                def _(pe):
                    def turn(t, u, r):
                        pe.wait_ge(ln.x_in, t + 1)
                        wait(pe, xT_in, t - 1)
                        for c in range(DC):
                            f = slice(c * P, (c + 1) * P)
                            last_one = nc.tensor.transpose(psT[u % 2][:, f], xl[:, u, f], ident[:])
                        last_one.then_inc(T_done, 1)

                    def product(t, u, r):
                        pe.wait_ge(xT_in, t + 1)
                        wait(pe, hb_in, t - 1)
                        for c in range(DC):
                            last_one = nc.tensor.matmul(psU[u % 2][:, :], xT[:, u % 2, c * P:(c + 1) * P], ws[:, c, :],
                                                        start=c == 0, stop=c == DC - 1)
                        last_one.then_inc(G_done, 1)
                    pe.wait_ge(w_ld[0], 16)
                    pipe(pe, [(turn, 0), (product, 1)], NT, Q)
            end_phase()

        full = sb(ctx, "full", [NT, D])

        with ExitStack() as s:
            slotidx = sb(s, "n2_idx", [P, 2, FIELDS], I32)
            gA = sb(s, "n2_gA", [P, Q, D])
            gB = sb(s, "n2_gB", [P, 2, D])
            hs = sb(s, "n2_hs", [P, Q, D])
            o = sb(s, "n2_o", [P, 2, D])
            ohA = sb(s, "n2_ohA", [P, Q, P])
            ohB = sb(s, "n2_ohB", [P, 2, P])
            kh = sb(s, "n2_kh", [P, 2, NT])
            ln = Norm(s, "n2", 2)
            psA = [ps(s, f"n2_psA{i}") for i in range(2)]
            psF = ps(s, "n2_psF")
            tp = TablePass(s, "t1", table1, sums1, D, gA, ohA, psA[0])
            clear = sem("n2_clear")
            idx_seen = sem("n2_idx_seen")
            idx_in = sem("n2_idx_in")
            gA_ld = [sem(f"n2_gA{i}") for i in range(Q)]
            gB_ld = [sem(f"n2_gB{i}") for i in range(2)]
            hs_ld = [sem(f"n2_hs{i}") for i in range(Q)]
            oh_in = sem("n2_oh_in")
            agg_done = sem("n2_agg_done")
            o_in = sem("n2_o_in")
            r_in = sem("n2_r_in")
            kh_in = sem("n2_kh_in")
            F_done = sem("n2_F_done")
            full_in = sem("n2_full_in")

            with nc.Block() as block:
                @block.sync
                def _(sp):
                    tp.on_sync(sp)
                    def load(t, u, r):
                        wait(sp, o_in, t + 1 - Q)
                        sp.dma_start(hs[:, u, :], table1[rows(t), :]).then_inc(hs_ld[u], 16)
                    pipe(sp, [(load, 0)], NT, Q)

                @block.gpsimd
                def _(pool):
                    tp.on_gpsimd(pool)
                    ln.begin(pool)
                    pool.memset(gA[:], 0.0).then_inc(clear, 1)
                    pool.memset(gB[:], 0.0).then_inc(clear, 1)
                    pool.wait_ge(clear, 2)

                    table_mode = pool.value_load(mode_i[0:1, 0:1], min_val=0, max_val=1)

                    def fetch(into, table, field, v, signal):
                        pool.indirect_dma_start(
                            out=into, out_offset=None, in_=table,
                            in_offset=bass.IndirectOffsetOnAxis(ap=slotidx[:, v, field:field + 1], axis=0),
                            bounds_check=NP - 1, oob_is_err=False).then_inc(signal, 16)

                    def gather(t, u, r):
                        if u % 2:
                            return
                        h = u // 2
                        k = r * 2 + h
                        wait(pool, gA_ld[u], 16 * r)
                        wait(pool, gA_ld[u + 1], 16 * r)
                        wait(pool, gB_ld[h], 16 * r)
                        nc.gpsimd.tensor_copy(slotidx[:, h, :], IDX[:, bass.ds(k, 1), :].rearrange("p a f -> p (a f)")
                                              ).then_inc(idx_in, 1)
                        wait(pool, agg_done, t + 2 - Q)
                        wait(pool, idx_in, k + 1)
                        pool.nop().then_inc(idx_seen, 1)
                        with pool.If(table_mode > 0):
                            fetch(gA[:, u, :], sums1, EID_A, h, gA_ld[u])
                            fetch(gA[:, u + 1, :], sums1, EID_A + 1, h, gA_ld[u + 1])
                        with pool.Else():
                            fetch(gA[:, u, :], table1, SRC_A, h, gA_ld[u])
                            fetch(gA[:, u + 1, :], table1, SRC_A + 1, h, gA_ld[u + 1])
                        fetch(gB[:, h, :], table1, SRC_B, h, gB_ld[h])

                    def power(t, u, r):
                        ln.power(pool, t, u % 2)
                    pipe(pool, [(gather, 0), (power, 4)], NT, Q)

                @block.vector
                def _(dve):
                    tp.on_vector(dve)
                    V = nc.vector
                    dve.wait_ge(clear, 2)

                    def hots(t, u, r):
                        wait(dve, agg_done, t + 1 - Q)
                        if u % 2 == 0:
                            wait(dve, agg_done, t + 2 - Q)
                            V.tensor_scalar(ohB[:, u // 2, :], iota[:], dlB[:, bass.ds(r * 2 + u // 2, 1)], None,
                                            ALU.is_equal)
                        V.tensor_scalar(ohA[:, u, :], iota[:], dlA[:, bass.ds(t, 1)], None,
                                        ALU.is_equal).then_inc(oh_in, 1)

                    def own(t, u, r):
                        dve.wait_ge(agg_done, t + 1)
                        dve.wait_ge(hs_ld[u], 16 * (r + 1))
                        wait(dve, r_in, t - 1)
                        V.tensor_tensor(o[:, u % 2, :], psA[u % 2][:, :], hs[:, u, :], ALU.add).then_inc(o_in, 1)

                    def sum_(t, u, r):
                        dve.wait_ge(r_in, t + 1)
                        wait(dve, ln.x_in, t - 1)
                        V.tensor_tensor(ln.y[:, u % 2, :], o[:, u % 2, :], state(t), ALU.add).then_inc(ln.y_in, 1)
                        ln.statistics(dve, t, u % 2)

                    def norm(t, u, r):
                        wait(dve, F_done, t - 1)
                        V.tensor_scalar(kh[:, u % 2, :], keys[:], skey[:, bass.ds(t, 1)], None,
                                        ALU.is_equal).then_inc(kh_in, 1)
                        ln.apply(dve, t, u % 2, state(t))
                    pipe(dve, [(hots, 0), (own, 1), (sum_, 2), (norm, 3)], NT, Q)
                    dve.wait_ge(full_in, 1)
                    V.tensor_copy(full[:], psF[0:NT, :])

                @block.scalar
                def _(act):
                    def relu(t, u, r):
                        act.wait_ge(o_in, t + 1)
                        nc.scalar.activation(o[:, u % 2, :], o[:, u % 2, :], ACT.Relu,
                                             scale=dis1[:, bass.ds(t, 1)]).then_inc(r_in, 1)
                    pipe(act, [(relu, 0)], NT, Q)

                @block.tensor
                def _(pe):
                    tp.on_tensor(pe)
                    mm = nc.tensor.matmul
                    mm(psF[0:NT, :], zeros_h[:, 0:NT], zeros_h[:], start=True, stop=False)

                    def sums(t, u, r):
                        h, half_ = u // 2, slice((u % 2) * HALF, (u % 2 + 1) * HALF)
                        pe.wait_ge(oh_in, t + 1)
                        pe.wait_ge(gA_ld[u], 16 * (r + 1))
                        pe.wait_ge(gB_ld[h], 16 * (r + 1))
                        wait(pe, o_in, t - 1)
                        mm(psA[u % 2][:, :], ohA[:, u, :], gA[:, u, :], start=True, stop=False)
                        mm(psA[u % 2][:, :], ohB[half_, h, :], gB[half_, h, :], start=False,
                           stop=True).then_inc(agg_done, 1)

                    def segments(t, u, r):
                        pe.wait_ge(ln.x_in, t + 1)
                        mm(psF[0:NT, :], kh[:, u % 2, :], state(t), start=False, stop=False).then_inc(F_done, 1)
                    pipe(pe, [(sums, 0), (segments, 3)], NT, Q)
                    mm(psF[0:NT, :], zeros_h[:, 0:NT], zeros_h[:], start=False, stop=True).then_inc(full_in, 1)
            end_phase()

        with ExitStack() as s:
            ws = sb(s, "wcs", [P, DC, HID])
            rid = sb(s, "n3_rid", [P, Q, P])
            inm = sb(s, "n3_in", [P, 2, P])
            ek = sb(s, "n3_ek", [NT, 2, P])
            xn = sb(s, "n3_xn", [P, 2, D])
            xT = sb(s, "n3_xT", [P, 2, D])
            hs = sb(s, "n3_h", [P, 2, HID])
            ln = Norm(s, "n3", 2)
            psM = [ps(s, f"n3_psM{i}") for i in range(2)]
            psT = [ps(s, f"n3_psT{i}") for i in range(2)]
            psU = [ps(s, f"n3_psU{i}") for i in range(2)]
            w_ld = sem("n3_w")
            rid_ld = [sem(f"n3_rid{i}") for i in range(Q)]
            h_st = [sem(f"n3_h_st{i}") for i in range(2)]
            sel_in = sem("n3_sel_in")
            M_done = sem("n3_M_done")
            X_in = sem("n3_X_in")
            T_done = sem("n3_T_done")
            xT_in = sem("n3_xT_in")
            G_done = sem("n3_G_done")
            h_in = sem("n3_h_in")

            with nc.Block() as block:
                @block.sync
                def _(sp):
                    sp.dma_start(ws[:], wc.rearrange("(c p) n -> p c n", p=P)).then_inc(w_ld, 16)

                    def load(t, u, r):
                        wait(sp, sel_in, t + 1 - Q)
                        sp.dma_start(rid[:, u, :], rid_dram[bass.ds(t, 1), :].to_broadcast([P, P])).then_inc(rid_ld[u], 16)

                    def store(t, u, r):
                        wait(sp, h_in, t + 1)
                        sp.dma_start(table3[rows(t), :], hs[:, u % 2, :]).then_inc(h_st[u % 2], 16)
                    pipe(sp, [(load, 0), (store, 6)], NT, Q)
                    for i in range(2):
                        sp.wait_ge(h_st[i], 16 * NT // 2)

                @block.gpsimd
                def _(pool):
                    ln.begin(pool)
                    pipe(pool, [(lambda t, u, r: ln.power(pool, t, u % 2), 0)], NT, Q)

                @block.vector
                def _(dve):
                    V = nc.vector

                    def select(t, u, r):
                        dve.wait_ge(rid_ld[u], 16 * (r + 1))
                        wait(dve, M_done, t - 1)
                        V.tensor_scalar(inm[:, u % 2, :], rid[:, u, :], skey_in[:, bass.ds(t, 1)], None, ALU.is_equal)
                        V.tensor_scalar(ek[:, u % 2, :], rid[0:NT, u, :], keycol[:], None,
                                        ALU.is_equal).then_inc(sel_in, 1)

                    def sum_(t, u, r):
                        dve.wait_ge(M_done, t + 1)
                        wait(dve, ln.x_in, t - 1)
                        V.scalar_tensor_tensor(out=ln.y[:, u % 2, :], in0=psM[u % 2][:, :], scalar=rcnt[:, bass.ds(t, 1)],
                                               in1=state(t), op0=ALU.mult, op1=ALU.add).then_inc(ln.y_in, 1)
                        ln.statistics(dve, t, u % 2)

                    def norm(t, u, r):
                        wait(dve, X_in, t - 1)
                        wait(dve, T_done, t - 1)
                        ln.apply(dve, t, u % 2, xn[:, u % 2, :])
                    pipe(dve, [(select, 0), (sum_, 1), (norm, 2)], NT, Q)

                @block.scalar
                def _(act):
                    def keep(t, u, r):
                        act.wait_ge(ln.x_in, t + 1)
                        nc.scalar.activation(state(t), xn[:, u % 2, :], ACT.Copy).then_inc(X_in, 1)

                    def turned(t, u, r):
                        act.wait_ge(T_done, t + 1)
                        wait(act, G_done, t - 1)
                        nc.scalar.activation(xT[:, u % 2, :], psT[u % 2][:, :], ACT.Copy).then_inc(xT_in, 1)

                    def scale(t, u, r):
                        act.wait_ge(G_done, t + 1)
                        wait(act, h_st[u % 2], 16 * (r * 2 + u // 2))
                        nc.scalar.activation(hs[:, u % 2, :], psU[u % 2][:, 0:HID], ACT.Copy,
                                             scale=dis3[:, bass.ds(t, 1)]).then_inc(h_in, 1)
                    pipe(act, [(keep, 0), (turned, 0), (scale, 1)], NT, Q)

                @block.tensor
                def _(pe):
                    mm = nc.tensor.matmul

                    def means(t, u, r):
                        pe.wait_ge(sel_in, t + 1)
                        wait(pe, ln.y_in, t - 1)
                        mm(psM[u % 2][:, :], ek[:, u % 2, :], full[:], start=True, stop=False)
                        mm(psM[u % 2][:, :], inm[:, u % 2, :], state(t), start=False, stop=True).then_inc(M_done, 1)

                    def turn(t, u, r):
                        pe.wait_ge(ln.x_in, t + 1)
                        wait(pe, xT_in, t - 1)
                        for c in range(DC):
                            f = slice(c * P, (c + 1) * P)
                            last_one = nc.tensor.transpose(psT[u % 2][:, f], xn[:, u % 2, f], ident[:])
                        last_one.then_inc(T_done, 1)

                    def product(t, u, r):
                        pe.wait_ge(xT_in, t + 1)
                        wait(pe, h_in, t - 1)
                        for c in range(DC):
                            last_one = mm(psU[u % 2][:, 0:HID], xT[:, u % 2, c * P:(c + 1) * P], ws[:, c, :],
                                          start=c == 0, stop=c == DC - 1)
                        last_one.then_inc(G_done, 1)
                    pe.wait_ge(w_ld, 16)
                    pipe(pe, [(means, 0), (turn, 2), (product, 3)], NT, Q)
            end_phase()

        with ExitStack() as s:
            ws = sb(s, "wls", [HID, D])
            bcs = sb(s, "bcs", [HID, 1])
            bcB = sb(s, "bcB", [HID, P])
            blB = sb(s, "blB", [P, D])
            cl = sb(s, "cl", [P, D])
            slotidx = sb(s, "n4_idx", [P, 2, FIELDS], I32)
            gA = sb(s, "n4_gA", [P, Q, HID])
            gB = sb(s, "n4_gB", [P, 2, HID])
            hs = sb(s, "n4_hs", [P, Q, HID])
            ohA = sb(s, "n4_ohA", [P, Q, P])
            ohB = sb(s, "n4_ohB", [P, 2, P])
            aT = sb(s, "n4_aT", [HID, 2, P])
            xc = sb(s, "n4_xc", [P, 2, D])
            xo = sb(s, "n4_xo", [P, 2, D])
            ln = Norm(s, "n4", 2)
            psA = [ps(s, f"n4_psA{i}") for i in range(2)]
            psO = [ps(s, f"n4_psO{i}") for i in range(2)]
            psC = ps(s, "n4_psC")
            w_ld = [sem(f"n4_w{i}") for i in range(3)]
            tp = TablePass(s, "t3", table3, sums3, HID, gA, ohA, psA[0])
            clear = sem("n4_clear")
            bc_in = sem("n4_bc_in")
            cl_done = sem("n4_cl_done")
            cl_in = sem("n4_cl_in")
            idx_seen = sem("n4_idx_seen")
            idx_in = sem("n4_idx_in")
            gA_ld = [sem(f"n4_gA{i}") for i in range(Q)]
            gB_ld = [sem(f"n4_gB{i}") for i in range(2)]
            hs_ld = [sem(f"n4_hs{i}") for i in range(Q)]
            o_st = [sem(f"n4_o_st{i}") for i in range(2)]
            oh_in = sem("n4_oh_in")
            agg_done = sem("n4_agg_done")
            aT_in = sem("n4_aT_in")
            O_done = sem("n4_O_done")
            xc_in = sem("n4_xc_in")

            with nc.Block() as block:
                @block.sync
                def _(sp):
                    tp.on_sync(sp)
                    sp.dma_start(ws[:], wl).then_inc(w_ld[0], 16)
                    sp.dma_start(bcs[:], bc).then_inc(w_ld[1], 16)
                    sp.dma_start(blB[:], bl.to_broadcast([P, D])).then_inc(w_ld[2], 16)

                    def load(t, u, r):
                        wait(sp, agg_done, t + 1 - Q)
                        sp.dma_start(hs[:, u, :], table3[rows(t), :]).then_inc(hs_ld[u], 16)

                    def store(t, u, r):
                        wait(sp, ln.x_in, t + 1)
                        sp.dma_start(out[rows(t), :], xo[:, u % 2, :]).then_inc(o_st[u % 2], 16)
                    pipe(sp, [(load, 0), (store, 6)], NT, Q)
                    for i in range(2):
                        sp.wait_ge(o_st[i], 16 * NT // 2)

                @block.gpsimd
                def _(pool):
                    tp.on_gpsimd(pool)
                    ln.begin(pool)
                    pool.memset(gA[:], 0.0).then_inc(clear, 1)
                    pool.memset(gB[:], 0.0).then_inc(clear, 1)
                    pool.wait_ge(clear, 2)
                    pool.wait_ge(cl_in, 1)

                    table_mode = pool.value_load(mode_i[0:1, 0:1], min_val=0, max_val=1)

                    def fetch(into, table, field, v, signal):
                        pool.indirect_dma_start(
                            out=into, out_offset=None, in_=table,
                            in_offset=bass.IndirectOffsetOnAxis(ap=slotidx[:, v, field:field + 1], axis=0),
                            bounds_check=NP - 1, oob_is_err=False).then_inc(signal, 16)

                    def gather(t, u, r):
                        if u % 2:
                            return
                        h = u // 2
                        k = r * 2 + h
                        wait(pool, gA_ld[u], 16 * r)
                        wait(pool, gA_ld[u + 1], 16 * r)
                        wait(pool, gB_ld[h], 16 * r)
                        nc.gpsimd.tensor_copy(slotidx[:, h, :], IDX[:, bass.ds(k, 1), :].rearrange("p a f -> p (a f)")
                                              ).then_inc(idx_in, 1)
                        wait(pool, agg_done, t + 2 - Q)
                        wait(pool, idx_in, k + 1)
                        pool.nop().then_inc(idx_seen, 1)
                        with pool.If(table_mode > 0):
                            fetch(gA[:, u, :], sums3, EID_A, h, gA_ld[u])
                            fetch(gA[:, u + 1, :], sums3, EID_A + 1, h, gA_ld[u + 1])
                        with pool.Else():
                            fetch(gA[:, u, :], table3, SRC_A, h, gA_ld[u])
                            fetch(gA[:, u + 1, :], table3, SRC_A + 1, h, gA_ld[u + 1])
                        fetch(gB[:, h, :], table3, SRC_B, h, gB_ld[h])

                    def addend(t, u, r):
                        wait(pool, ln.y_in, t - 1)
                        nc.gpsimd.tensor_tensor(xc[:, u % 2, :], state(t), cl[:], ALU.add).then_inc(xc_in, 1)

                    def power(t, u, r):
                        ln.power(pool, t, u % 2)
                    pipe(pool, [(gather, 0), (addend, 1), (power, 4)], NT, Q)

                @block.vector
                def _(dve):
                    tp.on_vector(dve)
                    V = nc.vector
                    dve.wait_ge(w_ld[1], 16)
                    V.tensor_scalar(bcB[:], ones[:], bcs[:], None, ALU.mult).then_inc(bc_in, 1)
                    dve.wait_ge(w_ld[2], 16)
                    dve.wait_ge(cl_done, 1)
                    V.tensor_tensor(cl[:], psC[:, :], blB[:], ALU.add).then_inc(cl_in, 1)
                    dve.wait_ge(clear, 2)

                    def hots(t, u, r):
                        wait(dve, agg_done, t + 1 - Q)
                        if u % 2 == 0:
                            wait(dve, agg_done, t + 2 - Q)
                            V.tensor_scalar(ohB[:, u // 2, :], iota[:], dlB[:, bass.ds(r * 2 + u // 2, 1)], None,
                                            ALU.is_equal)
                        V.tensor_scalar(ohA[:, u, :], iota[:], dlA[:, bass.ds(t, 1)], None,
                                        ALU.is_equal).then_inc(oh_in, 1)

                    def sum_(t, u, r):
                        dve.wait_ge(O_done, t + 1)
                        dve.wait_ge(xc_in, t + 1)
                        wait(dve, ln.x_in, t - 1)
                        V.scalar_tensor_tensor(out=ln.y[:, u % 2, :], in0=psO[u % 2][:, :], scalar=dis3[:, bass.ds(t, 1)],
                                               in1=xc[:, u % 2, :], op0=ALU.mult, op1=ALU.add).then_inc(ln.y_in, 1)
                        ln.statistics(dve, t, u % 2)

                    def norm(t, u, r):
                        wait(dve, o_st[u % 2], 16 * (r * 2 + u // 2))
                        ln.apply(dve, t, u % 2, xo[:, u % 2, :])
                    pipe(dve, [(hots, 0), (sum_, 2), (norm, 3)], NT, Q)

                @block.scalar
                def _(act):
                    def turned(t, u, r):
                        act.wait_ge(agg_done, t + 1)
                        wait(act, O_done, t - 1)
                        nc.scalar.activation(aT[:, u % 2, :], psA[u % 2][:, 0:P], ACT.Copy).then_inc(aT_in, 1)
                    pipe(act, [(turned, 0)], NT, Q)

                @block.tensor
                def _(pe):
                    tp.on_tensor(pe)
                    mm = nc.tensor.matmul
                    pe.wait_ge(w_ld[0], 16)
                    pe.wait_ge(bc_in, 1)
                    mm(psC[:, :], bcB[:], ws[:], start=True, stop=True).then_inc(cl_done, 1)

                    def sums(t, u, r):
                        h, half_ = u // 2, slice((u % 2) * HALF, (u % 2 + 1) * HALF)
                        pe.wait_ge(oh_in, t + 1)
                        pe.wait_ge(gA_ld[u], 16 * (r + 1))
                        pe.wait_ge(gB_ld[h], 16 * (r + 1))
                        pe.wait_ge(hs_ld[u], 16 * (r + 1))
                        wait(pe, aT_in, t - 1)
                        to = psA[u % 2][:, 0:P]
                        mm(to, hs[:, u, :], ident[:], start=True, stop=False)
                        mm(to, gA[:, u, :], ohA[:, u, :], start=False, stop=False)
                        mm(to, gB[half_, h, :], ohB[half_, h, :], start=False, stop=True).then_inc(agg_done, 1)

                    def product(t, u, r):
                        pe.wait_ge(aT_in, t + 1)
                        wait(pe, ln.y_in, t - 1)
                        mm(psO[u % 2][:, :], aT[:, u % 2, :], ws[:], start=True, stop=True).then_inc(O_done, 1)
                    pipe(pe, [(sums, 0), (product, 1)], NT, Q)


def _search_path():
    low, high = np.zeros(E + 1, np.int64), np.full(E + 1, E)
    mids, rights = [], []
    for _ in range(LEVELS):
        mid = low + (high - low) // 2
        right = np.arange(E + 1) > mid
        mids.append(mid)
        rights.append(right)
        low, high = np.where(right, mid, low), np.where(right, high, mid)
    return np.minimum(np.stack(mids, 1), E - 1), np.stack(rights, 1)


def _columns(a, fill=0):
    a = np.concatenate([a, np.full((NP - len(a), *a.shape[1:]), fill, a.dtype)])
    return np.ascontiguousarray(np.swapaxes(a.reshape(NT, P, *a.shape[1:]), 0, 1))


def _layout(i):
    i = {k: np.asarray(v) for k, v in i.items()}
    src, dst = i["src"], i["dst"]
    pad = np.full(NP + RUN + P - E, 2 * E, np.int32)
    srcp, dstp = np.concatenate([src, pad]), np.concatenate([dst, pad])
    mids, rights = _search_path()
    before = (np.arange(E + 1) - 1) % E
    left = np.where(rights, FAR, 0).astype(np.float32)
    return {
        "x": np.concatenate([i["x"], np.zeros((NP - N, D), np.float32)]),
        "ea": np.concatenate([i["edge_attr_512"], np.zeros((NP - E, D), np.float32)]),
        "src_cols": _columns(src, 2 * E), "dst_cols": _columns(dst, 2 * E),
        "runs": np.stack([np.concatenate([srcp[r * P:r * P + RUN], dstp[r * P:r * P + RUN]]) for r in range(NT)]),
        "dst_steps": np.stack([dstp[r * NT:r * NT + NT + 1] for r in range(P)]),
        "path": _columns(src[mids]),
        "path_right": _columns(rights.astype(np.float32)),
        "path_left": _columns(left, -FAR),
        "leaf_dst": _columns(dst[before]), "leaf_src": _columns(src[before]),
        "dst_rows": dstp[:NP].reshape(NT, P),
        "w1": i["L0_gnn_W1"], "b1": np.ascontiguousarray(i["L0_gnn_b1"].reshape(DC, P).T),
        "w2": i["L0_gnn_W2"],
        "bn_cols": np.stack([i[f"L0_gnn_{k}"].reshape(DC, P).T for k in ("gamma", "beta", "b2")], 1),
        "wt": np.ascontiguousarray(i["L1_gnn_W"].T), "b": i["L1_gnn_b"].reshape(1, D),
        "wc": i["L3_gnn_W_conv"], "bc": i["L3_gnn_b_conv"].reshape(HID, 1),
        "wl": i["L3_gnn_W_lin"], "bl": i["L3_gnn_b_lin"].reshape(1, D),
    }


def kernel(**inputs):
    import concourse.bacc as bacc
    from concourse.bass_utils import run_bass_kernel_spmd

    nc = bacc.Bacc("TRN2", target_bir_lowering=False, num_devices=1)
    arrays = {f"in_{k}": np.ascontiguousarray(a) for k, a in _layout(inputs).items()}
    args = [nc.dram_tensor(k, a.shape, mybir.dt.from_np(a.dtype), kind="ExternalInput").ap()
            for k, a in arrays.items()]
    args.append(nc.dram_tensor("out_x", [NP, D], F32, kind="ExternalOutput").ap())
    build(nc, *args)
    r = run_bass_kernel_spmd(nc, [arrays], core_ids=[0])
    return r.results[0]["out_x"][:N]
```

```python
from contextlib import ExitStack
import math

import numpy as np
import concourse.bass as bass
from concourse import mybir

F32 = mybir.dt.float32
F32R = mybir.dt.float32r
BF16 = mybir.dt.bfloat16
I32 = mybir.dt.int32
ALU = mybir.AluOpType
ACT = mybir.ActivationFunctionType
AX = mybir.AxisListType

P = 128
N = 10000
E = 10000
D = 512
HID = 128
DC = D // P
NT = 80
NP = NT * P
PAIRS = NT // 2
WINDOW = P + 64
HALF = WINDOW - P
RUN = 3 * P
LEVELS = math.ceil(math.log2(E + 1))
SKIP = 30000
FAR = 32768
EPS = 1e-5
FIELDS = 6
SRC_A, EID_A, SRC_B, EID_B = 0, 2, 4, 5


def build(nc, x, ea, src_cols, dst_cols, runs, dst_steps, path, path_right, path_left,
          leaf_dst, leaf_src, dst_rows, w1, b1, w2, bn_cols, wt, b, wc, bc, wl, bl, out):
    ctx = ExitStack()
    with ctx:
        live = []

        def sem(name):
            live.append(nc.alloc_semaphore(name))
            return live[-1]

        def end_phase():
            nc.clear_and_free_semaphores(live)
            nc.all_engine_barrier()
            live.clear()

        def sb(scope, name, shape, dt=F32):
            return scope.enter_context(nc.sbuf_tensor(name, shape, dt))

        def ps(scope, name, shape=(P, D), dt=F32):
            return scope.enter_context(nc.psum_tensor(name, list(shape), dt))

        def rows(t):
            return bass.ds(t * P, P)

        table0 = nc.dram_tensor("table0", [NP, D], F32).ap()
        table1 = nc.dram_tensor("table1", [NP, D], F32).ap()
        table3 = nc.dram_tensor("table3", [NP, HID], F32).ap()
        sums1 = nc.dram_tensor("sums1", [NP, D], F32).ap()
        sums3 = nc.dram_tensor("sums3", [NP, HID], F32).ap()
        d_dram = nc.dram_tensor("d_dram", [NP, D], F32).ap()
        rid_dram = nc.dram_tensor("rid_dram", [NT, P], F32).ap()

        iota = sb(ctx, "iota", [P, P])
        power_of = sb(ctx, "power_of", [P, 2])
        pcol = sb(ctx, "pcol", [P, 1])
        ident = sb(ctx, "ident", [P, P])
        ones = sb(ctx, "ones", [P, P])
        IDX = sb(ctx, "IDX", [P, PAIRS, FIELDS], I32)
        dlA = sb(ctx, "dlA", [P, NT])
        dlB = sb(ctx, "dlB", [P, PAIRS])
        dis1 = sb(ctx, "dis1", [P, NT])
        dis3 = sb(ctx, "dis3", [P, NT])
        skey = sb(ctx, "skey", [P, NT])
        skey_in = sb(ctx, "skey_in", [P, NT])
        rcnt = sb(ctx, "rcnt", [P, NT])
        keys = sb(ctx, "keys", [P, NT])
        keycol = sb(ctx, "keycol", [NT, 1])
        mode_i = sb(ctx, "mode_i", [P, 1], I32)

        ld = [sem(f"prep_load{i}") for i in range(10)]
        p_iota = sem("p_iota")
        p_dve = sem("p_dve")
        p_hot = sem("p_hot")
        p_src_col = sem("p_src_col")
        p_hot_src = sem("p_hot_src")
        p_far = sem("p_far")
        p_hot_high = sem("p_hot_high")
        p_src_seen = sem("p_src_seen")
        p_hot_used = sem("p_hot_used")
        p_run = sem("p_run")
        ev = {name: sem(name) for name in (
            "parts_in",
            "degrees_summed", "node_counts", "tile_counts", "tile_counts_in", "starts", "blocks_in", "flags_in",
            "flags_summed", "fields_in", "fields_turned", "lasts_in", "lasts_turned", "carries_in",
            "carries_turned", "rids_in", "last_rids_in", "last_rids_turned", "key_rows_in", "keys_turned",
            "columns_in", "columns_turned")}
        p_sqrt = sem("p_sqrt")
        with ExitStack() as s:
            iota_h = sb(s, "iota_h", [P, P], BF16)
            zeros_h = sb(s, "zeros_h", [P, D], BF16)
            sc = sb(s, "sc", [P, NT], I32)
            dc = sb(s, "dc", [P, NT], I32)
            steps = sb(s, "steps", [P, NT + 1], I32)
            pth = sb(s, "pth", [P, NT, LEVELS], I32)
            pr = sb(s, "pr", [P, NT, LEVELS])
            pl = sb(s, "pl", [P, NT, LEVELS])
            pm = sb(s, "pm", [P, NT, LEVELS])
            ldst = sb(s, "ldst", [P, NT], I32)
            lsrc = sb(s, "lsrc", [P, NT], I32)
            iota_i = sb(s, "iota_i", [P, P], I32)
            pcol_i = sb(s, "pcol_i", [P, 1], I32)
            node_i = sb(s, "node_i", [NT, P], I32)
            nodec_i = sb(s, "nodec_i", [P, NT], I32)
            node = sb(s, "node", [NT, P])
            nodec = sb(s, "nodec", [P, NT])
            tri = sb(s, "tri", [NT, NT])
            part_i = sb(s, "part_i", [P, 6, NT], I32)
            part = sb(s, "part", [P, 6, NT])
            low = sb(s, "low", [P, NT])
            upp = sb(s, "upp", [P, NT])
            tmp = sb(s, "tmp", [P, NT])
            low_i = sb(s, "low_i", [P, NT], I32)
            leaf = sb(s, "leaf", [P, NT])
            count = sb(s, "count", [P, NT])
            SLOTS = 4
            src_col = sb(s, "src_col", [P, 2, SLOTS])
            hot_high = sb(s, "hot_high", [P, SLOTS, 2, NT], BF16)
            far = sb(s, "far", [P, SLOTS, 2, NT])
            hot = sb(s, "hot", [P, SLOTS, 2, P], BF16)
            hot_leaf = sb(s, "hot_leaf", [P, SLOTS, 3, P])
            deg = sb(s, "deg", [P, 2, NT])
            cntc = sb(s, "cntc", [NT, 1])
            startc = sb(s, "startc", [NT, 1])
            start_i = sb(s, "start_i", [NT, 3], I32)
            blk = sb(s, "blk", [NT, 1], I32)
            bits_i = sb(s, "bits_i", [NT, 7], I32)
            bits = sb(s, "bits", [NT, 7])
            run_i = sb(s, "run_i", [NT, 2 * RUN], I32)
            run = sb(s, "run", [NT, 2, 2, RUN])
            diff = sb(s, "diff", [NT, 2, RUN])
            flags = sb(s, "flags", [P, 2])
            mode = sb(s, "mode", [P, 1])
            a0 = sb(s, "a0", [NT, WINDOW + 1])
            vld = sb(s, "vld", [NT, WINDOW])
            nvl = sb(s, "nvl", [NT, WINDOW])
            alt = sb(s, "alt", [NT, 2, P])
            fld = sb(s, "fld", [NT, 6, P])
            dcmp = sb(s, "dcmp", [P, NT])
            sg = sb(s, "sg", [NT, 4, P])
            hold = sb(s, "hold", [NT, 6, P])
            last = sb(s, "last", [NT, 4])
            lrow = sb(s, "lrow", [1, 8, NT])
            carry = sb(s, "carry", [NT, 4])
            psD = ps(s, "psD")
            psS = ps(s, "psS")
            psL = ps(s, "psL")
            psX = ps(s, "psX")
            psY = ps(s, "psY")
            psZ = ps(s, "psZ")

            with nc.Block() as block:
                @block.sync
                def _(sp):
                    for i, (to, of) in enumerate(((sc, src_cols), (dc, dst_cols), (steps, dst_steps), (pth, path),
                                                  (pr, path_right), (pl, path_left), (ldst, leaf_dst),
                                                  (lsrc, leaf_src))):
                        sp.dma_start(to[:], of).then_inc(ld[i], 16)

                    sp.wait_ge(ev["rids_in"], 1)
                    sp.dma_start(rid_dram, sg[:, 2, :]).then_inc(ld[8], 16)
                    sp.wait_ge(ld[8], 16)

                @block.gpsimd
                def _(pool):
                    nc.gpsimd.iota(iota_i[:], [[1, P]], base=0, channel_multiplier=0).then_inc(p_iota, 1)
                    nc.gpsimd.iota(pcol_i[:], [[1, 1]], base=0, channel_multiplier=1).then_inc(p_iota, 1)
                    nc.gpsimd.iota(node_i[:], [[1, P]], base=0, channel_multiplier=P).then_inc(p_iota, 1)
                    nc.gpsimd.iota(nodec_i[:], [[P, NT]], base=0, channel_multiplier=1).then_inc(p_iota, 1)
                    pool.wait_ge(ev["parts_in"], 1)
                    with pool.Fori(0, NT // (2 * SLOTS)) as k:
                        for h in (0, 1):
                            c = k * 2 * SLOTS + h * SLOTS
                            nc.gpsimd.tensor_copy(src_col[:, h, :], part[:, 1, bass.ds(c, SLOTS)]
                                                  ).then_inc(p_src_col, 1)
                            pool.wait_ge(p_src_col, k * 2 + h + 1)
                            for u in range(SLOTS):
                                pool.wait_ge(p_hot_used, c + u + 1)
                                pool.nop().then_inc(p_src_seen, 1)
                                nc.gpsimd.tensor_scalar(hot[:, u, 0, :], iota_h[:], src_col[:, h, u:u + 1], None,
                                                        ALU.is_equal).then_inc(p_hot_src, 1)
                    pool.wait_ge(ev["blocks_in"], 1)
                    pool.indirect_dma_start(out=run_i[:], out_offset=None, in_=runs,
                                            in_offset=bass.IndirectOffsetOnAxis(ap=blk[:], axis=0)).then_inc(p_run, 16)

                @block.scalar
                def _(act):
                    act.wait_ge(ev["parts_in"], 1)
                    act_steps = 16
                    with act.Fori(0, NT // act_steps) as k:
                        for j in range(act_steps):
                            c, u = k * act_steps + j, j % SLOTS
                            for i in range(2):
                                nc.scalar.activation(far[:, u, i, :], iota[:, 0:NT], ACT.Square, scale=-1.0,
                                                     bias=part[:, 2 * i, bass.ds(c, 1)]).then_inc(p_far, 1)
                            act.wait_ge(p_hot_used, c + 1)
                            act.wait_ge(p_far, c * 2 + 2)
                            nc.scalar.activation(hot_high[:, u, :, :], far[:, u, :, :], ACT.Relu, scale=-1.0,
                                                 bias=ones[:, 0:1]).then_inc(p_hot_high, 1)
                    act.wait_ge(p_sqrt, 1)
                    nc.scalar.activation(deg[:], deg[:], ACT.Sqrt).then_inc(p_sqrt, 1)

                @block.vector
                def _(dve):
                    n = [0]

                    def step(ins):
                        n[0] += 1
                        ins.then_inc(p_dve, 1)
                        dve.wait_ge(p_dve, n[0])

                    V = nc.vector
                    V.memset(ones[:], 1.0)
                    V.memset(zeros_h[:], 0.0)
                    V.memset(power_of[:, 0:1], EPS)
                    V.memset(power_of[:, 1:2], -0.5)
                    V.memset(flags[:], 0.0)
                    V.memset(lrow[:], 0.0)
                    V.memset(hot[:], 0.0)
                    dve.wait_ge(p_iota, 4)
                    V.tensor_copy(iota[:], iota_i[:])
                    V.tensor_copy(iota_h[:], iota_i[:])
                    V.tensor_copy(pcol[:], pcol_i[:])
                    V.tensor_copy(node[:], node_i[:])
                    step(V.tensor_copy(nodec[:], nodec_i[:]))
                    V.tensor_scalar(ident[:], iota[:], pcol[:], None, ALU.is_equal)
                    V.tensor_scalar(tri[:], iota[0:NT, 0:NT], pcol[0:NT], None, ALU.is_gt)
                    V.tensor_scalar(leaf[:], nodec[:], 1.0, None, ALU.add)
                    for i, c in enumerate((sc, dc)):
                        dve.wait_ge(ld[i], 16)
                        V.tensor_scalar(part_i[:, 2 * i, :], c[:], 7, None, ALU.arith_shift_right)
                        V.tensor_scalar(part_i[:, 2 * i + 1, :], c[:], P - 1, None, ALU.bitwise_and)
                    for i in (3, 4, 5):
                        dve.wait_ge(ld[i], 16)
                    step(V.tensor_tensor(pm[:], pth[:], pr[:], ALU.mult))
                    step(V.tensor_reduce(low[:], pm[:], AX.X, ALU.max))
                    step(V.tensor_tensor(pm[:], pth[:], pl[:], ALU.add))
                    step(V.tensor_reduce(upp[:], pm[:], AX.X, ALU.min))
                    step(V.tensor_tensor(tmp[:], low[:], upp[:], ALU.is_ge))
                    step(V.scalar_tensor_tensor(out=low[:], in0=tmp[:], scalar=float(FAR), in1=low[:],
                                                op0=ALU.mult, op1=ALU.add))
                    step(V.tensor_copy(low_i[:], low[:]))
                    V.tensor_scalar(part_i[:, 4, :], low_i[:], 7, None, ALU.arith_shift_right)
                    V.tensor_scalar(part_i[:, 5, :], low_i[:], P - 1, None, ALU.bitwise_and)
                    for i in (6, 7):
                        dve.wait_ge(ld[i], 16)
                    step(V.tensor_tensor(tmp[:], ldst[:], lsrc[:], ALU.subtract))
                    step(V.tensor_scalar(count[:], tmp[:], 1.0, None, ALU.add))
                    step(V.tensor_copy(part[:], part_i[:]))
                    dve.nop().then_inc(ev["parts_in"], 1)
                    with dve.Fori(0, NT // SLOTS) as k:
                        for u in range(SLOTS):
                            c = k * SLOTS + u
                            dve.wait_ge(p_hot_used, c + 1)

                            def col(f):
                                return part[:, f, bass.ds(c, 1)]
                            V.tensor_scalar(hot[:, u, 1, :], iota_h[:], col(3), None, ALU.is_equal)
                            V.tensor_scalar(hot_leaf[:, u, 0, 0:NT], iota[:, 0:NT], col(4), None, ALU.is_equal)
                            for f, by in enumerate((leaf, count)):
                                last_one = V.tensor_scalar(hot_leaf[:, u, 1 + f, :], iota[:], col(5),
                                                           by[:, bass.ds(c, 1)], ALU.is_equal, ALU.mult)
                            last_one.then_inc(p_hot, 1)
                    dve.wait_ge(ev["degrees_summed"], 1)
                    step(V.tensor_scalar(deg[:, 0, :], psS[:, 0:NT], 1.0, None, ALU.add))
                    V.tensor_scalar(deg[:, 1, :], psD[:, 0:NT], 1.0, None, ALU.add).then_inc(p_sqrt, 1)
                    V.tensor_copy(tmp[:], psD[:, 0:NT]).then_inc(ev["node_counts"], 1)
                    dve.wait_ge(ev["tile_counts"], 1)
                    V.tensor_copy(cntc[:], psX[0:NT, 0:1]).then_inc(ev["tile_counts_in"], 1)
                    dve.wait_ge(ev["starts"], 1)
                    step(V.tensor_copy(startc[:], psY[0:NT, 0:1]))
                    step(V.tensor_copy(start_i[:, 0:1], startc[:]))
                    V.tensor_scalar(blk[:], start_i[:, 0:1], 7, None, ALU.arith_shift_right).then_inc(ev["blocks_in"], 1)
                    for i in range(7):
                        step(V.tensor_scalar(bits_i[:, i:i + 1], start_i[:, 0:1], i, 1, ALU.logical_shift_right,
                                        ALU.bitwise_and))
                    step(V.tensor_copy(bits[:], bits_i[:]))
                    dve.wait_ge(p_sqrt, 2)
                    step(V.reciprocal(dis1[:], deg[:, 0, :]))
                    step(V.reciprocal(dis3[:], deg[:, 1, :]))
                    dve.wait_ge(ld[2], 16)
                    step(V.tensor_tensor(dcmp[:], steps[:, 0:NT], steps[:, 1:NT + 1], ALU.is_gt))
                    step(V.tensor_reduce(flags[:, 0:1], dcmp[:], AX.X, ALU.max))
                    dve.wait_ge(p_run, 16)
                    step(V.tensor_copy(run[:, 0, :, :], run_i[:].rearrange("t (a j) -> t a j", a=2)))
                    at = 0
                    for i in (6, 5, 4, 3, 2, 1, 0):
                        by = 1 << i
                        width = WINDOW + by
                        now, then = run[:, at, :, 0:width], run[:, at, :, by:by + width]
                        step(V.tensor_tensor(diff[:, :, 0:width], then, now, ALU.subtract))
                        step(V.scalar_tensor_tensor(out=run[:, 1 - at, :, 0:width], in0=diff[:, :, 0:width],
                                                    scalar=bits[:, i:i + 1], in1=now, op0=ALU.mult, op1=ALU.add))
                        at = 1 - at
                    src_run, dst_run = run[:, at, 0, :], run[:, at, 1, :]
                    step(V.tensor_scalar(a0[:], dst_run[:, 0:WINDOW + 1], node[:, 0:1], None, ALU.subtract))
                    step(V.tensor_scalar(flags[0:NT, 1:2], a0[:, WINDOW:WINDOW + 1], float(P), None, ALU.is_lt))
                    step(V.tensor_scalar(vld[:], a0[:, 0:WINDOW], float(P), None, ALU.is_lt))
                    dve.nop().then_inc(ev["flags_in"], 1)
                    dve.wait_ge(ev["flags_summed"], 1)
                    step(V.tensor_reduce(mode[:], psX[:, 8:10], AX.X, ALU.max))
                    step(V.tensor_scalar(mode[:], mode[:], 1.0, None, ALU.min))
                    step(V.tensor_copy(mode_i[:], mode[:]))
                    m = mode[0:NT]
                    step(V.tensor_scalar(tmp[0:NT, 0:1], m, -1.0, 1.0, ALU.mult, ALU.add))
                    step(V.tensor_scalar(vld[:], vld[:], tmp[0:NT, 0:1], None, ALU.mult))
                    step(V.tensor_scalar(nvl[:], vld[:], -1.0, 1.0, ALU.mult, ALU.add))
                    step(V.tensor_scalar(alt[:, 0, :], node[:], -float(SKIP), None, ALU.add))
                    step(V.tensor_scalar(alt[:, 1, :], iota[0:NT, :], 1.0, None, ALU.add))
                    step(V.tensor_scalar(alt[:, 0, :], alt[:, 0, :], m, float(SKIP), ALU.mult, ALU.add))
                    step(V.tensor_scalar(alt[:, 1, :], alt[:, 1, :], m, -1.0, ALU.mult, ALU.add))
                    nva, va = nvl[:, 0:P], vld[:, 0:P]
                    for i in range(2):
                        step(V.tensor_tensor(alt[:, i, :], alt[:, i, :], nva, ALU.mult))
                    step(V.tensor_tensor(fld[:, 0, :], src_run[:, 0:P], va, ALU.mult))
                    step(V.tensor_scalar(fld[:, 1, :], iota[0:NT, :], startc[:], None, ALU.add))
                    step(V.tensor_tensor(fld[:, 2, :], a0[:, 0:P], va, ALU.mult))
                    step(V.tensor_tensor(fld[:, 1, :], fld[:, 1, :], va, ALU.mult))
                    step(V.scalar_tensor_tensor(out=fld[:, 0, :], in0=nva, scalar=float(SKIP), in1=fld[:, 0, :],
                                                op0=ALU.mult, op1=ALU.add))
                    step(V.tensor_tensor(fld[:, 1, :], fld[:, 1, :], alt[:, 0, :], ALU.add))
                    step(V.tensor_tensor(fld[:, 2, :], fld[:, 2, :], alt[:, 1, :], ALU.add))
                    step(V.tensor_scalar(tmp[0:NT, 0:HALF], iota[0:NT, 0:HALF], startc[:], float(P), ALU.add, ALU.add))
                    vb, nvb = vld[:, P:WINDOW], nvl[:, P:WINDOW]
                    for h in (0, HALF):
                        to = slice(h, h + HALF)
                        step(V.tensor_tensor(fld[:, 3, to], src_run[:, P:WINDOW], vb, ALU.mult))
                        step(V.tensor_tensor(fld[:, 4, to], tmp[0:NT, 0:HALF], vb, ALU.mult))
                        step(V.tensor_tensor(fld[:, 5, to], a0[:, P:WINDOW], vb, ALU.mult))
                        step(V.tensor_tensor(fld[:, 5, to], fld[:, 5, to], nvb, ALU.subtract))
                        for f in (3, 4):
                            step(V.scalar_tensor_tensor(out=fld[:, f, to], in0=nvb, scalar=float(SKIP),
                                                        in1=fld[:, f, to], op0=ALU.mult, op1=ALU.add))
                    dve.nop().then_inc(ev["fields_in"], 1)
                    dve.wait_ge(ev["fields_turned"], 1)
                    two = "p (k u) -> p k u"
                    A = psY[:, 0:3 * NT].rearrange("p (f k u) -> p f k u", f=3, u=2)
                    for f, to in ((0, SRC_A), (1, EID_A)):
                        step(V.tensor_copy(IDX[:, :, to:to + 2], A[:, f, :, :]))
                    step(V.tensor_copy(dlA[:].rearrange(two, u=2), A[:, 2, :, :]))
                    B = psZ[:, 0:3 * NT].rearrange("p (f k u) -> p f k u", f=3, u=2)
                    for h in (0, 1):
                        to = slice(h * HALF, (h + 1) * HALF)
                        step(V.tensor_copy(IDX[to, :, SRC_B], B[to, 0, :, h]))
                        step(V.tensor_copy(IDX[to, :, EID_B], B[to, 1, :, h]))
                        step(V.tensor_copy(dlB[to, :], B[to, 2, :, h]))
                    step(V.tensor_copy(sg[:, 0:2, :], psL[0:NT, 0:2 * P].rearrange("t (f j) -> t f j", f=2)))
                    step(V.tensor_scalar(hold[:, 0, :], sg[:, 0, :], 0.0, None, ALU.is_equal))
                    step(V.scalar_tensor_tensor(out=hold[:, 1, :], in0=sg[:, 0, :], scalar=-1.0, in1=hold[:, 0, :],
                                                op0=ALU.add, op1=ALU.add))
                    step(V.tensor_copy(hold[:, 2, :], sg[:, 1, :]))
                    step(V.tensor_tensor_scan(hold[:, 3, :], hold[:, 0, :], hold[:, 1, :], 0.0, ALU.mult, ALU.add))
                    step(V.tensor_tensor_scan(hold[:, 4, :], hold[:, 0, :], hold[:, 2, :], 0.0, ALU.mult, ALU.add))
                    step(V.tensor_reduce(last[:, 0:1], hold[:, 0, :], AX.X, ALU.min))
                    step(V.tensor_copy(last[:, 1:2], hold[:, 3, P - 1:P]))
                    V.tensor_copy(last[:, 2:3], hold[:, 4, P - 1:P]).then_inc(ev["lasts_in"], 1)
                    dve.wait_ge(ev["lasts_turned"], 1)
                    step(V.tensor_copy(lrow[:, 0:3, :], psX[0:1, 0:3 * NT].rearrange("o (f t) -> o f t", f=3)))
                    step(V.tensor_tensor_scan(lrow[:, 3, :], lrow[:, 0, :], lrow[:, 1, :], 0.0, ALU.mult, ALU.add))
                    step(V.tensor_tensor_scan(lrow[:, 4, :], lrow[:, 0, :], lrow[:, 2, :], 0.0, ALU.mult, ALU.add))
                    step(V.tensor_copy(lrow[:, 5, 1:NT], lrow[:, 3, 0:NT - 1]))
                    V.tensor_copy(lrow[:, 6, 1:NT], lrow[:, 4, 0:NT - 1]).then_inc(ev["carries_in"], 1)
                    dve.wait_ge(ev["carries_turned"], 1)
                    step(V.tensor_copy(carry[:, 0:2], psY[0:NT, 0:2]))
                    step(V.tensor_tensor_scan(sg[:, 0, :], hold[:, 0, :], hold[:, 1, :], carry[:, 0:1], ALU.mult,
                                              ALU.add))
                    step(V.tensor_tensor_scan(sg[:, 1, :], hold[:, 0, :], hold[:, 2, :], carry[:, 1:2], ALU.mult,
                                              ALU.add))
                    step(V.tensor_scalar(sg[:, 2, :], sg[:, 0, :], 0.0, float(N), ALU.is_equal, ALU.mult))
                    step(V.tensor_tensor(sg[:, 2, :], sg[:, 2, :], sg[:, 0, :], ALU.add))
                    dve.nop().then_inc(ev["rids_in"], 1)
                    V.tensor_copy(last[:, 3:4], sg[:, 2, P - 1:P]).then_inc(ev["last_rids_in"], 1)
                    dve.wait_ge(ev["last_rids_turned"], 1)
                    step(V.memset(lrow[:, 0, 0:1], float(N)))
                    step(V.tensor_copy(lrow[:, 0, 1:NT], psX[0:1, 0:NT - 1]))
                    step(V.memset(lrow[:, 1, 0:1], 0.0))
                    step(V.tensor_tensor(lrow[:, 1, 1:NT], lrow[:, 0, 1:NT], lrow[:, 0, 0:NT - 1], ALU.is_equal))
                    step(V.tensor_scalar(lrow[:, 2, 1:NT], lrow[:, 0, 1:NT], float(N), None, ALU.is_equal))
                    step(V.memset(lrow[:, 2, 0:1], 0.0))
                    step(V.tensor_tensor(lrow[:, 1, :], lrow[:, 1, :], lrow[:, 2, :], ALU.add))
                    step(V.scalar_tensor_tensor(out=lrow[:, 1, :], in0=lrow[:, 1, :], scalar=-float(FAR),
                                                in1=lrow[:, 0, :], op0=ALU.mult, op1=ALU.add))
                    dve.nop().then_inc(ev["key_rows_in"], 1)
                    dve.wait_ge(ev["keys_turned"], 1)
                    step(V.tensor_copy(carry[:, 2:3], psY[0:NT, 4:5]))
                    step(V.tensor_copy(keycol[:], psY[0:NT, 5:6]))
                    step(V.tensor_copy(keys[:], psZ[:, 0:NT]))
                    step(V.tensor_scalar(hold[:, 3, :], sg[:, 2, :], carry[:, 2:3], 0.0, ALU.is_equal, ALU.is_equal))
                    step(V.tensor_scalar(hold[:, 4, :], sg[:, 2, :], last[:, 3:4], 0.0, ALU.is_equal, ALU.is_equal))
                    step(V.tensor_scalar(hold[:, 5, :], node[:], float(N), None, ALU.is_lt))
                    step(V.tensor_tensor(sg[:, 0, :], sg[:, 0, :], hold[:, 5, :], ALU.mult))
                    step(V.tensor_tensor(sg[:, 3, :], sg[:, 0, :], hold[:, 3, :], ALU.mult))
                    step(V.tensor_tensor(sg[:, 3, :], sg[:, 3, :], hold[:, 4, :], ALU.mult))
                    dve.nop().then_inc(ev["columns_in"], 1)
                    dve.wait_ge(ev["columns_turned"], 1)
                    step(V.tensor_copy(skey[:], psX[:, 0:NT]))
                    step(V.tensor_copy(skey_in[:], psX[:, NT:2 * NT]))
                    step(V.reciprocal(rcnt[:], psX[:, 2 * NT:3 * NT]))

                @block.tensor
                def _(pe):
                    mm = nc.tensor.matmul
                    pe.wait_ge(p_dve, 1)
                    for o, m_, w in ((psD, P, NT), (psS, P, NT), (psL, NT, 2 * P)):
                        last_one = mm(o[0:m_, 0:w], zeros_h[:, 0:m_], zeros_h[:, 0:w], start=True, stop=False)
                    last_one.then_inc(p_hot_used, SLOTS)
                    with pe.Fori(0, NT // SLOTS) as k:
                        for u in range(SLOTS):
                            pe.wait_ge(p_hot, k * SLOTS + u + 1)
                            pe.wait_ge(p_hot_src, k * SLOTS + u + 1)
                            pe.wait_ge(p_hot_high, k * SLOTS + u + 1)
                            mm(psS[:, 0:NT], hot[:, u, 0, :], hot_high[:, u, 0, :], start=False, stop=False)
                            mm(psD[:, 0:NT], hot[:, u, 1, :], hot_high[:, u, 1, :], start=False, stop=False)
                            mm(psL[0:NT, 0:2 * P], hot_leaf[:, u, 0, 0:NT],
                               hot_leaf[:, u, 1:3, :].rearrange("p f j -> p (f j)"),
                               start=False, stop=False).then_inc(p_hot_used, 1)
                    for o, m_, w in ((psD, P, NT), (psS, P, NT), (psL, NT, 2 * P)):
                        last_one = mm(o[0:m_, 0:w], zeros_h[:, 0:m_], zeros_h[:, 0:w], start=False, stop=True)
                    last_one.then_inc(ev["degrees_summed"], 1)
                    pe.wait_ge(ev["node_counts"], 1)
                    mm(psX[0:NT, 0:1], tmp[:], ones[:, 0:1], start=True, stop=True).then_inc(ev["tile_counts"], 1)
                    pe.wait_ge(ev["tile_counts_in"], 1)
                    mm(psY[0:NT, 0:1], tri[:], cntc[:], start=True, stop=True).then_inc(ev["starts"], 1)
                    pe.wait_ge(ev["flags_in"], 1)
                    mm(psX[:, 8:10], ones[:], flags[:], start=True, stop=True).then_inc(ev["flags_summed"], 1)
                    pe.wait_ge(ev["fields_in"], 1)
                    for f in range(3):
                        nc.tensor.transpose(psY[:, f * NT:(f + 1) * NT], fld[:, f, :], ident[0:NT, 0:NT])
                    for f in range(3):
                        last_one = nc.tensor.transpose(psZ[:, f * NT:(f + 1) * NT], fld[:, 3 + f, :],
                                                       ident[0:NT, 0:NT])
                    last_one.then_inc(ev["fields_turned"], 1)
                    pe.wait_ge(ev["lasts_in"], 1)
                    for f in range(3):
                        last_one = mm(psX[0:1, f * NT:(f + 1) * NT], last[:, f:f + 1], ident[0:NT, 0:NT],
                                      start=True, stop=True)
                    last_one.then_inc(ev["lasts_turned"], 1)
                    pe.wait_ge(ev["carries_in"], 1)
                    for f in range(2):
                        last_one = mm(psY[0:NT, f:f + 1], lrow[:, 5 + f, :], ones[0:1, 0:1], start=True, stop=True)
                    last_one.then_inc(ev["carries_turned"], 1)
                    pe.wait_ge(ev["last_rids_in"], 1)
                    mm(psX[0:1, 0:NT], last[:, 3:4], ident[0:NT, 0:NT],
                       start=True, stop=True).then_inc(ev["last_rids_turned"], 1)
                    pe.wait_ge(ev["key_rows_in"], 1)
                    mm(psY[0:NT, 4:5], lrow[:, 0, :], ones[0:1, 0:1], start=True, stop=True)
                    mm(psY[0:NT, 5:6], lrow[:, 1, :], ones[0:1, 0:1], start=True, stop=True)
                    mm(psZ[:, 0:NT], ones[0:1, :], lrow[:, 1, :], start=True, stop=True).then_inc(ev["keys_turned"], 1)
                    pe.wait_ge(ev["columns_in"], 1)
                    for f, of in enumerate((0, 3, 1)):
                        last_one = nc.tensor.transpose(psX[:, f * NT:(f + 1) * NT], sg[:, of, :], ident[0:NT, 0:NT])
                    last_one.then_inc(ev["columns_turned"], 1)
            end_phase()

        def wait(eng, semaphore, value):
            if not (isinstance(value, int) and value <= 0):
                eng.wait_ge(semaphore, value)

        def pipe(eng, stages, count, unroll):
            first = 2 * unroll
            for t in range(first):
                for f, lag, *more in stages:
                    if t - lag >= 0:
                        f(t - lag, (t - lag) % unroll, (t - lag) // unroll, *more)
            with eng.Fori(2, count // unroll) as r:
                for u in range(unroll):
                    for f, lag, *more in stages:
                        f(r * unroll + (u - lag), (u - lag) % unroll, r + (u - lag) // unroll, *more)
            for t in range(count, count + max(stage[1] for stage in stages)):
                for f, lag, *more in stages:
                    if t - lag < count:
                        f(t - lag, (t - lag) % unroll, (t - lag) // unroll, *more)

        class TablePass:

            def __init__(self, scope, name, table, sums, width, buffers, squares, psum, edge_rows=None):
                self.msg, self.cur, self.edge, self.zero = (buffers[:, i, :] for i in range(4))
                self.eq, self.eq_below, self.below = (squares[:, i, :] for i in range(3))
                self.psum = psum
                self.table, self.sums, self.edge_rows = table, sums, edge_rows
                self.src_i = sb(scope, f"{name}_src_i", [P, NT], I32)
                self.dst_i = sb(scope, f"{name}_dst_i", [P, NT], I32)
                self.dst = sb(scope, f"{name}_dst", [P, NT])
                self.row_i = sb(scope, f"{name}_row_i", [P, P], I32)
                self.dup = sb(scope, f"{name}_dup", [P, 1])
                self.to = sb(scope, f"{name}_to", [P, 1], I32)
                self.of = sb(scope, f"{name}_of", [P, 1], I32)
                self.width = width
                self.cols_ld = [sem(f"{name}_cols{i}") for i in range(2)]
                self.zero_in = sem(f"{name}_zero_in")
                self.zeroed = sem(f"{name}_zeroed")
                self.step_in = sem(f"{name}_step")
                self.tile = sem(f"{name}_tile")
                self.row_ld = sem(f"{name}_row_ld")
                self.edge_ld = sem(f"{name}_edge_ld")
                self.of_in = sem(f"{name}_of_in")
                self.msg_ld = sem(f"{name}_msg_ld")
                self.msg_in = sem(f"{name}_msg_in")
                self.to_in = sem(f"{name}_to_in")
                self.sum_done = sem(f"{name}_sum_done")
                self.cur_ld = sem(f"{name}_cur_ld")
                self.cur_in = sem(f"{name}_cur_in")
                self.cur_st = sem(f"{name}_cur_st")
                self.seen = sem(f"{name}_seen")
                self.seen_sp = sem(f"{name}_seen_sp")

            def on_sync(self, sp):
                mode = sp.value_load(mode_i[0:1, 0:1], min_val=0, max_val=1)
                with sp.If(mode > 0):
                    sp.dma_start(self.src_i[:], src_cols).then_inc(self.cols_ld[0], 16)
                    sp.dma_start(self.dst_i[:], dst_cols).then_inc(self.cols_ld[1], 16)
                    sp.wait_ge(self.zero_in, 1)
                    with sp.Fori(0, NT) as t:
                        sp.dma_start(self.sums[rows(t), :], self.zero).then_inc(self.zeroed, 16)
                        sp.wait_ge(self.zeroed, 16 * (t + 1))
                        sp.nop().then_inc(self.seen_sp, 1)
                    with sp.Fori(0, NT) as t:
                        sp.wait_ge(self.tile, t + 1)
                        sp.nop().then_inc(self.seen_sp, 1)
                        sp.dma_start(self.row_i[:], dst_rows[bass.ds(t, 1), :].to_broadcast([P, P])
                                     ).then_inc(self.row_ld, 16)
                        if self.edge_rows is not None:
                            sp.dma_start(self.edge, self.edge_rows[rows(t), :]).then_inc(self.edge_ld, 16)

            def on_gpsimd(self, pool):
                mode = pool.value_load(mode_i[0:1, 0:1], min_val=0, max_val=1)
                with pool.If(mode > 0):
                    pool.wait_ge(self.cols_ld[0], 16)
                    pool.wait_ge(self.zero_in, 1)
                    pool.wait_ge(self.zeroed, 16 * NT)
                    pool.nop().then_inc(self.tile, 1)
                    with pool.Fori(0, NT) as t:
                        nc.gpsimd.tensor_copy(self.of[:], self.src_i[:, bass.ds(t, 1)]).then_inc(self.of_in, 1)
                        pool.wait_ge(self.of_in, t + 1)
                        pool.nop().then_inc(self.seen, 1)
                        pool.indirect_dma_start(out=self.msg, out_offset=None, in_=self.table,
                                                in_offset=bass.IndirectOffsetOnAxis(ap=self.of[:], axis=0),
                                                bounds_check=N - 1, oob_is_err=False).then_inc(self.msg_ld, 16)
                        pool.wait_ge(self.to_in, t + 1)
                        pool.nop().then_inc(self.seen, 1)
                        pool.indirect_dma_start(out=self.cur, out_offset=None, in_=self.sums,
                                                in_offset=bass.IndirectOffsetOnAxis(ap=self.to[:], axis=0),
                                                bounds_check=N - 1, oob_is_err=False).then_inc(self.cur_ld, 16)
                        pool.wait_ge(self.cur_in, t + 1)
                        pool.nop().then_inc(self.seen, 1)
                        pool.indirect_dma_start(out=self.sums, in_=self.cur, in_offset=None,
                                                out_offset=bass.IndirectOffsetOnAxis(ap=self.to[:], axis=0),
                                                bounds_check=N - 1, oob_is_err=False).then_inc(self.cur_st, 16)
                        pool.wait_ge(self.cur_st, 16 * (t + 1))
                        pool.wait_ge(self.msg_ld, 16 * (t + 1))
                        pool.nop().then_inc(self.tile, 1)

            def on_vector(self, dve):
                V = nc.vector
                mode = dve.value_load(mode_i[0:1, 0:1], min_val=0, max_val=1)
                with dve.If(mode > 0):
                    V.memset(self.msg, 0.0)
                    V.memset(self.cur, 0.0)
                    V.tensor_scalar(self.below, iota[:], pcol[:], None, ALU.is_lt)
                    V.memset(self.zero, 0.0).then_inc(self.zero_in, 1)
                    dve.wait_ge(self.cols_ld[1], 16)
                    V.tensor_copy(self.dst[:], self.dst_i[:]).then_inc(self.step_in, 1)
                    dve.wait_ge(self.step_in, 1)
                    steps_ = 3 if self.edge_rows is None else 4
                    with dve.Fori(0, NT) as t:
                        n = [0]

                        def step(ins):
                            n[0] += 1
                            ins.then_inc(self.step_in, 1)
                            dve.wait_ge(self.step_in, t * steps_ + (n[0] + 1))
                        dve.wait_ge(self.row_ld, 16 * (t + 1))
                        step(V.tensor_scalar(self.eq, self.row_i[:], self.dst[:, bass.ds(t, 1)], None, ALU.is_equal))
                        step(V.tensor_tensor(self.eq_below, self.eq, self.below, ALU.mult))
                        step(V.tensor_reduce(self.dup[:], self.eq_below, AX.X, ALU.max))
                        V.tensor_scalar(self.to[:], self.dup[:], float(SKIP), self.dst[:, bass.ds(t, 1)],
                                        ALU.mult, ALU.add).then_inc(self.to_in, 1)
                        dve.wait_ge(self.msg_ld, 16 * (t + 1))
                        if self.edge_rows is not None:
                            dve.wait_ge(self.edge_ld, 16 * (t + 1))
                            step(V.tensor_tensor(self.msg, self.msg, self.edge, ALU.add))
                            V.tensor_scalar(self.msg, self.msg, 0.0, None, ALU.max).then_inc(self.msg_in, 1)
                        else:
                            dve.nop().then_inc(self.msg_in, 1)
                        dve.wait_ge(self.cur_ld, 16 * (t + 1))
                        dve.wait_ge(self.sum_done, t + 1)
                        V.tensor_tensor(self.cur, self.cur, self.psum[:, 0:self.width],
                                        ALU.add).then_inc(self.cur_in, 1)

            def on_tensor(self, pe):
                mode = pe.value_load(mode_i[0:1, 0:1], min_val=0, max_val=1)
                with pe.If(mode > 0):
                    with pe.Fori(0, NT) as t:
                        pe.wait_ge(self.msg_in, t + 1)
                        nc.tensor.matmul(self.psum[:, 0:self.width], self.eq, self.msg,
                                         start=True, stop=True).then_inc(self.sum_done, 1)

        aB = sb(ctx, "aB", [P, D])
        cB = sb(ctx, "cB", [P, D])

        NQ, Q = NT // 4, 4
        with ExitStack() as s:
            w1p = sb(s, "w1p", [P, 2, DC, D], F32R)
            w2p = sb(s, "w2p", [P, 2, DC, D], F32R)
            b1s = sb(s, "b1s", [P, DC])
            bn_in = sb(s, "bn_in", [P, 3, DC])
            slotidx = sb(s, "slotidx", [P, 2, FIELDS], I32)
            gA = sb(s, "gA", [P, 2 * Q, D])
            mA = sb(s, "mA", [P, 2 * Q, D])
            gB = sb(s, "gB", [P, Q, D])
            mB = sb(s, "mB", [P, Q, D])
            pA = sb(s, "pA", [P, Q, 2, D], F32R)
            pB = sb(s, "pB", [P, 2, 2, D], F32R)
            xs = sb(s, "xs", [P, 2 * Q, D])
            ohA = sb(s, "ohA", [P, Q, P], F32R)
            ohB = sb(s, "ohB", [P, 2, P], F32R)
            hs = sb(s, "hs", [P, Q, D])
            hT = sb(s, "hT", [P, 2, DC, Q * P], F32R)
            gf = sb(s, "gf", [P, 2, Q * P])
            gT = sb(s, "gT", [P, 2, DC, Q * P], F32R)
            ds = sb(s, "ds", [P, Q, D])
            sq = sb(s, "sq", [P, Q, D])
            real = sb(s, "real", [P, NT])
            S1 = sb(s, "S1", [P, D])
            S2 = sb(s, "S2", [P, D])
            col = sb(s, "col", [P, 6, DC])
            psA = [ps(s, f"psA{i}") for i in range(2)]
            psT = [ps(s, f"psT{i}") for i in range(2)]
            psG = [ps(s, f"psG{i}") for i in range(2)]
            psU = [ps(s, f"psU{i}") for i in range(2)]

            tp = TablePass(s, "t0", x, table0, D, gA, sq[:, :, 0:P], psA[0], ea)
            w_ld = [sem(f"l0_weights{i}") for i in range(4)]
            w_hi = sem("l0_weights_high")
            w_lo = sem("l0_weights_low")
            clear = sem("l0_clear")
            idx_seen = sem("l0_idx_seen")
            idx_in = sem("l0_idx_in")
            gA_ld = [sem(f"l0_gA{i}") for i in range(2 * Q)]
            mA_ld = [sem(f"l0_mA{i}") for i in range(2 * Q)]
            gB_ld = [sem(f"l0_gB{i}") for i in range(Q)]
            mB_ld = [sem(f"l0_mB{i}") for i in range(Q)]
            xs_ld = [sem(f"l0_x{i}") for i in range(2 * Q)]
            d_st = [sem(f"l0_d{i}") for i in range(Q)]
            sumA = sem("l0_sumA")
            sumB = sem("l0_sumB")
            hiA = sem("l0_highA")
            hiB = sem("l0_highB")
            loA = sem("l0_lowA")
            loB = sem("l0_lowB")
            agg_done = sem("l0_agg_done")
            h_in = sem("l0_h_in")
            T_done = sem("l0_T_done")
            hT_hi = sem("l0_hT_high")
            hT_lo = sem("l0_hT_low")
            g1_done = sem("l0_g1_done")
            gf_in = sem("l0_gf_in")
            gT_hi = sem("l0_gT_high")
            gT_lo = sem("l0_gT_low")
            g2_done = sem("l0_g2_done")
            d_in = sem("l0_d_in")
            s1_in = sem("l0_s1_in")
            sq_in = sem("l0_sq_in")
            s2_in = sem("l0_s2_in")
            bn_sum = sem("bn_sum")
            bn_var = sem("bn_var")
            bn_pow = sem("bn_pow")
            bn_step = sem("bn_step")
            bn_diag = sem("bn_diag")
            bn_rows = sem("bn_rows")

            with nc.Block() as block:
                @block.sync
                def _(sp):
                    sp.dma_start(ds[:], w1.rearrange("(c p) n -> p c n", p=P)).then_inc(w_ld[0], 16)
                    sp.dma_start(hs[:], w2.rearrange("(c p) n -> p c n", p=P)).then_inc(w_ld[1], 16)
                    sp.dma_start(b1s[:], b1).then_inc(w_ld[2], 16)
                    sp.dma_start(bn_in[:], bn_cols).then_inc(w_ld[3], 16)
                    tp.on_sync(sp)

                    def load(q, v, r):
                        for u in range(Q):
                            wait(sp, d_in, Q * q + u - 2 * Q + 1)
                            sp.dma_start(xs[:, Q * v + u, :], x[rows(q * Q + u), :]).then_inc(xs_ld[Q * v + u], 16)

                    def store(q, v, r, u):
                        wait(sp, d_in, Q * q + u + 1)
                        sp.dma_start(d_dram[rows(q * Q + u), :], ds[:, u, :]).then_inc(d_st[u], 16)
                    pipe(sp, [(store, 2, 0), (store, 2, 1), (store, 2, 2), (store, 2, 3), (load, 0)], NQ, 2)
                    for u in range(Q):
                        sp.wait_ge(d_st[u], 16 * NQ)

                @block.gpsimd
                def _(pool):
                    tp.on_gpsimd(pool)
                    pool.memset(gA[:], 0.0).then_inc(clear, 1)
                    pool.memset(gB[:], 0.0).then_inc(clear, 1)
                    pool.memset(S2[:], 0.0).then_inc(clear, 1)
                    pool.wait_ge(clear, 5)
                    table_mode = pool.value_load(mode_i[0:1, 0:1], min_val=0, max_val=1)

                    def fetch(into, table, field, v, signal, bound):
                        pool.indirect_dma_start(
                            out=into, out_offset=None, in_=table,
                            in_offset=bass.IndirectOffsetOnAxis(ap=slotidx[:, v, field:field + 1], axis=0),
                            bounds_check=bound, oob_is_err=False).then_inc(signal, 16)

                    def gather(q, v, r, h):
                        k = q * 2 + h
                        a, b_ = Q * v + 2 * h, 2 * v + h
                        before, round_ = (0, r) if v else (1, r - 1)
                        for w in (gA_ld, mA_ld):
                            for u in (0, 1):
                                wait(pool, w[Q * before + 2 * h + u], 16 * (round_ + 1))
                        wait(pool, gB_ld[2 * before + h], 16 * (round_ + 1))
                        wait(pool, mB_ld[2 * before + h], 16 * (round_ + 1))
                        nc.gpsimd.tensor_copy(slotidx[:, h, :], IDX[:, bass.ds(k, 1), :].rearrange("p a f -> p (a f)")
                                              ).then_inc(idx_in, 1)
                        wait(pool, loA, Q * q + 2 * h + 2 - 2 * Q)
                        wait(pool, loB, k + 1 - Q)
                        wait(pool, idx_in, k + 1)
                        pool.nop().then_inc(idx_seen, 1)
                        for u in (0, 1):
                            fetch(gA[:, a + u, :], x, SRC_A + u, h, gA_ld[a + u], N - 1)
                        with pool.If(table_mode > 0):
                            for u in (0, 1):
                                fetch(mA[:, a + u, :], table0, EID_A + u, h, mA_ld[a + u], NP - 1)
                        with pool.Else():
                            for u in (0, 1):
                                fetch(mA[:, a + u, :], ea, EID_A + u, h, mA_ld[a + u], N - 1)
                        fetch(gB[:, b_, :], x, SRC_B, h, gB_ld[b_], N - 1)
                        fetch(mB[:, b_, :], ea, EID_B, h, mB_ld[b_], N - 1)

                    def squares(q, v, r, u):
                        wait(pool, sq_in, Q * q + u + 1)
                        wait(pool, s2_in, Q * q + u)
                        nc.gpsimd.tensor_tensor(S2[:], S2[:], sq[:, u, :], ALU.add).then_inc(s2_in, 1)
                    pipe(pool, [(squares, 3, 0), (gather, 0, 0), (squares, 3, 1), (squares, 3, 2), (gather, 0, 1),
                                (squares, 3, 3)], NQ, 2)
                    pool.wait_ge(bn_var, 1)
                    nc.gpsimd.tensor_tensor(col[:, 3, :], col[:, 1, :], power_of[:, 1:2].to_broadcast([P, DC]),
                                            ALU.pow).then_inc(bn_pow, 1)

                @block.vector
                def _(dve):
                    V = nc.vector
                    tp.on_vector(dve)
                    V.memset(mA[:], 0.0).then_inc(clear, 1)
                    V.memset(mB[:], 0.0).then_inc(clear, 1)
                    V.memset(real[:, 0:N // P], 1.0)
                    for t in range(N // P, NT):
                        V.tensor_scalar(real[:, t:t + 1], pcol[:], float(N - t * P), None, ALU.is_lt)
                    V.memset(S1[:], 0.0).then_inc(s1_in, 1)
                    for i, (w, of) in enumerate(((w1p, ds), (w2p, hs))):
                        dve.wait_ge(w_hi, i + 1)
                        V.tensor_tensor(w[:, 1, :, :], of[:], w[:, 0, :, :], ALU.subtract).then_inc(w_lo, 1)
                    dve.wait_ge(clear, 5)

                    def addA(q, v, r, u):
                        t = Q * q + u
                        dve.wait_ge(gA_ld[Q * v + u], 16 * (r + 1))
                        dve.wait_ge(mA_ld[Q * v + u], 16 * (r + 1))
                        V.tensor_tensor(mA[:, Q * v + u, :], mA[:, Q * v + u, :], gA[:, Q * v + u, :],
                                        ALU.add).then_inc(sumA, 1)
                        wait(dve, agg_done, t + 1 - Q)
                        V.tensor_scalar(ohA[:, u, :], iota[:], dlA[:, bass.ds(t, 1)], None, ALU.is_equal)

                    def addB(q, v, r, h):
                        b_ = 2 * v + h
                        dve.wait_ge(gB_ld[b_], 16 * (r + 1))
                        dve.wait_ge(mB_ld[b_], 16 * (r + 1))
                        V.tensor_tensor(mB[:, b_, :], mB[:, b_, :], gB[:, b_, :], ALU.add).then_inc(sumB, 1)
                        wait(dve, agg_done, Q * q + 2 * h + 2 - Q)
                        V.tensor_scalar(ohB[:, h, :], iota[:], dlB[:, bass.ds(q * 2 + h, 1)], None, ALU.is_equal)

                    def lowA(q, v, r, u):
                        dve.wait_ge(hiA, Q * q + u + 1)
                        V.scalar_tensor_tensor(out=pA[:, u, 1, :], in0=mA[:, Q * v + u, :], scalar=0.0,
                                               in1=pA[:, u, 0, :], op0=ALU.max, op1=ALU.subtract).then_inc(loA, 1)

                    def lowB(q, v, r, h):
                        dve.wait_ge(hiB, 2 * q + h + 1)
                        V.scalar_tensor_tensor(out=pB[:, h, 1, :], in0=mB[:, 2 * v + h, :], scalar=0.0,
                                               in1=pB[:, h, 0, :], op0=ALU.max, op1=ALU.subtract).then_inc(loB, 1)

                    def with_x(q, v, r, u):
                        t = Q * q + u
                        dve.wait_ge(xs_ld[Q * v + u], 16 * (r + 1))
                        dve.wait_ge(agg_done, t + 1)
                        wait(dve, T_done, t + 1 - Q)
                        V.tensor_tensor(hs[:, u, :], psA[u % 2][:, :], xs[:, Q * v + u, :], ALU.add).then_inc(h_in, 1)

                    def low_h(q, v, r, u):
                        dve.wait_ge(hT_hi, Q * q + u + 1)
                        o = slice(u * P, (u + 1) * P)
                        V.tensor_tensor(hT[:, 1, :, o], psT[u % 2][:, :].rearrange("p (c n) -> p c n", c=DC),
                                        hT[:, 0, :, o], ALU.subtract).then_inc(hT_lo, 1)

                    def low_g(q, v, r, c):
                        dve.wait_ge(gT_hi, DC * q + c + 1)
                        V.tensor_tensor(gT[:, 1, c, :], gf[:, c % 2, :], gT[:, 0, c, :], ALU.subtract
                                        ).then_inc(gT_lo, 1)

                    def residual(q, v, r, u):
                        t = Q * q + u
                        dve.wait_ge(g2_done, t + 1)
                        wait(dve, d_st[u], 16 * q)
                        wait(dve, sq_in, t + 1 - Q)
                        V.tensor_tensor(ds[:, u, :], psU[u % 2][:, :], xs[:, Q * v + u, :], ALU.add).then_inc(d_in, 1)

                    def total(q, v, r, u):
                        t = Q * q + u
                        dve.wait_ge(d_in, t + 1)
                        dve.wait_ge(s1_in, t + 1)
                        V.scalar_tensor_tensor(out=S1[:], in0=ds[:, u, :], scalar=real[:, bass.ds(t, 1)], in1=S1[:],
                                               op0=ALU.mult, op1=ALU.add).then_inc(s1_in, 1)
                    pipe(dve, [(with_x, 1, 0), (low_g, 2, 0), (addA, 0, 0), (with_x, 1, 1), (lowA, 0, 0),
                               (low_g, 2, 1), (addB, 0, 0), (with_x, 1, 2), (addA, 0, 1), (lowB, 0, 0),
                               (low_g, 2, 2), (lowA, 0, 1), (with_x, 1, 3), (low_g, 2, 3),
                               (low_h, 1, 0), (addA, 0, 2), (low_h, 1, 1), (residual, 2, 0), (lowA, 0, 2),
                               (total, 2, 0), (addB, 0, 1), (low_h, 1, 2), (residual, 2, 1), (lowB, 0, 1),
                               (total, 2, 1), (addA, 0, 3), (low_h, 1, 3), (residual, 2, 2), (lowA, 0, 3),
                               (total, 2, 2), (residual, 2, 3), (total, 2, 3)], NQ, 2)
                    n = [0]

                    def step(ins):
                        n[0] += 1
                        ins.then_inc(bn_step, 1)
                        dve.wait_ge(bn_step, n[0])
                    mean, var, tmp_, pow_, a_, c_ = (col[:, i, :] for i in range(6))
                    gamma, beta, b2 = (bn_in[:, i, :] for i in range(3))
                    dve.wait_ge(bn_sum, 1)
                    dve.wait_ge(w_ld[3], 16)
                    step(V.tensor_scalar(mean, psA[0][:, 0:DC], 1.0 / N, None, ALU.mult))
                    step(V.tensor_scalar(var, psA[0][:, DC:2 * DC], 1.0 / N, EPS, ALU.mult, ALU.add))
                    step(V.tensor_tensor(tmp_, mean, mean, ALU.mult))
                    V.tensor_tensor(var, var, tmp_, ALU.subtract).then_inc(bn_var, 1)
                    step(V.tensor_tensor(mean, mean, b2, ALU.add))
                    step(V.tensor_tensor(c_, b2, mean, ALU.subtract))
                    dve.wait_ge(bn_pow, 1)
                    step(V.tensor_tensor(a_, pow_, gamma, ALU.mult))
                    step(V.tensor_tensor(c_, c_, a_, ALU.mult))
                    step(V.tensor_tensor(c_, c_, beta, ALU.add))
                    for i in range(2):
                        for c in range(DC):
                            last_one = V.tensor_scalar(sq[:, i, c * P:(c + 1) * P], ident[:], col[:, 4 + i, c:c + 1],
                                                       None, ALU.mult)
                    last_one.then_inc(bn_diag, 1)
                    dve.wait_ge(bn_rows, 1)
                    V.tensor_copy(aB[:], psT[0][:, :])
                    V.tensor_copy(cB[:], psT[1][:, :])

                @block.scalar
                def _(act):
                    for i, (w, of) in enumerate(((w1p, ds), (w2p, hs))):
                        act.wait_ge(w_ld[i], 16)
                        nc.scalar.activation(w[:, 0, :, :], of[:], ACT.Copy).then_inc(w_hi, 1)
                    act.wait_ge(w_ld[2], 16)

                    def highA(q, v, r, u):
                        t = Q * q + u
                        wait(act, agg_done, t + 1 - Q)
                        act.wait_ge(sumA, t + 1)
                        nc.scalar.activation(pA[:, u, 0, :], mA[:, Q * v + u, :], ACT.Relu).then_inc(hiA, 1)

                    def highB(q, v, r, h):
                        wait(act, agg_done, Q * q + 2 * h + 2 - Q)
                        act.wait_ge(sumB, 2 * q + h + 1)
                        nc.scalar.activation(pB[:, h, 0, :], mB[:, 2 * v + h, :], ACT.Relu).then_inc(hiB, 1)

                    def relus(q, v, r, c):
                        j = DC * q + c
                        act.wait_ge(g1_done, j + 1)
                        wait(act, gT_lo, j - 1)
                        nc.scalar.activation(gf[:, c % 2, :], psG[c % 2][:, :], ACT.Relu,
                                             bias=b1s[:, c:c + 1]).then_inc(gf_in, 1)
                        wait(act, g2_done, Q * q)
                        act.wait_ge(gf_in, j + 1)
                        nc.scalar.activation(gT[:, 0, c, :], gf[:, c % 2, :], ACT.Copy).then_inc(gT_hi, 1)

                    def high_h(q, v, r, u):
                        act.wait_ge(T_done, Q * q + u + 1)
                        wait(act, g1_done, DC * q)
                        nc.scalar.activation(hT[:, 0, :, u * P:(u + 1) * P],
                                             psT[u % 2][:, :].rearrange("p (c n) -> p c n", c=DC),
                                             ACT.Copy).then_inc(hT_hi, 1)

                    def squares(q, v, r, u):
                        t = Q * q + u
                        act.wait_ge(d_in, t + 1)
                        wait(act, s2_in, t + 1 - Q)
                        nc.scalar.activation(sq[:, u, :], ds[:, u, :], ACT.Square,
                                             scale=real[:, bass.ds(t, 1)]).then_inc(sq_in, 1)
                    pipe(act, [(relus, 2, 0), (highA, 0, 0), (relus, 2, 1), (highB, 0, 0), (relus, 2, 2),
                               (highA, 0, 1), (relus, 2, 3), (high_h, 1, 0), (high_h, 1, 1), (highA, 0, 2),
                               (squares, 2, 0), (highB, 0, 1), (high_h, 1, 2), (squares, 2, 1), (high_h, 1, 3),
                               (highA, 0, 3), (squares, 2, 2), (squares, 2, 3)], NQ, 2)

                @block.tensor
                def _(pe):
                    mm = nc.tensor.matmul
                    tp.on_tensor(pe)

                    def sums(q, v, r, u):
                        t = Q * q + u
                        half_ = slice((u % 2) * HALF, (u % 2 + 1) * HALF)
                        pe.wait_ge(loA, t + 1)
                        pe.wait_ge(loB, 2 * q + u // 2 + 1)
                        wait(pe, h_in, t - 1)
                        o = psA[u % 2][:, :]
                        mm(o, ohA[:, u, :], pA[:, u, 0, :], start=True, stop=False)
                        mm(o, ohA[:, u, :], pA[:, u, 1, :], start=False, stop=False)
                        mm(o, ohB[half_, u // 2, :], pB[half_, u // 2, 0, :], start=False, stop=False)
                        mm(o, ohB[half_, u // 2, :], pB[half_, u // 2, 1, :], start=False, stop=True
                           ).then_inc(agg_done, 1)

                    def turn(q, v, r, u):
                        t = Q * q + u
                        pe.wait_ge(h_in, t + 1)
                        wait(pe, hT_lo, t - 1)
                        for c in range(DC):
                            f = slice(c * P, (c + 1) * P)
                            last_one = nc.tensor.transpose(psT[u % 2][:, f], hs[:, u, f], ident[:])
                        last_one.then_inc(T_done, 1)

                    def first(q, v, r, m):
                        if isinstance(q, int) and q == 0 and m == 0:
                            pe.wait_ge(w_lo, 2)
                        pe.wait_ge(hT_lo, Q * q + Q)
                        wait(pe, gf_in, DC * q + m - 1)
                        for c in range(DC):
                            f = slice(m * P, (m + 1) * P)
                            for i, j in ((0, 0), (0, 1), (1, 0)):
                                last_one = mm(psG[m % 2][:, :], w1p[:, i, c, f], hT[:, j, c, :],
                                              start=c + i + j == 0, stop=c + i == DC)
                        last_one.then_inc(g1_done, 1)

                    def second(q, v, r, u):
                        pe.wait_ge(gT_lo, DC * q + DC)
                        wait(pe, d_in, Q * q + u - 1)
                        for c in range(DC):
                            f = slice(u * P, (u + 1) * P)
                            for i, j in ((0, 0), (0, 1), (1, 0)):
                                last_one = mm(psU[u % 2][:, :], gT[:, i, c, f], w2p[:, j, c, :],
                                              start=c + i + j == 0, stop=c + i == DC)
                        last_one.then_inc(g2_done, 1)
                    pipe(pe, [(first, 2, 0), (sums, 1, 0), (first, 2, 1), (sums, 1, 1), (first, 2, 2), (sums, 1, 2),
                              (first, 2, 3), (sums, 1, 3), (turn, 1, 0), (turn, 1, 1), (second, 2, 0), (turn, 1, 2),
                              (second, 2, 1), (turn, 1, 3), (second, 2, 2), (second, 2, 3)], NQ, 2)
                    pe.wait_ge(s1_in, NT + 1)
                    pe.wait_ge(s2_in, NT)
                    for i, of in enumerate((S1, S2)):
                        for c in range(DC):
                            last_one = mm(psA[0][:, DC * i + c:DC * i + c + 1], of[:, c * P:(c + 1) * P], ones[:, 0:1],
                                          start=True, stop=True)
                    last_one.then_inc(bn_sum, 1)
                    pe.wait_ge(bn_diag, 1)
                    for i in range(2):
                        last_one = mm(psT[i][:, :], ones[:], sq[:, i, :], start=True, stop=True)
                    last_one.then_inc(bn_rows, 1)
            end_phase()

        X = sb(ctx, "X", [P, NT, D])

        class Norm:

            def __init__(self, scope, name, slots, y=None):
                self.slots = slots
                self.y = sb(scope, f"{name}_y", [P, slots, D]) if y is None else y
                self.st = sb(scope, f"{name}_st", [P, slots, 6])
                self.mv = sb(scope, f"{name}_mv", [P, slots, 2])
                self.ve = sb(scope, f"{name}_ve", [P, slots])
                self.rs = sb(scope, f"{name}_rs", [P, slots])
                self.y_in = sem(f"{name}_y_in")
                self.st_in = sem(f"{name}_st_in")
                self.mv_in = sem(f"{name}_mv_in")
                self.ve_in = sem(f"{name}_ve_in")
                self.rs_in = sem(f"{name}_rs_in")
                self.x_in = sem(f"{name}_x_in")
                self.seen = sem(f"{name}_seen")

            def statistics(self, dve, t, u):
                dve.wait_ge(self.y_in, t + 1)
                nc.vector.bn_stats(self.st[:, u, :], self.y[:, u, :]).then_inc(self.st_in, 1)

            def aggregate(self, dve, t, u):
                wait(dve, self.rs_in, t + 1 - self.slots)
                dve.wait_ge(self.st_in, t + 1)
                dve.nop().then_inc(self.seen, 1)
                nc.vector.bn_aggr(self.mv[:, u, :], self.st[:, u, :]).then_inc(self.mv_in, 1)

            def power(self, pool, t, u):
                wait(pool, self.x_in, t + 1 - self.slots)
                pool.wait_ge(self.mv_in, t + 1)
                nc.gpsimd.tensor_tensor(self.ve[:, u:u + 1], self.mv[:, u, 1:2], power_of[:, 0:1],
                                        ALU.add).then_inc(self.ve_in, 1)
                pool.wait_ge(self.ve_in, t + 1)
                nc.gpsimd.tensor_tensor(self.rs[:, u:u + 1], self.ve[:, u:u + 1], power_of[:, 1:2],
                                        ALU.pow).then_inc(self.rs_in, 1)

            def power_of_two_tiles(self, pool, t, u):
                if u % 2 == 0:
                    return
                wait(pool, self.x_in, t + 1 - self.slots)
                pool.wait_ge(self.mv_in, t + 1)
                both = slice(u - 1, u + 1)
                nc.gpsimd.tensor_tensor(self.ve[:, both], self.mv[:, both, 1], power_of[:, 0:1].to_broadcast([P, 2]),
                                        ALU.add).then_inc(self.ve_in, 2)
                pool.wait_ge(self.ve_in, t + 1)
                nc.gpsimd.tensor_tensor(self.rs[:, both], self.ve[:, both], power_of[:, 1:2].to_broadcast([P, 2]),
                                        ALU.pow).then_inc(self.rs_in, 2)

            def apply(self, dve, t, u, to):
                dve.wait_ge(self.rs_in, t + 1)
                nc.vector.tensor_scalar(to, self.y[:, u, :], self.mv[:, u, 0:1], self.rs[:, u:u + 1],
                                        ALU.subtract, ALU.mult).then_inc(self.x_in, 1)

        def state(t):
            return X[:, bass.ds(t, 1), :].rearrange("p a d -> p (a d)")

        with ExitStack() as s:
            wp = sb(s, "wt_parts", [P, 2, DC, D], F32R)
            bp = sb(s, "bp", [P, D], F32R)
            pick = sb(s, "pick", [P, P], F32R)
            xl = sb(s, "n1_x", [P, Q, D])
            xT = sb(s, "n1_xT", [P, 2, 2, D], F32R)
            hs = sb(s, "n1_h", [P, 2, D])
            ln = Norm(s, "n1", Q, xl)
            two = ln.rs
            w_stage = X[:, NT - DC:NT, :]
            bB = X[:, NT - DC - 1, :]
            psT = [ps(s, f"n1_psT{i}") for i in range(2)]
            psU = [ps(s, f"n1_psU{i}") for i in range(2)]
            w_ld = [sem(f"n1_w{i}") for i in range(2)]
            w_hi = sem("n1_w_high")
            w_lo = sem("n1_w_low")
            pick_in = sem("n1_pick")
            d_ld = [sem(f"n1_d_ld{i}") for i in range(Q)]
            x_ld = [sem(f"n1_x_ld{i}") for i in range(Q)]
            h_st = [sem(f"n1_h_st{i}") for i in range(2)]
            da_in = sem("n1_da_in")
            xc_in = sem("n1_xc_in")
            X_in = sem("n1_X_in")
            T_done = sem("n1_T_done")
            xT_hi = sem("n1_xT_high")
            xT_lo = sem("n1_xT_low")
            G_done = sem("n1_G_done")
            h_in = sem("n1_h_in")

            with nc.Block() as block:
                @block.sync
                def _(sp):
                    sp.dma_start(w_stage, wt.rearrange("(c p) n -> p c n", p=P)).then_inc(w_ld[0], 16)
                    sp.dma_start(bB, b.to_broadcast([P, D])).then_inc(w_ld[1], 16)

                    def load(t, u, r):
                        wait(sp, X_in, t + 1 - Q)
                        wait(sp, T_done, t + 1 - Q)
                        if not isinstance(t, int):
                            sp.wait_ge(w_lo, 2)
                        sp.dma_start(state(t), d_dram[rows(t), :]).then_inc(d_ld[u], 16)
                        sp.dma_start(xl[:, u, :], x[rows(t), :]).then_inc(x_ld[u], 16)

                    def store(t, u, r):
                        wait(sp, h_in, t + 1)
                        sp.dma_start(table1[rows(t), :], hs[:, u % 2, :]).then_inc(h_st[u % 2], 16)
                    pipe(sp, [(load, 0), (store, 6)], NT, Q)
                    for i in range(2):
                        sp.wait_ge(h_st[i], 16 * NT // 2)

                @block.gpsimd
                def _(pool):
                    def norm_input(t, u, r):
                        pool.wait_ge(d_ld[u], 16 * (r + 1))
                        nc.gpsimd.tensor_tensor(state(t), state(t), aB[:], ALU.mult).then_inc(da_in, 1)
                        pool.wait_ge(x_ld[u], 16 * (r + 1))
                        nc.gpsimd.tensor_tensor(xl[:, u, :], xl[:, u, :], cB[:], ALU.add).then_inc(xc_in, 1)

                    def power(t, u, r):
                        ln.power(pool, t, u)
                    pipe(pool, [(norm_input, 0), (power, 1)], NT, Q)

                @block.vector
                def _(dve):
                    V = nc.vector
                    V.tensor_scalar(two[:, 0:1], pcol[:], 0.0, None, ALU.is_equal).then_inc(pick_in, 1)
                    V.tensor_scalar(two[:, 1:2], pcol[:], float(P // 2), None, ALU.is_equal).then_inc(pick_in, 1)
                    dve.wait_ge(pick_in, 2)
                    V.tensor_scalar(pick[:], ones[:], two[:, 0:1], None, ALU.mult).then_inc(pick_in, 1)
                    dve.wait_ge(pick_in, 3)
                    V.tensor_scalar(pick[:], pick[:], two[:, 1:2], None, ALU.add).then_inc(pick_in, 1)
                    dve.wait_ge(w_hi, 1)
                    V.tensor_tensor(wp[:, 1, :, :], w_stage, wp[:, 0, :, :], ALU.subtract).then_inc(w_lo, 1)
                    dve.wait_ge(w_hi, 2)
                    low_half = slice(P // 2, P)
                    V.tensor_tensor(bp[low_half, :], X[low_half, NT - DC - 1, :], bp[low_half, :], ALU.subtract).then_inc(w_lo, 1)

                    def sum_(t, u, r):
                        dve.wait_ge(da_in, t + 1)
                        dve.wait_ge(xc_in, t + 1)
                        V.tensor_tensor(xl[:, u, :], state(t), xl[:, u, :], ALU.add).then_inc(ln.y_in, 1)

                    def statistics(t, u, r):
                        ln.statistics(dve, t, u)

                    def aggregate(t, u, r):
                        ln.aggregate(dve, t, u)

                    def norm(t, u, r):
                        ln.apply(dve, t, u, xl[:, u, :])

                    def low(t, u, r):
                        dve.wait_ge(xT_hi, t + 1)
                        V.tensor_tensor(xT[:, u % 2, 1, :], psT[u % 2][:, :], xT[:, u % 2, 0, :], ALU.subtract
                                        ).then_inc(xT_lo, 1)
                    pipe(dve, [(sum_, 0), (norm, 1), (statistics, 0), (low, 2), (aggregate, 0)], NT, Q)

                @block.scalar
                def _(act):
                    act.wait_ge(w_ld[0], 16)
                    nc.scalar.activation(wp[:, 0, :, :], w_stage, ACT.Copy).then_inc(w_hi, 1)
                    act.wait_ge(w_ld[1], 16)
                    nc.scalar.activation(bp[:], bB, ACT.Copy).then_inc(w_hi, 1)

                    def keep(t, u, r):
                        act.wait_ge(ln.x_in, t + 1)
                        nc.scalar.activation(state(t), xl[:, u, :], ACT.Copy).then_inc(X_in, 1)

                    def high(t, u, r):
                        act.wait_ge(T_done, t + 1)
                        wait(act, G_done, t - 1)
                        nc.scalar.activation(xT[:, u % 2, 0, :], psT[u % 2][:, :], ACT.Copy).then_inc(xT_hi, 1)

                    def scale(t, u, r):
                        act.wait_ge(G_done, t + 1)
                        wait(act, h_st[u % 2], 16 * (r * 2 + u // 2))
                        nc.scalar.activation(hs[:, u % 2, :], psU[u % 2][:, :], ACT.Copy,
                                             scale=dis1[:, bass.ds(t, 1)]).then_inc(h_in, 1)
                    pipe(act, [(high, 0), (keep, 0), (scale, 1)], NT, Q)

                @block.tensor
                def _(pe):
                    mm = nc.tensor.matmul

                    def turn(t, u, r):
                        pe.wait_ge(ln.x_in, t + 1)
                        wait(pe, xT_lo, t - 1)
                        for c in range(DC):
                            f = slice(c * P, (c + 1) * P)
                            last_one = nc.tensor.transpose(psT[u % 2][:, f], xl[:, u, f], ident[:])
                        last_one.then_inc(T_done, 1)

                    def product(t, u, r):
                        if isinstance(t, int) and t == 0:
                            pe.wait_ge(pick_in, 4)
                            pe.wait_ge(w_lo, 2)
                        pe.wait_ge(xT_lo, t + 1)
                        wait(pe, h_in, t - 1)
                        mm(psU[u % 2][:, :], pick[:], bp[:], start=True, stop=False)
                        for c in range(DC):
                            f = slice(c * P, (c + 1) * P)
                            for i, j in ((0, 0), (0, 1), (1, 0)):
                                last_one = mm(psU[u % 2][:, :], xT[:, u % 2, i, f], wp[:, j, c, :], start=False,
                                              stop=c + i == DC)
                        last_one.then_inc(G_done, 1)
                    pipe(pe, [(turn, 0), (product, 1)], NT, Q)
            end_phase()

        full = aB[0:NT, :]
        G = 8

        with ExitStack() as s:
            slotidx = sb(s, "n2_idx", [P, G // 2, FIELDS], I32)
            gA = sb(s, "n2_gA", [P, G, D])
            gB = sb(s, "n2_gB", [P, G // 2, D])
            ohA = sb(s, "n2_ohA", [P, Q, P])
            ohB = sb(s, "n2_ohB", [P, 2, P])
            ln = Norm(s, "n2", Q)
            kh = cB[:].rearrange("p (u n) -> p u n", u=4)
            far = cB[:].rearrange("p (u n) -> p u n", u=4)[:, 2:4, :]
            psA = [ps(s, f"n2_psA{i}") for i in range(2)]
            psF = ps(s, "n2_psF")
            tp = TablePass(s, "t1", table1, sums1, D, gA, ohA, psA[0])
            clear = sem("n2_clear")
            idx_seen = sem("n2_idx_seen")
            idx_in = sem("n2_idx_in")
            gA_ld = [sem(f"n2_gA{i}") for i in range(G)]
            gB_ld = [sem(f"n2_gB{i}") for i in range(G // 2)]
            hs_ld = [sem(f"n2_hs{i}") for i in range(Q)]
            far_in = sem("n2_far_in")
            oh_in = sem("n2_oh_in")
            ohB_in = sem("n2_ohB_in")
            agg_done = sem("n2_agg_done")
            o_in = sem("n2_o_in")
            r_in = sem("n2_r_in")
            F_done = sem("n2_F_done")

            with nc.Block() as block:
                @block.sync
                def _(sp):
                    tp.on_sync(sp)
                    def load(t, u, r):
                        wait(sp, ln.x_in, t + 1 - Q)
                        sp.dma_start(ln.y[:, u % Q, :], table1[rows(t), :]).then_inc(hs_ld[u % Q], 16)
                    pipe(sp, [(load, 0)], NT, G)

                @block.gpsimd
                def _(pool):
                    tp.on_gpsimd(pool)
                    pool.memset(gA[:], 0.0).then_inc(clear, 1)
                    pool.memset(gB[:], 0.0).then_inc(clear, 1)
                    pool.wait_ge(clear, 2)

                    table_mode = pool.value_load(mode_i[0:1, 0:1], min_val=0, max_val=1)

                    def fetch(into, table, field, v, signal):
                        pool.indirect_dma_start(
                            out=into, out_offset=None, in_=table,
                            in_offset=bass.IndirectOffsetOnAxis(ap=slotidx[:, v, field:field + 1], axis=0),
                            bounds_check=NP - 1, oob_is_err=False).then_inc(signal, 16)

                    def gather(t, u, r):
                        if u % 2:
                            return
                        h = u // 2
                        k = r * (G // 2) + h
                        wait(pool, gA_ld[u], 16 * r)
                        wait(pool, gA_ld[u + 1], 16 * r)
                        wait(pool, gB_ld[h], 16 * r)
                        nc.gpsimd.tensor_copy(slotidx[:, h, :], IDX[:, bass.ds(k, 1), :].rearrange("p a f -> p (a f)")
                                              ).then_inc(idx_in, 1)
                        wait(pool, agg_done, t + 2 - G)
                        wait(pool, idx_in, k + 1)
                        pool.nop().then_inc(idx_seen, 1)
                        with pool.If(table_mode > 0):
                            fetch(gA[:, u, :], sums1, EID_A, h, gA_ld[u])
                            fetch(gA[:, u + 1, :], sums1, EID_A + 1, h, gA_ld[u + 1])
                        with pool.Else():
                            fetch(gA[:, u, :], table1, SRC_A, h, gA_ld[u])
                            fetch(gA[:, u + 1, :], table1, SRC_A + 1, h, gA_ld[u + 1])
                        fetch(gB[:, h, :], table1, SRC_B, h, gB_ld[h])

                    def power(t, u, r):
                        ln.power(pool, t, u % Q)
                    pipe(pool, [(gather, 0), (power, 6)], NT, G)

                @block.vector
                def _(dve):
                    tp.on_vector(dve)
                    V = nc.vector
                    dve.wait_ge(clear, 2)

                    def hotB(t, u, r):
                        if u % 2 == 0:
                            wait(dve, agg_done, t + 2 - Q)
                            V.tensor_scalar(ohB[:, u // 2 % 2, :], iota[:], dlB[:, bass.ds(r * (G // 2) + u // 2, 1)],
                                            None, ALU.is_equal).then_inc(ohB_in, 1)

                    def own(t, u, r):
                        dve.wait_ge(agg_done, t + 1)
                        dve.wait_ge(hs_ld[u % Q], 16 * (r * (G // Q) + u // Q + 1))
                        V.tensor_tensor(ln.y[:, u % Q, :], psA[u % 2][:, :], ln.y[:, u % Q, :], ALU.add
                                        ).then_inc(o_in, 1)

                    def sum_(t, u, r):
                        dve.wait_ge(r_in, t + 1)
                        V.tensor_tensor(ln.y[:, u % Q, :], ln.y[:, u % Q, :], state(t), ALU.add).then_inc(ln.y_in, 1)

                    def statistics(t, u, r):
                        ln.statistics(dve, t, u % Q)

                    def aggregate(t, u, r):
                        ln.aggregate(dve, t, u % Q)

                    def norm(t, u, r):
                        wait(dve, F_done, t - 1)
                        V.tensor_scalar(kh[:, u % 2, 0:NT], keys[:], skey[:, bass.ds(t, 1)], None, ALU.is_equal)
                        ln.apply(dve, t, u % Q, state(t))
                    pipe(dve, [(sum_, 3), (own, 2), (statistics, 3), (hotB, 0), (aggregate, 3), (norm, 4)], NT, G)
                    dve.wait_ge(F_done, NT)
                    V.tensor_copy(full, psF[0:NT, :])

                @block.scalar
                def _(act):
                    def relu(t, u, r):
                        act.wait_ge(o_in, t + 1)
                        nc.scalar.activation(ln.y[:, u % Q, :], ln.y[:, u % Q, :], ACT.Relu,
                                             scale=dis1[:, bass.ds(t, 1)]).then_inc(r_in, 1)

                    def hots(t, u, r):
                        wait(act, oh_in, t - 1)
                        nc.scalar.activation(far[:, u % 2, :], iota[:], ACT.Square, scale=-1.0,
                                             bias=dlA[:, bass.ds(t, 1)]).then_inc(far_in, 1)
                        wait(act, agg_done, t + 1 - Q)
                        act.wait_ge(far_in, t + 1)
                        nc.scalar.activation(ohA[:, u % Q, :], far[:, u % 2, :], ACT.Relu, scale=-1.0,
                                             bias=ones[:, 0:1]).then_inc(oh_in, 1)
                    act.wait_ge(clear, 2)
                    pipe(act, [(relu, 2), (hots, 0)], NT, G)

                @block.tensor
                def _(pe):
                    tp.on_tensor(pe)
                    mm = nc.tensor.matmul

                    def sums(t, u, r):
                        h, half_ = u // 2, slice((u % 2) * HALF, (u % 2 + 1) * HALF)
                        pe.wait_ge(oh_in, t + 1)
                        pe.wait_ge(ohB_in, r * (G // 2) + h + 1)
                        pe.wait_ge(gA_ld[u], 16 * (r + 1))
                        pe.wait_ge(gB_ld[h], 16 * (r + 1))
                        wait(pe, o_in, t - 1)
                        mm(psA[u % 2][:, :], ohA[:, u % Q, :], gA[:, u, :], start=True, stop=False)
                        mm(psA[u % 2][:, :], ohB[half_, h % 2, :], gB[half_, h, :], start=False,
                           stop=True).then_inc(agg_done, 1)

                    def segments(t, u, r):
                        pe.wait_ge(ln.x_in, t + 1)
                        first_one, last_one = isinstance(t, int) and t == 0, isinstance(t, int) and t == NT - 1
                        mm(psF[0:NT, :], kh[:, u % 2, 0:NT], state(t), start=first_one, stop=last_one
                           ).then_inc(F_done, 1)
                    pipe(pe, [(sums, 0), (segments, 4)], NT, G)
            end_phase()

        with ExitStack() as s:
            ws = sb(s, "wcs", [P, DC, HID])
            rid = sb(s, "n3_rid", [P, Q, P])
            inm = sb(s, "n3_in", [P, 2, P])
            ek = sb(s, "n3_ek", [NT, 2, P], F32R)
            xn = sb(s, "n3_xn", [P, 2, D])
            xT = sb(s, "n3_xT", [P, 2, D])
            hs = sb(s, "n3_h", [P, 2, HID])
            wls = sb(s, "n3_wl", [HID, D])
            bcs = sb(s, "bcs", [HID, 1])
            bcB = sb(s, "bcB", [HID, P])
            blB = sb(s, "blB", [P, D])
            cl = sb(s, "cl", [P, D])
            fp = sb(s, "n3_full", [NT, 2, D], F32R)
            ln = Norm(s, "n3", Q)
            psM = [ps(s, f"n3_psM{i}") for i in range(2)]
            psT = [ps(s, f"n3_psT{i}") for i in range(2)]
            psU = [ps(s, f"n3_psU{i}") for i in range(2)]
            psC = ps(s, "n3_psC")
            w_ld = sem("n3_w")
            wl_ld = [sem(f"n3_wl{i}") for i in range(3)]
            bc_in = sem("n3_bc_in")
            cl_done = sem("n3_cl_done")
            cl_in = sem("n3_cl_in")
            full_hi = sem("n3_full_high")
            full_lo = sem("n3_full_low")
            rid_ld = [sem(f"n3_rid{i}") for i in range(Q)]
            h_st = [sem(f"n3_h_st{i}") for i in range(2)]
            sel_in = sem("n3_sel_in")
            M_done = sem("n3_M_done")
            X_in = sem("n3_X_in")
            T_done = sem("n3_T_done")
            xT_in = sem("n3_xT_in")
            G_done = sem("n3_G_done")
            h_in = sem("n3_h_in")

            with nc.Block() as block:
                @block.sync
                def _(sp):
                    sp.dma_start(ws[:], wc.rearrange("(c p) n -> p c n", p=P)).then_inc(w_ld, 16)
                    sp.dma_start(wls[:], wl).then_inc(wl_ld[0], 16)
                    sp.dma_start(bcs[:], bc).then_inc(wl_ld[1], 16)
                    sp.dma_start(blB[:], bl.to_broadcast([P, D])).then_inc(wl_ld[2], 16)

                    def load(t, u, r):
                        wait(sp, sel_in, t + 1 - Q)
                        sp.dma_start(rid[:, u, :], rid_dram[bass.ds(t, 1), :].to_broadcast([P, P])).then_inc(rid_ld[u], 16)

                    def store(t, u, r):
                        wait(sp, h_in, t + 1)
                        sp.dma_start(table3[rows(t), :], hs[:, u % 2, :]).then_inc(h_st[u % 2], 16)
                    pipe(sp, [(load, 0), (store, 6)], NT, Q)
                    for i in range(2):
                        sp.wait_ge(h_st[i], 16 * NT // 2)

                @block.gpsimd
                def _(pool):
                    pool.wait_ge(cl_in, 1)

                    def power(t, u, r):
                        ln.power(pool, t, u)

                    def keep(t, u, r):
                        pool.wait_ge(ln.x_in, t + 1)
                        nc.gpsimd.tensor_tensor(state(t), xn[:, u % 2, :], cl[:], ALU.add).then_inc(X_in, 1)
                    pipe(pool, [(power, 0), (keep, 1)], NT, Q)

                @block.vector
                def _(dve):
                    V = nc.vector
                    dve.wait_ge(full_hi, 1)
                    V.tensor_tensor(fp[:, 1, :], full, fp[:, 0, :], ALU.subtract).then_inc(full_lo, 1)
                    dve.wait_ge(wl_ld[1], 16)
                    V.tensor_scalar(bcB[:], ones[:], bcs[:], None, ALU.mult).then_inc(bc_in, 1)
                    dve.wait_ge(wl_ld[2], 16)
                    dve.wait_ge(cl_done, 1)
                    V.tensor_tensor(cl[:], psC[:, :], blB[:], ALU.add).then_inc(cl_in, 1)

                    def select(t, u, r):
                        dve.wait_ge(rid_ld[u], 16 * (r + 1))
                        wait(dve, M_done, t - 1)
                        V.tensor_scalar(inm[:, u % 2, :], rid[:, u, :], skey_in[:, bass.ds(t, 1)], None, ALU.is_equal)
                        V.tensor_scalar(ek[:, u % 2, :], rid[0:NT, u, :], keycol[:], None,
                                        ALU.is_equal).then_inc(sel_in, 1)

                    def sum_(t, u, r):
                        dve.wait_ge(M_done, t + 1)
                        wait(dve, ln.x_in, t + 1 - Q)
                        V.scalar_tensor_tensor(out=ln.y[:, u, :], in0=psM[u % 2][:, :], scalar=rcnt[:, bass.ds(t, 1)],
                                               in1=state(t), op0=ALU.mult, op1=ALU.add).then_inc(ln.y_in, 1)

                    def statistics(t, u, r):
                        ln.statistics(dve, t, u)

                    def aggregate(t, u, r):
                        ln.aggregate(dve, t, u)

                    def norm(t, u, r):
                        wait(dve, X_in, t - 1)
                        wait(dve, T_done, t - 1)
                        ln.apply(dve, t, u, xn[:, u % 2, :])
                    pipe(dve, [(select, 0), (sum_, 1), (statistics, 1), (norm, 2), (aggregate, 1)], NT, Q)

                @block.scalar
                def _(act):
                    nc.scalar.activation(fp[:, 0, :], full, ACT.Copy).then_inc(full_hi, 1)

                    def turned(t, u, r):
                        act.wait_ge(T_done, t + 1)
                        wait(act, G_done, t - 1)
                        nc.scalar.activation(xT[:, u % 2, :], psT[u % 2][:, :], ACT.Copy).then_inc(xT_in, 1)

                    def scale(t, u, r):
                        act.wait_ge(G_done, t + 1)
                        wait(act, h_st[u % 2], 16 * (r * 2 + u // 2))
                        nc.scalar.activation(hs[:, u % 2, :], psU[u % 2][:, 0:HID], ACT.Copy,
                                             scale=dis3[:, bass.ds(t, 1)]).then_inc(h_in, 1)
                    pipe(act, [(turned, 0), (scale, 1)], NT, Q)

                @block.tensor
                def _(pe):
                    mm = nc.tensor.matmul

                    def means(t, u, r):
                        pe.wait_ge(sel_in, t + 1)
                        wait(pe, ln.y_in, t - 1)
                        for i in range(2):
                            mm(psM[u % 2][:, :], ek[:, u % 2, :], fp[:, i, :], start=i == 0, stop=False)
                        mm(psM[u % 2][:, :], inm[:, u % 2, :], state(t), start=False, stop=True).then_inc(M_done, 1)

                    def turn(t, u, r):
                        pe.wait_ge(ln.x_in, t + 1)
                        wait(pe, xT_in, t - 1)
                        for c in range(DC):
                            f = slice(c * P, (c + 1) * P)
                            last_one = nc.tensor.transpose(psT[u % 2][:, f], xn[:, u % 2, f], ident[:])
                        last_one.then_inc(T_done, 1)

                    def product(t, u, r):
                        pe.wait_ge(xT_in, t + 1)
                        wait(pe, h_in, t - 1)
                        for c in range(DC):
                            last_one = mm(psU[u % 2][:, 0:HID], xT[:, u % 2, c * P:(c + 1) * P], ws[:, c, :],
                                          start=c == 0, stop=c == DC - 1)
                        last_one.then_inc(G_done, 1)
                    pe.wait_ge(wl_ld[0], 16)
                    pe.wait_ge(bc_in, 1)
                    mm(psC[:, :], bcB[:], wls[:], start=True, stop=True).then_inc(cl_done, 1)
                    pe.wait_ge(full_lo, 1)
                    pe.wait_ge(w_ld, 16)
                    pipe(pe, [(means, 0), (turn, 2), (product, 3)], NT, Q)
            end_phase()

        with ExitStack() as s:
            ws = sb(s, "wls", [HID, D])
            slotidx = sb(s, "n4_idx", [P, G // 2, FIELDS], I32)
            gA = sb(s, "n4_gA", [P, G, HID])
            gB = sb(s, "n4_gB", [P, G // 2, HID])
            hs = sb(s, "n4_hs", [P, G, HID])
            ohA = sb(s, "n4_ohA", [P, G, P])
            ohB = sb(s, "n4_ohB", [P, G // 2, P])
            aT = sb(s, "n4_aT", [HID, 2, P])
            xo = sb(s, "n4_xo", [P, 2, D])
            ln = Norm(s, "n4", Q)
            psA = [ps(s, f"n4_psA{i}") for i in range(2)]
            psO = [ps(s, f"n4_psO{i}") for i in range(2)]
            w_ld = sem("n4_w")
            tp = TablePass(s, "t3", table3, sums3, HID, gA, ohA, psA[0])
            clear = sem("n4_clear")
            idx_seen = sem("n4_idx_seen")
            idx_in = sem("n4_idx_in")
            gA_ld = [sem(f"n4_gA{i}") for i in range(G)]
            gB_ld = [sem(f"n4_gB{i}") for i in range(G // 2)]
            hs_ld = [sem(f"n4_hs{i}") for i in range(G)]
            o_st = [sem(f"n4_o_st{i}") for i in range(2)]
            oh_in = sem("n4_oh_in")
            agg_done = sem("n4_agg_done")
            aT_in = sem("n4_aT_in")
            O_done = sem("n4_O_done")

            with nc.Block() as block:
                @block.sync
                def _(sp):
                    tp.on_sync(sp)
                    sp.dma_start(ws[:], wl).then_inc(w_ld, 16)

                    def load(t, u, r):
                        wait(sp, agg_done, t + 1 - G)
                        sp.dma_start(hs[:, u, :], table3[rows(t), :]).then_inc(hs_ld[u], 16)

                    def store(t, u, r):
                        wait(sp, ln.x_in, t + 1)
                        sp.dma_start(out[rows(t), :], xo[:, u % 2, :]).then_inc(o_st[u % 2], 16)
                    pipe(sp, [(load, 0), (store, 7)], NT, G)
                    for i in range(2):
                        sp.wait_ge(o_st[i], 16 * NT // 2)

                @block.gpsimd
                def _(pool):
                    tp.on_gpsimd(pool)
                    pool.memset(gA[:], 0.0).then_inc(clear, 1)
                    pool.memset(gB[:], 0.0).then_inc(clear, 1)
                    pool.wait_ge(clear, 2)

                    table_mode = pool.value_load(mode_i[0:1, 0:1], min_val=0, max_val=1)

                    def fetch(into, table, field, v, signal):
                        pool.indirect_dma_start(
                            out=into, out_offset=None, in_=table,
                            in_offset=bass.IndirectOffsetOnAxis(ap=slotidx[:, v, field:field + 1], axis=0),
                            bounds_check=NP - 1, oob_is_err=False).then_inc(signal, 16)

                    def indices(t, u, r):
                        if u % 2:
                            return
                        h = u // 2
                        k = r * (G // 2) + h
                        wait(pool, gA_ld[u], 16 * r)
                        wait(pool, gA_ld[u + 1], 16 * r)
                        wait(pool, gB_ld[h], 16 * r)
                        nc.gpsimd.tensor_copy(slotidx[:, h, :], IDX[:, bass.ds(k, 1), :].rearrange("p a f -> p (a f)")
                                              ).then_inc(idx_in, 1)

                    def gather(t, u, r):
                        if u % 2:
                            return
                        h = u // 2
                        k = r * (G // 2) + h
                        wait(pool, agg_done, t + 2 - G)
                        wait(pool, idx_in, k + 1)
                        pool.nop().then_inc(idx_seen, 1)
                        with pool.If(table_mode > 0):
                            fetch(gA[:, u, :], sums3, EID_A, h, gA_ld[u])
                            fetch(gA[:, u + 1, :], sums3, EID_A + 1, h, gA_ld[u + 1])
                        with pool.Else():
                            fetch(gA[:, u, :], table3, SRC_A, h, gA_ld[u])
                            fetch(gA[:, u + 1, :], table3, SRC_A + 1, h, gA_ld[u + 1])
                        fetch(gB[:, h, :], table3, SRC_B, h, gB_ld[h])

                    def power(t, u, r):
                        ln.power_of_two_tiles(pool, t, u % Q)
                    pipe(pool, [(indices, 0), (gather, 2), (power, 8)], NT, G)

                @block.vector
                def _(dve):
                    tp.on_vector(dve)
                    V = nc.vector
                    dve.wait_ge(clear, 2)

                    def hots(t, u, r):
                        wait(dve, agg_done, t + 1 - G)
                        if u % 2 == 0:
                            wait(dve, agg_done, t + 2 - G)
                            V.tensor_scalar(ohB[:, u // 2, :], iota[:], dlB[:, bass.ds(r * (G // 2) + u // 2, 1)], None,
                                            ALU.is_equal)
                        V.tensor_scalar(ohA[:, u, :], iota[:], dlA[:, bass.ds(t, 1)], None,
                                        ALU.is_equal).then_inc(oh_in, 1)

                    def sum_(t, u, r):
                        dve.wait_ge(O_done, t + 1)
                        wait(dve, ln.x_in, t + 1 - Q)
                        V.scalar_tensor_tensor(out=ln.y[:, u % Q, :], in0=psO[u % 2][:, :], scalar=dis3[:, bass.ds(t, 1)],
                                               in1=state(t), op0=ALU.mult, op1=ALU.add).then_inc(ln.y_in, 1)

                    def statistics(t, u, r):
                        ln.statistics(dve, t, u % Q)

                    def aggregate(t, u, r):
                        ln.aggregate(dve, t, u % Q)

                    def norm(t, u, r):
                        wait(dve, o_st[u % 2], 16 * (r * (G // 2) + u // 2))
                        ln.apply(dve, t, u % Q, xo[:, u % 2, :])
                    pipe(dve, [(sum_, 3), (hots, 0), (statistics, 3), (norm, 5), (aggregate, 3)], NT, G)

                @block.scalar
                def _(act):
                    def turned(t, u, r):
                        act.wait_ge(agg_done, t + 1)
                        wait(act, O_done, t - 1)
                        nc.scalar.activation(aT[:, u % 2, :], psA[u % 2][:, 0:P], ACT.Copy).then_inc(aT_in, 1)
                    pipe(act, [(turned, 0)], NT, G)

                @block.tensor
                def _(pe):
                    tp.on_tensor(pe)
                    mm = nc.tensor.matmul
                    pe.wait_ge(w_ld, 16)

                    def sums(t, u, r):
                        h, half_ = u // 2, slice((u % 2) * HALF, (u % 2 + 1) * HALF)
                        pe.wait_ge(oh_in, t + 1)
                        pe.wait_ge(gA_ld[u], 16 * (r + 1))
                        pe.wait_ge(gB_ld[h], 16 * (r + 1))
                        pe.wait_ge(hs_ld[u], 16 * (r + 1))
                        wait(pe, aT_in, t - 1)
                        to = psA[u % 2][:, 0:P]
                        mm(to, hs[:, u, :], ident[:], start=True, stop=False)
                        mm(to, gA[:, u, :], ohA[:, u, :], start=False, stop=False)
                        mm(to, gB[half_, h, :], ohB[half_, h, :], start=False, stop=True).then_inc(agg_done, 1)

                    def product(t, u, r):
                        pe.wait_ge(aT_in, t + 1)
                        wait(pe, ln.y_in, t - 1)
                        mm(psO[u % 2][:, :], aT[:, u % 2, :], ws[:], start=True, stop=True).then_inc(O_done, 1)
                    pipe(pe, [(sums, 0), (product, 1)], NT, G)


def _search_path():
    low, high = np.zeros(E + 1, np.int64), np.full(E + 1, E)
    mids, rights = [], []
    for _ in range(LEVELS):
        mid = low + (high - low) // 2
        right = np.arange(E + 1) > mid
        mids.append(mid)
        rights.append(right)
        low, high = np.where(right, mid, low), np.where(right, high, mid)
    return np.minimum(np.stack(mids, 1), E - 1), np.stack(rights, 1)


def _columns(a, fill=0):
    a = np.concatenate([a, np.full((NP - len(a), *a.shape[1:]), fill, a.dtype)])
    return np.ascontiguousarray(np.swapaxes(a.reshape(NT, P, *a.shape[1:]), 0, 1))


def _layout(i):
    i = {k: np.asarray(v) for k, v in i.items()}
    src, dst = i["src"], i["dst"]
    pad = np.full(NP + RUN + P - E, 2 * E, np.int32)
    srcp, dstp = np.concatenate([src, pad]), np.concatenate([dst, pad])
    mids, rights = _search_path()
    before = (np.arange(E + 1) - 1) % E
    left = np.where(rights, FAR, 0).astype(np.float32)
    return {
        "x": np.concatenate([i["x"], np.zeros((NP - N, D), np.float32)]),
        "ea": np.concatenate([i["edge_attr_512"], np.zeros((NP - E, D), np.float32)]),
        "src_cols": _columns(src, 2 * E), "dst_cols": _columns(dst, 2 * E),
        "runs": np.stack([np.concatenate([srcp[r * P:r * P + RUN], dstp[r * P:r * P + RUN]]) for r in range(NT)]),
        "dst_steps": np.stack([dstp[r * NT:r * NT + NT + 1] for r in range(P)]),
        "path": _columns(src[mids]),
        "path_right": _columns(rights.astype(np.float32)),
        "path_left": _columns(left, -FAR),
        "leaf_dst": _columns(dst[before]), "leaf_src": _columns(src[before]),
        "dst_rows": dstp[:NP].reshape(NT, P),
        "w1": i["L0_gnn_W1"], "b1": np.ascontiguousarray(i["L0_gnn_b1"].reshape(DC, P).T),
        "w2": i["L0_gnn_W2"],
        "bn_cols": np.stack([i[f"L0_gnn_{k}"].reshape(DC, P).T for k in ("gamma", "beta", "b2")], 1),
        "wt": np.ascontiguousarray(i["L1_gnn_W"].T), "b": i["L1_gnn_b"].reshape(1, D),
        "wc": i["L3_gnn_W_conv"], "bc": i["L3_gnn_b_conv"].reshape(HID, 1),
        "wl": i["L3_gnn_W_lin"], "bl": i["L3_gnn_b_lin"].reshape(1, D),
    }


def kernel(**inputs):
    import concourse.bacc as bacc
    from concourse.bass_utils import run_bass_kernel_spmd

    nc = bacc.Bacc("TRN2", target_bir_lowering=False, num_devices=1)
    arrays = {f"in_{k}": np.ascontiguousarray(a) for k, a in _layout(inputs).items()}
    args = [nc.dram_tensor(k, a.shape, mybir.dt.from_np(a.dtype), kind="ExternalInput").ap()
            for k, a in arrays.items()]
    args.append(nc.dram_tensor("out_x", [NP, D], F32, kind="ExternalOutput").ap())
    build(nc, *args)
    r = run_bass_kernel_spmd(nc, [arrays], core_ids=[0])
    return r.results[0]["out_x"][:N]
```
